# Optimizing a Trainium2 kernel written in Bass

```python
import numpy as np
import jax
import jax.numpy as jnp

def _softmax(x, axis=-1):
    return jax.nn.softmax(x, axis=axis)

def _gelu(x):
    return jax.nn.gelu(x, approximate=True)

def _silu(x):
    return jax.nn.silu(x)

def _sigmoid(x):
    return jax.nn.sigmoid(x)

def _layernorm(x, axis=-1, eps=1e-05):
    m = jnp.mean(x, axis=axis, keepdims=True)
    v = jnp.var(x, axis=axis, keepdims=True)
    return (x - m) / jnp.sqrt(v + eps)

def _scatter_add(tgt, idx, src, axis=0):
    return tgt.at[idx].add(src)

def _segment_sum(src, seg, n):
    return jax.ops.segment_sum(src, seg, n)
kernel_name = 'mk_gnn_resnorm_d4_gnn_r8_dd09c9'

def setup_inputs(seed: int=0):
    np.random.seed(seed)
    _w = jnp.asarray

    def _rec_inputs():
        import jax
        import jax.numpy as jnp
        _gk = jax.random.key(seed)
        x = -0.0001126 + 1 * jax.random.normal(jax.random.fold_in(_gk, 1), (1250, 768), jnp.float32)
        src = jax.random.randint(jax.random.fold_in(_gk, 2), (20000,), 0, 1250, jnp.int32)
        dst = jax.random.randint(jax.random.fold_in(_gk, 3), (20000,), 0, 1250, jnp.int32)
        _o = jnp.argsort(dst, stable=True)
        src = src[_o]
        dst = dst[_o]
        return (x, src, dst)
    x, src, dst = _rec_inputs()

    def _L0_gnn_setup():
        import jax, jax.numpy as jnp
        import numpy as np
        N_NODES = 1250
        N_EDGES = 10000
        IN_DIM, HID, OUT_DIM, HEADS = (768, 512, 768, 4)
        NEG_SLOPE = 0.2

        def _gat_layer(x, src, dst, W, a_src, a_dst, b, heads, d_out, concat):
            N = x.shape[0]
            h = (x @ W).reshape(N, heads, d_out)
            as_n = jnp.einsum('nhd,hd->nh', h, a_src)
            ad_n = jnp.einsum('nhd,hd->nh', h, a_dst)
            e = jax.nn.leaky_relu(as_n[src] + ad_n[dst], NEG_SLOPE)
            e_max = jax.lax.stop_gradient(jax.ops.segment_max(e, dst, num_segments=N))
            ex = jnp.exp(e - e_max[dst])
            denom = jax.ops.segment_sum(ex, dst, num_segments=N)
            alpha = ex / (denom[dst] + 1e-16)
            msg = alpha[:, :, None] * h[src]
            out = jax.ops.segment_sum(msg, dst, num_segments=N)
            out = out.reshape(N, heads * d_out) if concat else out.mean(axis=1)
            return out + b
        key = jax.random.key(seed)
        ks = jax.random.split(key, 10)
        g = 0.05
        return {'x': jax.random.normal(ks[0], (N_NODES, IN_DIM), jnp.float32), 'edge_index': jax.random.randint(ks[1], (2, N_EDGES), 0, N_NODES, jnp.int64), 'W1': jax.random.normal(ks[2], (IN_DIM, HEADS * HID), jnp.float32) * g, 'a1_src': jax.random.normal(ks[3], (HEADS, HID), jnp.float32) * g, 'a1_dst': jax.random.normal(ks[4], (HEADS, HID), jnp.float32) * g, 'b1': jnp.zeros((HEADS * HID,), jnp.float32), 'W2': jax.random.normal(ks[5], (HEADS * HID, OUT_DIM), jnp.float32) * g, 'a2_src': jax.random.normal(ks[6], (1, OUT_DIM), jnp.float32) * g, 'a2_dst': jax.random.normal(ks[7], (1, OUT_DIM), jnp.float32) * g, 'b2': jnp.zeros((OUT_DIM,), jnp.float32)}
    _L0_gnn_all = _L0_gnn_setup()
    _L0_gnn_in = {k: v for k, v in _L0_gnn_all.items() if k in ('W1', 'a1_src', 'a1_dst', 'b1', 'W2', 'a2_src', 'a2_dst', 'b2')}
    del _L0_gnn_all

    def _L1_gnn_setup():
        import jax, jax.numpy as jnp
        import numpy as np
        N_NODES = 1250
        N_EDGES = 12500
        DIM = 768
        key = jax.random.key(seed)
        k1, k2, k3, k4 = jax.random.split(key, 4)
        x = jax.random.normal(k1, (N_NODES, DIM), dtype=jnp.float32)
        edge_index = jax.random.randint(k2, (2, N_EDGES), 0, N_NODES, dtype=jnp.int32)
        W = jax.random.normal(k3, (DIM, DIM), dtype=jnp.float32) / np.sqrt(DIM)
        b = jnp.zeros((DIM,), dtype=jnp.float32)
        return {'x': x, 'edge_index': edge_index, 'W': W, 'b': b}
    _L1_gnn_all = _L1_gnn_setup()
    _L1_gnn_in = {k: v for k, v in _L1_gnn_all.items() if k in ('W', 'b')}
    del _L1_gnn_all

    def _L2_gnn_setup():
        import jax, jax.numpy as jnp
        import numpy as np
        N_NODES = 1250
        N_EDGES = 12500
        DIM = 768
        NEG_SLOPE = 0.2

        def gat_conv(x, src, dst, W, att_src, att_dst, bias, num_nodes):
            h = x @ W
            a_s = h @ att_src
            a_d = h @ att_dst
            e = jax.nn.leaky_relu(a_s[src] + a_d[dst], NEG_SLOPE)
            m = jax.ops.segment_max(e, dst, num_segments=num_nodes)
            e = jnp.exp(e - m[dst])
            denom = jax.ops.segment_sum(e, dst, num_segments=num_nodes)
            alpha = e / denom[dst]
            msg = alpha[:, None] * h[src]
            out = jax.ops.segment_sum(msg, dst, num_segments=num_nodes)
            return out + bias
        key = jax.random.key(seed)
        ks = jax.random.split(key, 12)
        s = 1.0 / np.sqrt(DIM)
        inp = {'x': jax.random.normal(ks[0], (N_NODES, DIM), dtype=jnp.float32), 'edge_index': jax.random.randint(ks[1], (2, N_EDGES), 0, N_NODES, dtype=jnp.int64), 'W1': jax.random.normal(ks[2], (DIM, DIM), dtype=jnp.float32) * s, 'att_src1': jax.random.normal(ks[3], (DIM,), dtype=jnp.float32) * s, 'att_dst1': jax.random.normal(ks[4], (DIM,), dtype=jnp.float32) * s, 'b1': jnp.zeros((DIM,), dtype=jnp.float32), 'W2': jax.random.normal(ks[5], (DIM, DIM), dtype=jnp.float32) * s, 'att_src2': jax.random.normal(ks[6], (DIM,), dtype=jnp.float32) * s, 'att_dst2': jax.random.normal(ks[7], (DIM,), dtype=jnp.float32) * s, 'b2': jnp.zeros((DIM,), dtype=jnp.float32)}
        return inp
    _L2_gnn_all = _L2_gnn_setup()
    _L2_gnn_in = {k: v for k, v in _L2_gnn_all.items() if k in ('W1', 'att_src1', 'att_dst1', 'b1', 'W2', 'att_src2', 'att_dst2', 'b2')}
    del _L2_gnn_all

    def _L3_gnn_setup():
        import jax, jax.numpy as jnp
        import numpy as np
        N_NODES = 1250
        D = 768
        N_EDGES = 20000

        def gcn_conv(x, W, b, src, dst, n_nodes):
            h = x @ W
            deg = jax.ops.segment_sum(jnp.ones_like(dst, dtype=h.dtype), dst, num_segments=n_nodes)
            dinv = jnp.where(deg > 0, jax.lax.rsqrt(deg), 0.0)
            norm = dinv[src] * dinv[dst]
            msgs = h[src] * norm[:, None]
            out = jax.ops.segment_sum(msgs, dst, num_segments=n_nodes)
            return out + b

        def add_self_loops(edge_index, n_nodes):
            loop = jnp.arange(n_nodes, dtype=edge_index.dtype)
            src = jnp.concatenate([edge_index[0], loop])
            dst = jnp.concatenate([edge_index[1], loop])
            return (src, dst)
        key = jax.random.key(seed)
        k1, k2, k3, k4 = jax.random.split(key, 4)
        x = jax.random.normal(k1, (N_NODES, D), dtype=jnp.float32)
        edge_index = jax.random.randint(k2, (2, N_EDGES), 0, N_NODES, dtype=jnp.int32)
        glorot = float(np.sqrt(6.0 / (D + D)))
        W1 = jax.random.uniform(k3, (D, D), jnp.float32, -glorot, glorot)
        W2 = jax.random.uniform(k4, (D, D), jnp.float32, -glorot, glorot)
        b1 = jnp.zeros((D,), jnp.float32)
        b2 = jnp.zeros((D,), jnp.float32)
        return {'x': x, 'W1': W1, 'b1': b1, 'W2': W2, 'b2': b2, 'edge_index': edge_index}
    _L3_gnn_all = _L3_gnn_setup()
    _L3_gnn_in = {k: v for k, v in _L3_gnn_all.items() if k in ('W1', 'b1', 'W2', 'b2')}
    del _L3_gnn_all
    return {'x': x, 'src': src, 'dst': dst, 'L0_gnn_W1': _L0_gnn_in['W1'], 'L0_gnn_a1_src': _L0_gnn_in['a1_src'], 'L0_gnn_a1_dst': _L0_gnn_in['a1_dst'], 'L0_gnn_b1': _L0_gnn_in['b1'], 'L0_gnn_W2': _L0_gnn_in['W2'], 'L0_gnn_a2_src': _L0_gnn_in['a2_src'], 'L0_gnn_a2_dst': _L0_gnn_in['a2_dst'], 'L0_gnn_b2': _L0_gnn_in['b2'], 'L1_gnn_W': _L1_gnn_in['W'], 'L1_gnn_b': _L1_gnn_in['b'], 'L2_gnn_W1': _L2_gnn_in['W1'], 'L2_gnn_att_src1': _L2_gnn_in['att_src1'], 'L2_gnn_att_dst1': _L2_gnn_in['att_dst1'], 'L2_gnn_b1': _L2_gnn_in['b1'], 'L2_gnn_W2': _L2_gnn_in['W2'], 'L2_gnn_att_src2': _L2_gnn_in['att_src2'], 'L2_gnn_att_dst2': _L2_gnn_in['att_dst2'], 'L2_gnn_b2': _L2_gnn_in['b2'], 'L3_gnn_W1': _L3_gnn_in['W1'], 'L3_gnn_b1': _L3_gnn_in['b1'], 'L3_gnn_W2': _L3_gnn_in['W2'], 'L3_gnn_b2': _L3_gnn_in['b2']}

def reference(x, src, dst, L0_gnn_W1, L0_gnn_a1_src, L0_gnn_a1_dst, L0_gnn_b1, L0_gnn_W2, L0_gnn_a2_src, L0_gnn_a2_dst, L0_gnn_b2, L1_gnn_W, L1_gnn_b, L2_gnn_W1, L2_gnn_att_src1, L2_gnn_att_dst1, L2_gnn_b1, L2_gnn_W2, L2_gnn_att_src2, L2_gnn_att_dst2, L2_gnn_b2, L3_gnn_W1, L3_gnn_b1, L3_gnn_W2, L3_gnn_b2):
    import jax
    import jax.numpy as jnp

    def _L0_gnn_ref(x, edge_index, W1, a1_src, a1_dst, b1, W2, a2_src, a2_dst, b2):
        import jax, jax.numpy as jnp
        import numpy as np
        N_NODES = 1250
        N_EDGES = 10000
        IN_DIM, HID, OUT_DIM, HEADS = (768, 512, 768, 4)
        NEG_SLOPE = 0.2

        def _gat_layer(x, src, dst, W, a_src, a_dst, b, heads, d_out, concat):
            N = x.shape[0]
            h = (x @ W).reshape(N, heads, d_out)
            as_n = jnp.einsum('nhd,hd->nh', h, a_src)
            ad_n = jnp.einsum('nhd,hd->nh', h, a_dst)
            e = jax.nn.leaky_relu(as_n[src] + ad_n[dst], NEG_SLOPE)
            e_max = jax.lax.stop_gradient(jax.ops.segment_max(e, dst, num_segments=N))
            ex = jnp.exp(e - e_max[dst])
            denom = jax.ops.segment_sum(ex, dst, num_segments=N)
            alpha = ex / (denom[dst] + 1e-16)
            msg = alpha[:, :, None] * h[src]
            out = jax.ops.segment_sum(msg, dst, num_segments=N)
            out = out.reshape(N, heads * d_out) if concat else out.mean(axis=1)
            return out + b
        N = x.shape[0]
        loops = jnp.arange(N, dtype=edge_index.dtype)
        src = jnp.concatenate([edge_index[0], loops])
        dst = jnp.concatenate([edge_index[1], loops])
        h = _gat_layer(x, src, dst, W1, a1_src, a1_dst, b1, HEADS, HID, True)
        h = jax.nn.elu(h)
        out = _gat_layer(h, src, dst, W2, a2_src, a2_dst, b2, 1, OUT_DIM, False)
        return out

    def _L1_gnn_ref(x, edge_index, W, b):
        import jax, jax.numpy as jnp
        import numpy as np
        N_NODES = 1250
        N_EDGES = 12500
        DIM = 768
        n = x.shape[0]
        loop = jnp.arange(n, dtype=edge_index.dtype)
        src = jnp.concatenate([edge_index[0], loop])
        dst = jnp.concatenate([edge_index[1], loop])
        deg = jax.ops.segment_sum(jnp.ones_like(dst, dtype=x.dtype), dst, num_segments=n)
        deg_inv_sqrt = jnp.where(deg > 0, jax.lax.rsqrt(deg), 0.0)
        norm = deg_inv_sqrt[src] * deg_inv_sqrt[dst]
        h = x @ W
        msg = h[src] * norm[:, None]
        out = jax.ops.segment_sum(msg, dst, num_segments=n)
        return out + b

    def _L2_gnn_ref(x, edge_index, W1, att_src1, att_dst1, b1, W2, att_src2, att_dst2, b2):
        import jax, jax.numpy as jnp
        import numpy as np
        N_NODES = 1250
        N_EDGES = 12500
        DIM = 768
        NEG_SLOPE = 0.2

        def gat_conv(x, src, dst, W, att_src, att_dst, bias, num_nodes):
            h = x @ W
            a_s = h @ att_src
            a_d = h @ att_dst
            e = jax.nn.leaky_relu(a_s[src] + a_d[dst], NEG_SLOPE)
            m = jax.ops.segment_max(e, dst, num_segments=num_nodes)
            e = jnp.exp(e - m[dst])
            denom = jax.ops.segment_sum(e, dst, num_segments=num_nodes)
            alpha = e / denom[dst]
            msg = alpha[:, None] * h[src]
            out = jax.ops.segment_sum(msg, dst, num_segments=num_nodes)
            return out + bias
        n = x.shape[0]
        loops = jnp.arange(n, dtype=edge_index.dtype)
        src = jnp.concatenate([edge_index[0], loops])
        dst = jnp.concatenate([edge_index[1], loops])
        h = gat_conv(x, src, dst, W1, att_src1, att_dst1, b1, n)
        h = jax.nn.relu(h)
        out = gat_conv(h, src, dst, W2, att_src2, att_dst2, b2, n)
        return out

    def _L3_gnn_ref(x, W1, b1, W2, b2, edge_index):
        import jax, jax.numpy as jnp
        import numpy as np
        N_NODES = 1250
        D = 768
        N_EDGES = 20000

        def gcn_conv(x, W, b, src, dst, n_nodes):
            h = x @ W
            deg = jax.ops.segment_sum(jnp.ones_like(dst, dtype=h.dtype), dst, num_segments=n_nodes)
            dinv = jnp.where(deg > 0, jax.lax.rsqrt(deg), 0.0)
            norm = dinv[src] * dinv[dst]
            msgs = h[src] * norm[:, None]
            out = jax.ops.segment_sum(msgs, dst, num_segments=n_nodes)
            return out + b

        def add_self_loops(edge_index, n_nodes):
            loop = jnp.arange(n_nodes, dtype=edge_index.dtype)
            src = jnp.concatenate([edge_index[0], loop])
            dst = jnp.concatenate([edge_index[1], loop])
            return (src, dst)
        n = x.shape[0]
        src, dst = add_self_loops(edge_index, n)
        h = gcn_conv(x, W1, b1, src, dst, n)
        h = jax.nn.relu(h)
        out = gcn_conv(h, W2, b2, src, dst, n)
        return out
    edge_index = jnp.stack([src, dst])
    x = _layernorm(x + _L0_gnn_ref(x, edge_index, L0_gnn_W1, L0_gnn_a1_src, L0_gnn_a1_dst, L0_gnn_b1, L0_gnn_W2, L0_gnn_a2_src, L0_gnn_a2_dst, L0_gnn_b2), axis=-1)
    x = _layernorm(x + _L1_gnn_ref(x, edge_index, L1_gnn_W, L1_gnn_b), axis=-1)
    x = _layernorm(x + _L2_gnn_ref(x, edge_index, L2_gnn_W1, L2_gnn_att_src1, L2_gnn_att_dst1, L2_gnn_b1, L2_gnn_W2, L2_gnn_att_src2, L2_gnn_att_dst2, L2_gnn_b2), axis=-1)
    x = _layernorm(x + _L3_gnn_ref(x, L3_gnn_W1, L3_gnn_b1, L3_gnn_W2, L3_gnn_b2, edge_index), axis=-1)
    return x

_drawn_inputs = setup_inputs


def setup_inputs(seed=0):
    import zlib

    import numpy as np

    out = dict(_drawn_inputs(seed))
    spreads = {'L0_gnn_b1': (0.0, 0.1),
     'L0_gnn_b2': (0.0, 0.1),
     'L1_gnn_b': (0.0, 0.1),
     'L2_gnn_b1': (0.0, 0.1),
     'L2_gnn_b2': (0.0, 0.1),
     'L3_gnn_b1': (0.0, 0.1),
     'L3_gnn_b2': (0.0, 0.1)}
    factors = {'L2_gnn_att_dst1': 6.086, 'L2_gnn_att_src2': 7.214, 'L2_gnn_att_dst2': 8.0}
    for name, (base, spread) in spreads.items():
        noise = np.random.default_rng([zlib.crc32(name.encode()), seed]).standard_normal(out[name].shape)
        drawn = base * np.exp(spread * noise) if base else spread * noise
        out[name] = jnp.asarray(drawn.astype(out[name].dtype))
    for name, factor in factors.items():
        out[name] = (out[name] * factor).astype(out[name].dtype)
    return out
```

```python
from collections import namedtuple
from contextlib import ExitStack

import concourse.bass as bass
from concourse import mybir

F32, F32R, BF16, F16 = mybir.dt.float32, mybir.dt.float32r, mybir.dt.bfloat16, mybir.dt.float16
I32, I16 = mybir.dt.int32, mybir.dt.int16
ALU = mybir.AluOpType
ACT = mybir.ActivationFunctionType
AX = mybir.AxisListType
ds = bass.ds

N, D, E = 1250, 768, 20000
HEADS, HID = 4, 512
P = 125
T = N // P
KD = D // 128
KH = HID // 128
HALF = D // 2
HW = D + 2
TW, TS = 418, 416
NC1 = 3
BW = 2 * P
NC2 = T // 2
RING = 5
SLOPE = 0.2
EPS = 1e-5
EXACT = 4096.0
NONE = -1e30

EC = E // P
PER = EC // T
SLACK = 3
WIN = PER + 2 * SLACK
ECP = EC + 2 * SLACK
OH = 4
MID = 4
TURN_AT = 7
GRAPH_STEPS = 4 + 2 + 2 + 2 + 4 + T + 2

Stages = namedtuple("Stages", "graph turn_input weights scores product columns across along fold degree_row")

assert NC2 % 2 == 1 and T % 2 == 0 and T % RING == 0 and (WIN - 2) % OH == 0 and (ECP - 2) % OH == 0
assert TS * (NC1 - 1) + TW == N and EC * P == E and EC % 2 == 0 and PER * T == EC


def build(nc, x, src, dst, L0_W1, L0_a1s, L0_a1d, L0_b1, L0_W2, L0_a2s, L0_a2d, L0_b2, L1_W, L1_b,
          L2_W1, L2_a1s, L2_a1d, L2_b1, L2_W2, L2_a2s, L2_a2d, L2_b2, L3_W1, L3_b1, L3_W2, L3_b2, out):
    counts_dram = nc.dram_tensor("counts_dram", (T, P, N), I16, kind="Internal").ap()
    masks_dram = nc.dram_tensor("masks_dram", (T, P, N), BF16, kind="Internal").ap()
    heads_dram = nc.dram_tensor("heads_dram", (T, P, D), F32, kind="Internal").ap()
    y_dram = [nc.dram_tensor(f"y{n}_dram", (T, P, D), F32, kind="Internal").ap() for n in range(3)]
    x_blocks = x.rearrange("(t p) f -> t p f", p=P)
    out_blocks = out.rearrange("(t p) f -> t p f", p=P)

    with ExitStack() as ctx:
        place = [0]

        def at(name, shape, dt, offset=None):
            size = mybir.dt.size(dt)
            for n in shape[1:]:
                size *= n
            if offset is None:
                offset = place[0]
                place[0] += (size + 31) // 32 * 32
            return nc.alloc_sbuf_tensor_at(name, shape, dt, offset=offset)

        base0 = nc.sbuf_base
        place[0] = (base0 + 31) // 32 * 32

        def sem(name):
            return ctx.enter_context(nc.semaphore(name))

        XT = at("XT", [128, KD, N], F32)
        ys_hi = at("ys_hi", [128, 2, KD, P], F32R)
        ys_lo = at("ys_lo", [128, 2, KD, P], F32R)
        h_at = place[0]
        h_hi = at("h_hi", [P, T * HW], F32R)
        h_lo_at = place[0]
        h_lo = at("h_lo", [P, T * HW], F32R)
        w_hi = at("w_hi", [128, KD * D], F32R)
        w_lo = at("w_lo", [128, KD * D], F32R)
        x_row = at("x_row", [128, N], F32)
        y_row = at("y_row", [P, N], F32)
        tb_at = place[0]
        tb = at("tb", [P, RING, TW], F32)
        p_hi = at("p_hi", [P, RING, TW], F32R)
        p_lo = at("p_lo", [P, RING, TW], F32R)
        c_in = at("c_in", [P, RING, TW], I16)
        acc = at("acc", [P, TW], F32)
        r_row = at("r_row", [128, TW], F32)
        ws = at("ws", [128, 2, D], F32)
        ev = at("ev", [128, 4, D], F32)
        bias_row = at("bias_row", [P, D], F32)
        a_row = at("a_row", [128, 2, D], F32)
        ident = at("ident", [128, 128], F32)
        ones = at("ones", [P, 1], F32)
        wa = at("wa", [128, KD, 2], F32)
        score = at("score", [P, T, 2], F32)
        score_sum = at("score_sum", [P, T, 2], F32)
        s08 = at("s08", [P, T], F32)
        s02 = at("s02", [P, T], F32)
        pair_max = at("pair_max", [P, 2], F32)
        amax = at("amax", [P, T], F32)
        mcol = at("mcol", [P, T], F32)
        xcol = at("xcol", [P, T], F32)
        ycol = at("ycol", [P, T], F32)
        deg = at("deg", [P, T], F32)
        dinv = at("dinv", [P, T], F32)
        b_col = at("b_col", [128, HEADS * KH + 2 * KD], F32)
        rden = at("rden", [P, 2, 2], F32)
        stats = at("stats", [P, 2, 2, 6], F32)
        mv = at("mv", [P, 2, 2], F32)
        rstd = at("rstd", [P, 2], F32)
        eps_col = at("eps_col", [P, 1], F32)
        params = at("params", [1, 4], I32)
        assert place[0] <= nc.sbuf_usable_end, (place[0], nc.sbuf_usable_end)

        ot = [at(f"ot{i}", [128, KH // 2, N], F32, offset=o + T * HID * 4) for i, o in enumerate((h_at, h_lo_at))]
        junk = at("junk", [P, N], BF16, offset=tb_at)
        mask_in = [at(f"mask_in{i}", [P, N], BF16, offset=tb_at + 2528 * (i + 1)) for i in range(2)]
        g = [h_at]

        def graph(name, shape, dt):
            size = mybir.dt.size(dt)
            for n in shape[1:]:
                size *= n
            g[0] += (size + 31) // 32 * 32
            return at(name, shape, dt, offset=g[0] - (size + 31) // 32 * 32)

        iota_i = graph("iota_i", [P, N], I32)
        iota = graph("iota", [P, N], F16)
        oh_src = graph("oh_src", [P, OH, N], BF16)
        oh_dst = graph("oh_dst", [P, OH, P], BF16)
        ct = graph("ct", [P, N], F32)
        c_out = graph("c_out", [P, T, P], I16)
        m_out = graph("m_out", [P, N], BF16)
        e_int = graph("e_int", [EC // 2, 2, BW], I32)
        e_flt = graph("e_flt", [EC // 2, 2, BW], F32)
        src_col = graph("src_col", [P, ECP], F32)
        dst_col = graph("dst_col", [P, ECP], F32)
        lim_i = graph("lim_i", [P, 2, 12 * PER], I32)
        lim = graph("lim", [P, 2, 12 * PER], F32)
        out_of = graph("out_of", [P, 2, EC], F32)
        bad = graph("bad", [P, 1], F32)
        many = graph("many", [P, T], F32)
        many_any = graph("many_any", [P, 1], F32)
        par_f = graph("par_f", [1, 4], F32)
        zeros = graph("zeros", [P, D], F32)
        assert g[0] <= h_at + 2 * T * HW * 4

        ps = ctx.enter_context(nc.psum_tensor("ps", [128, 8, 512], F32))

        edges_in, graph_const, graph_step = sem("edges_in"), sem("graph_const"), sem("graph_step")
        edges_flt, edges_turned, edges_col = sem("edges_flt"), sem("edges_turned"), sem("edges_col")
        bad_ready, bad_summed, par_ready = sem("bad_ready"), sem("bad_summed"), sem("par_ready")
        oh_ready, oh_used, ct_summed, ct_out = sem("oh_ready"), sem("oh_used"), sem("ct_summed"), sem("ct_out")
        ct_loop, ct_deg, ct_turned, c_ready = sem("ct_loop"), sem("ct_deg"), sem("ct_turned"), sem("c_ready")
        m_ready, c_stored, m_stored = sem("m_ready"), sem("c_stored"), sem("m_stored")
        many_ready, many_summed, low_ready = sem("many_ready"), sem("many_summed"), sem("low_ready")
        root, dinv_ready, zeroed = sem("root"), sem("dinv_ready"), sem("zeroed")
        held = sem("held")
        x_in = [sem(f"x_in{i}") for i in range(2)]
        y_ready, y_turned, xt_ready = sem("y_ready"), sem("y_turned"), sem("xt_ready")
        w_in = [sem(f"w_in{i}") for i in range(2)]
        a_in, w_high, w_low, w_dot = sem("a_in"), sem("w_high"), sem("w_low"), sem("w_dot")
        split_high, split_low, gemm_done = sem("split_high"), sem("split_low"), sem("gemm_done")
        gemm_act, gemm_dve = sem("gemm_act"), sem("gemm_dve")
        fold_act, fold_dve = sem("fold_act"), sem("fold_dve")
        sum_in, sum_added = [sem(f"sum_in{i}") for i in range(2)], [sem(f"sum_added{i}") for i in range(2)]
        ones_set = sem("ones_set")
        score_mm, score_ready, row_mm, row_ready = sem("score_mm"), sem("score_ready"), sem("row_mm"), sem("row_ready")
        mask_ld = [sem(f"mask_ld{i}") for i in range(2)]
        maxed, step, xy_ready, amax_ready = sem("maxed"), sem("step"), sem("xy_ready"), sem("amax_ready")
        c_ld = [sem(f"c_ld{i}") for i in range(RING)]
        t_ready, e_ready, p_ready = sem("t_ready"), sem("e_ready"), sem("p_ready")
        p_high, p_low, tile_used, acc_done = sem("p_high"), sem("p_low"), sem("tile_used"), sem("acc_done")
        den_mm, r_ready, agg_mm = sem("den_mm"), sem("r_ready"), sem("agg_mm")
        ev_scaled, ev_act, ev_exp, ev_done = sem("ev_scaled"), sem("ev_act"), sem("ev_exp"), sem("ev_done")
        b_in = sem("b_in")
        agg2_mm, agg2_read, res_in, res_ready = sem("agg2_mm"), sem("agg2_read"), [sem(f"res_in{i}") for i in range(2)], sem("res_ready")
        bias_in, var_ready, std_ready, ln_step = sem("bias_in"), sem("var_ready"), sem("std_ready"), sem("ln_step")
        stored = [sem(f"stored{i}") for i in range(2)]

        START = dict(wp=0, dot=0, av=0, q=0, sp=0, sc=0, rows=0, mp=0, step=GRAPH_STEPS, xy=0, tile=0, gat=0,
                     acc=0, c1=0, f1=0, den=0, elu=0, c2=0, y=T, ln=0, chunks=0)
        HEAD = dict(wp=(KD + KH) // 2, dot=KD + KH, av=2, q=2 * T, sp=T // 2, sc=2, rows=3, mp=T // 2,
                    step=5 + NC1, xy=1, tile=T * NC1, gat=T * NC1, acc=T * NC1, c1=NC1, f1=KH * NC1, den=NC1,
                    elu=KH * NC1, c2=0, y=0, ln=0, chunks=NC1)

        def in_head(hd):
            return {k: START[k] + HEAD[k] * hd for k in START}

        def after_heads():
            return {k: START[k] + HEAD[k] * HEADS for k in START}

        def weights_of(name, hd=None):
            if name == "L0_W1":
                return KD, HID, lambda k: L0_W1[k * 128:(k + 1) * 128, ds(hd * HID, HID)]
            if name == "L0_W2":
                return KH, D, lambda k: L0_W2[ds(hd * HID + k * 128, 128), :]
            w = {"L1_W": L1_W, "L2_W1": L2_W1, "L2_W2": L2_W2, "L3_W1": L3_W1, "L3_W2": L3_W2}[name]
            return KD, D, lambda k: w[k * 128:(k + 1) * 128, :]

        def vectors_of(name, hd=None):
            if name == "L0_W1":
                return L0_a1s[ds(hd, 1), :], L0_a1d[ds(hd, 1), :]
            if name == "L0_W2":
                return L0_a2s, L0_a2d
            if name == "L2_W1":
                return L2_a1s.rearrange("(a f) -> a f", a=1), L2_a1d.rearrange("(a f) -> a f", a=1)
            if name == "L2_W2":
                return L2_a2s.rearrange("(a f) -> a f", a=1), L2_a2d.rearrange("(a f) -> a f", a=1)
            return None

        def sources(kb):
            return [(XT, 0)] if kb == KD else [(ot[0], 0), (ot[1], KH // 2)]

        def source_block(kb, k, cols):
            return XT[:, k, cols] if kb == KD else ot[k // (KH // 2)][:, k % (KH // 2), cols]

        def h_view(h, width):
            return (h[:, 0:T * HID].rearrange("p (t f) -> p t f", f=HID) if width == HID
                    else h[:].rearrange("p (t f) -> p t f", f=HW))

        def h_block(h, width, t):
            v = h_view(h, width)[:, ds(t, 1), 0:width]
            return (v.rearrange("p t f -> p (t f)") if width == HID
                    else v.rearrange("p t (b f) -> p (t b) f", b=2))

        def ps_block(r, width):
            return ps[:P, 2 * r, 0:HID] if width == HID else ps[:P, 2 * r:2 * r + 2, 0:HALF]

        def halves(tile):
            return tile.rearrange("p (b f) -> p b f", b=2)

        def blocks_ahead(prepare, finish):
            def run(eng):
                prepare(0, 0)
                with eng.Fori(0, T // 2 - 1) as i:
                    for r in range(2):
                        prepare(2 * i + r + 1, (r + 1) % 2)
                        finish(2 * i + r, r, i)
                prepare(T - 1, 1)
                finish(T - 2, 0, T // 2 - 1)
                finish(T - 1, 1, T // 2 - 1)
            return run

        def program(eng, do):
            do.graph()
            do.turn_input()
            with eng.Fori(0, HEADS) as hd:
                n = in_head(hd)
                do.weights(n, "L0_W1", hd)
                n = dict(n, wp=n["wp"] + KD // 2, dot=n["dot"] + KD, av=n["av"] + 1)
                do.scores(n, KD, "use")
                n = dict(n, sc=n["sc"] + 1, rows=n["rows"] + 1, step=n["step"] + 2)
                do.product(n, KD, HID, True, None, "h")
                n = dict(n, q=n["q"] + T, mp=n["mp"] + T // 2)
                do.columns(n)
                n = dict(n, xy=n["xy"] + 1, rows=n["rows"] + 2, step=n["step"] + 3)
                do.across(n, "gat", KH, "elu", hd * KH, ("L0_W2", hd), 1e-16)
                n = dict(n, wp=n["wp"] + KH // 2, dot=n["dot"] + KH, av=n["av"] + 1, chunks=n["chunks"] + NC1, tile=n["tile"] + T * NC1,
                         gat=n["gat"] + T * NC1, acc=n["acc"] + T * NC1, c1=n["c1"] + NC1, den=n["den"] + NC1,
                         f1=n["f1"] + KH * NC1, elu=n["elu"] + KH * NC1, step=n["step"] + NC1)
                do.scores(n, KH, "add")
                n = dict(n, sc=n["sc"] + 1)
                do.product(n, KH, D, False, None, "sum")
            n = after_heads()
            do.fold(n)
            n = dict(n, mp=n["mp"] + T // 2, step=n["step"] + 3, rows=n["rows"] + 1)
            do.columns(n)
            n = dict(n, xy=n["xy"] + 1, rows=n["rows"] + 2, step=n["step"] + 3)
            do.along(n, "gat", 0, ("L1_W", None), 1e-16)
            n = after_along(n, "gat", "L1_W", 1e-16)

            do.product(n, KD, D, False, dinv, "h")
            n = dict(n, q=n["q"] + T)
            do.along(n, "gcn", 1, ("L2_W1", None), 0.0)
            n = after_along(n, "gcn", "L2_W1", 0.0)

            do.scores(n, KD, "use")
            n = dict(n, sc=n["sc"] + 1, rows=n["rows"] + 1, step=n["step"] + 2)
            do.product(n, KD, D, True, None, "h")
            n = dict(n, q=n["q"] + T, mp=n["mp"] + T // 2)
            do.columns(n)
            n = dict(n, xy=n["xy"] + 1, rows=n["rows"] + 2, step=n["step"] + 3)
            do.across(n, "gat", KD, "relu", HEADS * KH, ("L2_W2", None), 0.0)
            n = dict(n, wp=n["wp"] + KD // 2, dot=n["dot"] + KD, av=n["av"] + 1, chunks=n["chunks"] + NC1, tile=n["tile"] + T * NC1,
                     gat=n["gat"] + T * NC1, acc=n["acc"] + T * NC1, c1=n["c1"] + NC1, den=n["den"] + NC1,
                     f1=n["f1"] + KD * NC1)
            do.scores(n, KD, "use")
            n = dict(n, sc=n["sc"] + 1, rows=n["rows"] + 1, step=n["step"] + 2)
            do.product(n, KD, D, True, None, "h")
            n = dict(n, q=n["q"] + T, mp=n["mp"] + T // 2)
            do.columns(n)
            n = dict(n, xy=n["xy"] + 1, rows=n["rows"] + 2, step=n["step"] + 3)
            do.along(n, "gat", 2, ("L3_W1", None), 0.0)
            n = after_along(n, "gat", "L3_W1", 0.0)

            do.product(n, KD, D, False, dinv, "h")
            n = dict(n, q=n["q"] + T)
            do.degree_row(n)
            n = dict(n, rows=n["rows"] + 1)
            do.across(n, "gcn", KD, "relu", HEADS * KH + KD, ("L3_W2", None), 0.0)
            n = dict(n, wp=n["wp"] + KD // 2, chunks=n["chunks"] + NC1, tile=n["tile"] + T * NC1, c1=n["c1"] + NC1, f1=n["f1"] + KD * NC1)
            do.product(n, KD, D, False, dinv, "h")
            n = dict(n, q=n["q"] + T)
            do.along(n, "gcn", 3, None, 0.0)
        def ln_links(kind, eps):
            return (0 if kind == "gcn" else 4 if eps else 2) + 5

        def after_along(n, kind, following, eps):
            n = dict(n, chunks=n["chunks"] + NC2, tile=n["tile"] + T * NC2, c2=n["c2"] + NC2, y=n["y"] + T, wp=n["wp"] + KD // 2,
                     ln=n["ln"] + NC2 * ln_links(kind, eps))
            if kind == "gat":
                n["gat"] += T * NC2
            if vectors_of(following) is not None:
                n = dict(n, dot=n["dot"] + KD, av=n["av"] + 1)
            return n

        C_T = counts_dram.rearrange("t p n -> p t n")
        PASSES = ((0, 0), (0, 1), (1, 0))

        def hold(eng, semaphore, value):
            eng.wait_ge(semaphore, value)
            eng.sem_inc(held, 1)

        block = ctx.enter_context(nc.Block())

        @block.sync
        def _(sp):
            def graph():
                for i, e in enumerate((src, dst)):
                    sp.dma_start(e_int[:, i, :], e.rearrange("(q c) -> q c", c=BW)).then_inc(edges_in, 16)
                for i, (b, o, k) in enumerate(((L0_b1, 0, HEADS * KH), (L2_b1, HEADS * KH, KD),
                                               (L3_b1, HEADS * KH + KD, KD))):
                    sp.dma_start(b_col[:, o:o + k], b.rearrange("(k p) -> p k", p=128),
                                 allow_slow_non_contiguous=True).then_inc(b_in, 16)
                sp.wait_ge(graph_const, 2)
                for t in range(T):
                    sp.dma_start(heads_dram[t], zeros[:]).then_inc(zeroed, 16)
                with sp.Fori(0, T) as b:
                    hold(sp, m_ready, b + 1)
                    sp.dma_start(masks_dram[ds(b, 1)].rearrange("b p n -> (b p) n"), m_out[:]).then_inc(m_stored, 16)
                    hold(sp, c_ready, b + 1)
                    sp.dma_start(C_T[:, :, ds(b * P, P)], c_out[:]).then_inc(c_stored, 16)

            def turn_input():
                with sp.Fori(0, T // 2) as i:
                    for r in range(2):
                        hold(sp, y_turned, 2 * i + r + 1)
                        sp.dma_start(ev[:P, r, :], x_blocks[ds(2 * i + r, 1)].rearrange("t p f -> (t p) f")
                                     ).then_inc(x_in[r], 16)
                sp.wait_ge(c_stored, 16 * T)
                sp.wait_ge(m_stored, 16 * T)
                sp.wait_ge(zeroed, 16 * T)

            def vectors(n, name, hd):
                hold(sp, w_dot, 2 * n["dot"] + 4)
                for j, a in enumerate(vectors_of(name, hd)):
                    width = a.shape[1]
                    sp.dma_start(a_row[:, j, 0:width], a.broadcast_to([128, width])).then_inc(a_in, 16)

            def piece(n, name, hd, k):
                kb, width, rows = weights_of(name, hd)
                if k == 0 and vectors_of(name, hd) is not None:
                    vectors(n, name, hd)
                hold(sp, w_low, 2 * n["wp"] + k + 1)
                hold(sp, w_dot, 2 * n["dot"] + (4 if vectors_of(name, hd) is None else 2 * k + 2))
                sp.dma_start(ws[:, k % 2, 0:width], rows(k)).then_inc(w_in[k % 2], 16)

            def weights(n, name, hd):
                for k in range(weights_of(name, hd)[0]):
                    piece(n, name, hd, k)

            def masks_free(n):
                hold(sp, p_low, n["tile"] + RING)
                hold(sp, acc_done, n["acc"] + RING)

            def mask(n, i, r):
                hold(sp, maxed, 2 * n["mp"] + 2 * i + r + 1)
                sp.dma_start(mask_in[r][:], masks_dram[ds(2 * i + r, 1)].rearrange("t p n -> (t p) n")
                             ).then_inc(mask_ld[r], 16)

            def product(n, kb, width, maxima, scale, kind):
                if maxima:
                    masks_free(n)
                    with sp.Fori(0, T // 2) as i:
                        for r in range(2):
                            mask(n, i, r)

            def fold(n):
                masks_free(n)
                with sp.Fori(0, T // 2) as i:
                    for r in range(2):
                        if r == 0:
                            for q in range(2):
                                hold(sp, sum_added[q], 16 * n["sp"])
                        hold(sp, fold_dve, 2 * i + r + 1)
                        sp.dma_start(ev[:P, r, :], heads_dram[ds(2 * i + r, 1)].rearrange("t p f -> (t p) f")
                                     ).then_inc(sum_in[r], 16)
                        mask(n, i, r)

            def counts(n, c, cstat, width, off, hook):
                tile = n["tile"] + c * T
                for s in range(T):
                    hold(sp, p_low, tile + s + 1)
                    sp.dma_start(c_in[:, s % RING, 0:width], counts_dram[s][:, ds(off, width)]
                                 ).then_inc(c_ld[s % RING], 16)
                    hook(s)

            def hook_weights(n, following):
                def hook(s):
                    if following is not None and 0 <= s - 2 < weights_of(*following)[0]:
                        piece(n, *following, s - 2)
                return hook

            def across(n, kind, fb, act, bias, following, eps):
                counts(n, 0, 0, TW, 0, hook_weights(n, following))
                with sp.Fori(1, NC1) as c:
                    counts(n, c, 1, TW, c * TS, lambda s: None)

            def along(n, kind, layer, following, eps):
                hold(sp, ev_done, n["f1"] + 2)
                if layer:
                    for r in range(2):
                        hold(sp, stored[r], 16 * n["c2"])
                res = x_blocks if layer == 0 else y_dram[layer - 1]
                hold(sp, res_ready, 2 * n["c2"])
                last_bias = (L0_b2, L1_b, L2_b2, L3_b2)[layer]
                sp.dma_start(bias_row[:], last_bias.rearrange("(a f) -> a f", a=1).broadcast_to([P, D])
                             ).then_inc(bias_in, 16)

                def residual(c):
                    for r in range(2):
                        hold(sp, agg2_read, 2 * n["c2"] + 2 * c)
                        sp.dma_start(ev[:P, 2 + r, :], res[ds(2 * c + r, 1)].rearrange("t p f -> (t p) f")
                                     ).then_inc(res_in[r], 16)

                residual(0)
                counts(n, 0, 0, BW, 0, hook_weights(n, following))
                with sp.Fori(1, NC2) as c:
                    counts(n, c, 1, BW, c * BW, lambda s: residual(c) if s == 8 else None)

            def none(*_):
                pass

            program(sp, Stages(graph, turn_input, weights, none, product, none, across, along, fold, none))

        @block.gpsimd
        def _(pool):
            pool.sem_inc(w_low, 2)
            pool.sem_inc(acc_done, RING)

            def graph():
                nc.gpsimd.memset(ident[:], 0.0).then_inc(graph_step, 1)
                nc.gpsimd.memset(ones[:], 1.0).then_inc(graph_step, 1)
                pool.wait_ge(graph_step, 2)
                nc.gpsimd.affine_select(out=ident[:], in_=ident[:], compare_op=ALU.not_equal, fill=1.0, base=0,
                                        pattern=[[-1, 128]], channel_multiplier=1).then_inc(graph_const, 1)
                nc.gpsimd.memset(zeros[:], 0.0).then_inc(graph_const, 1)
                nc.gpsimd.iota(iota_i[:], pattern=[[1, N]], base=0, channel_multiplier=0).then_inc(graph_const, 1)
                nc.gpsimd.iota(lim_i[:, 0, :], pattern=[[P, 12], [0, PER]], base=-P,
                               channel_multiplier=0).then_inc(graph_const, 1)
                nc.gpsimd.iota(lim_i[:, 1, :], pattern=[[P, 12], [0, PER]], base=P,
                               channel_multiplier=0).then_inc(graph_const, 1)
                with pool.Fori(0, T) as b:
                    pool.wait_ge(ct_out, b + 1)
                    diagonal = ct[:, ds(b * P, P)]
                    nc.gpsimd.tensor_tensor(diagonal, diagonal, ident[:P, :P], ALU.add).then_inc(ct_loop, 1)
                    pool.wait_ge(ct_loop, b + 1)
                    hold(pool, m_stored, 16 * b)
                    nc.gpsimd.tensor_scalar(m_out[:], ct[:], 0.0, NONE, ALU.is_equal, ALU.mult).then_inc(m_ready, 1)

            def piece(n, name, hd, k):
                width = weights_of(name, hd)[1]
                pool.wait_ge(w_high, 2 * n["wp"] + k + 1)
                nc.gpsimd.tensor_tensor(w_lo[:, k * width:(k + 1) * width], ws[:, k % 2, 0:width],
                                        w_hi[:, k * width:(k + 1) * width].bitcast(F32),
                                        ALU.subtract).then_inc(w_low, 1)

            def weights(n, name, hd):
                for k in range(weights_of(name, hd)[0]):
                    piece(n, name, hd, k)

            def product(n, kb, width, maxima, scale, kind):
                if kind != "sum":
                    return
                pool.wait_ge(zeroed, 16 * T)
                with pool.Fori(0, T // 2) as i:
                    for r in range(2):
                        q = n["q"] + 2 * i + r
                        pool.wait_ge(gemm_act, q + 3)
                        pool.wait_ge(gemm_dve, q + 3)
                        pool.dma_start(heads_dram[ds(2 * i + r, 1)].rearrange("t p f -> (t p) f"), ev[:P, r, :],
                                       accum_op=ALU.add).then_inc(sum_added[r], 16)

            def hook_weights(n, following, s):
                if following is not None and 0 <= s - 2 < weights_of(*following)[0]:
                    piece(n, *following, s - 2)

            def sum_tiles(n, c, hook):
                g, a = n["gat"] + c * T, n["acc"] + c * T
                for s in range(T):
                    pool.wait_ge(p_ready, g + s + 1)
                    if s == 0:
                        hold(pool, den_mm, n["den"] + c)
                        nc.gpsimd.tensor_copy(acc[:], tb[:, 0, :]).then_inc(acc_done, 1)
                    else:
                        pool.wait_ge(acc_done, a + s + RING)
                        nc.gpsimd.tensor_tensor(acc[:], acc[:], tb[:, s % RING, :], ALU.add).then_inc(acc_done, 1)
                    hook(s)

            def elu_part(n, c, fb):
                for f in range(fb):
                    e = n["elu"] + c * fb + f
                    hold(pool, ev_act, 2 * e + 1)
                    nc.gpsimd.tensor_scalar(ev[:, 2 + f % 2, 0:TW], ev[:, 2 + f % 2, 0:TW], 1.0, -1.0,
                                            ALU.min, ALU.add).then_inc(ev_exp, 1)

            def across(n, kind, fb, act, bias, following, eps):
                if kind == "gat":
                    sum_tiles(n, 0, lambda s: hook_weights(n, following, s))
                else:
                    for s in range(T):
                        hook_weights(n, following, s)
                with pool.Fori(1, NC1) as c:
                    if kind == "gat":
                        sum_tiles(n, c, lambda s: elu_part(n, c - 1, fb) if s == MID - 1 and act == "elu" else None)
                if act == "elu":
                    elu_part(n, NC1 - 1, fb)

            def along(n, kind, layer, following, eps):
                dest = out_blocks if layer == 3 else y_dram[layer]

                def residual(c):
                    for r in range(2):
                        pool.wait_ge(bias_in, 16 * (layer + 1))
                        pool.wait_ge(res_in[r], 16 * (n["c2"] + c + 1))
                        nc.gpsimd.tensor_tensor(ev[:P, 2 + r, :], ev[:P, 2 + r, :], bias_row[:],
                                                ALU.add).then_inc(res_ready, 1)

                def store(c):
                    for r in range(2):
                        pool.wait_ge(y_ready, 2 * (n["c2"] + c) + r + 1)
                        pool.dma_start(dest[ds(2 * c + r, 1)].rearrange("t p f -> (t p) f"), ev[:P, r, :]
                                       ).then_inc(stored[r], 16)

                residual(0)
                for s in range(T):
                    hook_weights(n, following, s)
                with pool.Fori(1, NC2) as c:
                    store(c - 1)
                    residual(c)
                store(NC2 - 1)
                if layer == 3:
                    for r in range(2):
                        pool.wait_ge(stored[r], 16 * (n["c2"] + NC2))

            def none(*_):
                pass

            program(pool, Stages(graph, none, weights, none, product, none, across, along, none, none))

        @block.scalar
        def _(act):
            def graph():
                with act.Fori(0, T) as b:
                    act.wait_ge(ct_summed, b + 1)
                    act.wait_ge(ct_turned, b)
                    act.wait_ge(m_ready, b)
                    act.wait_ge(ct_deg, b)
                    for j in range(3):
                        o, w = (TW + TS * (j - 1), TS) if j else (0, TW)
                        last = nc.scalar.activation(ct[:, o:o + w], ps[:P, j, 0:w], ACT.Copy)
                    last.then_inc(ct_out, 1)
                    act.wait_ge(ct_turned, b + 1)
                    act.wait_ge(c_stored, 16 * b)
                    for j in range(3):
                        k = min(4, T - 4 * j)
                        last = nc.scalar.activation(c_out[:, 4 * j:4 * j + k, :],
                                                    ps[:P, 4 + j, 0:k * P].rearrange("p (k q) -> p k q", q=P), ACT.Copy)
                    last.then_inc(c_ready, 1)
                act.wait_ge(ct_deg, T)
                nc.scalar.activation(dinv[:], deg[:], ACT.Sqrt).then_inc(root, 1)

            def turned(y, t, r, bank):
                act.wait_ge(y_turned, y + 3)
                for j in range(2):
                    last = nc.scalar.activation(XT[:, 3 * j:3 * j + 3, ds(t * P, P)],
                                                ps[:, bank + 2 * r + j, 0:3 * P].rearrange("p (k q) -> p k q", q=P), ACT.Copy)
                last.then_inc(xt_ready, 1)

            def turn_input():
                with act.Fori(0, T // 2) as i:
                    for r in range(2):
                        turned(2 * i + r, 2 * i + r, r, 4)

            def piece(n, name, hd, k):
                width = weights_of(name, hd)[1]
                if k == 0:
                    act.wait_ge(gemm_done, n["q"] + 2)
                act.wait_ge(w_in[k % 2], 16 * (n["wp"] + k // 2 + 1))
                nc.scalar.activation(w_hi[:, k * width:(k + 1) * width], ws[:, k % 2, 0:width],
                                     ACT.Copy).then_inc(w_high, 1)

            def weights(n, name, hd):
                for k in range(weights_of(name, hd)[0]):
                    piece(n, name, hd, k)

            def row(dest, parts, n, k):
                act.wait_ge(row_mm, n["rows"] + k + 1)
                for j in range(3):
                    w = min(4, T - 4 * j) * P
                    last = nc.scalar.activation(dest[:parts, 4 * P * j:4 * P * j + w], ps[:parts, 5 + j, 0:w], ACT.Copy)
                last.then_inc(row_ready, 1)

            def scores(n, kb, what):
                if what == "use":
                    act.wait_ge(t_ready, n["gat"])
                    row(x_row, P, n, 0)

            def product(n, kb, width, maxima, scale, kind):
                act.wait_ge(xt_ready, n["y"] + 2)
                act.wait_ge(ev_done, n["f1"] + 2)

                def prepare(t, r):
                    q = n["q"] + t
                    act.wait_ge(gemm_done, q + 1)
                    src_ = sources(kb)
                    for tile, k0 in src_:
                        kn = kb // len(src_)
                        last = nc.scalar.activation(ys_hi[:, r, k0:k0 + kn, :], tile[:, 0:kn, ds(t * P, P)], ACT.Copy)
                    last.then_inc(split_high, 1)

                def finish(t, r, i):
                    q = n["q"] + t
                    act.wait_ge(gemm_done, q + 3)
                    if kind == "sum":
                        act.wait_ge(sum_added[r], 16 * (n["sp"] + i))
                        nc.scalar.activation(ev[:P, r, 0:HALF], ps[:P, 2 * r, 0:HALF], ACT.Copy).then_inc(gemm_act, 1)
                    else:
                        nc.scalar.activation(h_block(h_hi, width, t), ps_block(r, width), ACT.Copy,
                                             scale=1.0 if scale is None else scale[:, ds(t, 1)]).then_inc(gemm_act, 1)

                if scale is not None:
                    act.wait_ge(dinv_ready, 1)
                blocks_ahead(prepare, finish)(act)

            def columns(n):
                act.wait_ge(maxed, 2 * n["mp"] + 2)
                row(x_row, P, n, 0)
                act.wait_ge(t_ready, n["gat"])
                row(y_row, P, n, 1)

            def degree_row(n):
                row(x_row, 128, n, 0)

            def fold(n):
                act.wait_ge(t_ready, n["gat"])
                row(x_row, P, n, 0)
                with act.Fori(0, T // 2) as i:
                    for r in range(2):
                        act.wait_ge(sum_in[r], 16 * (i + 1))
                        nc.scalar.activation(h_block(h_hi, D, 2 * i + r), halves(ev[:P, r, :]), ACT.Copy).then_inc(fold_act, 1)

            def tiles(n, c, kind, width, hook):
                t0, g = n["tile"] + c * T, n["gat"] + c * T

                def exp(s):
                    act.wait_ge(t_ready, g + s + 1)
                    nc.scalar.activation(tb[:, s % RING, 0:width], tb[:, s % RING, 0:width], ACT.Exp,
                                         bias=s02[:, s:s + 1]).then_inc(e_ready, 1)

                def high(s):
                    if kind == "gat":
                        act.wait_ge(p_ready, g + s + 1)
                        tile = tb[:, s % RING, 0:width]
                    else:
                        act.wait_ge(c_ld[s % RING], 16 * (2 * (n["chunks"] + c) + s // RING + 1))
                        tile = c_in[:, s % RING, 0:width]
                    act.wait_ge(tile_used, t0 + s + 1)
                    nc.scalar.activation(p_hi[:, s % RING, 0:width], tile, ACT.Copy).then_inc(p_high, 1)

                for s in range(T + 1):
                    if s < T and kind == "gat":
                        exp(s)
                    if s < T and kind == "gcn":
                        high(s)
                    if s >= 1 and kind == "gat":
                        high(s - 1)
                    hook(s)

            def hook_weights(n, following, s):
                if following is not None and 0 <= s - 2 < weights_of(*following)[0]:
                    piece(n, *following, s - 2)

            def across(n, kind, fb, what, bias, following, eps):
                act.wait_ge(b_in, 48)

                def finish(c):
                    for f in range(fb):
                        v = n["f1"] + c * fb + f
                        act.wait_ge(ev_scaled, v + 1)
                        z, b = ev[:, f % 2, 0:TW], b_col[:, ds(bias + f, 1)]
                        if what == "elu":
                            nc.scalar.activation(ev[:, 2 + f % 2, 0:TW], z, ACT.Exp, bias=b).then_inc(ev_act, 1)
                            hold(act, ev_act, 2 * (n["elu"] + c * fb + f) + 1)
                            nc.scalar.activation(z, z, ACT.Relu, bias=b).then_inc(ev_act, 1)
                        else:
                            nc.scalar.activation(XT[:, f, ds(c * TS, TW)], z, ACT.Relu, bias=b).then_inc(ev_done, 1)

                tiles(n, 0, kind, TW, lambda s: hook_weights(n, following, s))
                with act.Fori(1, NC1) as c:
                    tiles(n, c, kind, TW, lambda s: finish(c - 1) if s == MID else None)
                finish(NC1 - 1)

            def along(n, kind, layer, following, eps):
                def deviation(c):
                    act.wait_ge(var_ready, 2 * (n["c2"] + c) + 2)
                    nc.scalar.activation(rstd[:], mv[:, :, 1], ACT.Sqrt, bias=eps_col[:, 0:1]).then_inc(std_ready, 1)

                def turn(c, bank):
                    if layer < 3:
                        for r in range(2):
                            turned(n["y"] + 2 * c + r, 2 * c + r, r, bank)

                tiles(n, 0, kind, BW, lambda s: hook_weights(n, following, s))
                with act.Fori(0, NC2 // 2) as i:
                    for k, bank in ((0, 0), (1, 4)):
                        c = 2 * i + k
                        tiles(n, c + 1, kind, BW,
                              lambda s: deviation(c) if s == MID else turn(c, bank) if s == T else None)
                deviation(NC2 - 1)
                turn(NC2 - 1, 0)

            program(act, Stages(graph, turn_input, weights, scores, product, columns, across, along, fold, degree_row))

        @block.vector
        def _(dve):
            dve.sem_inc(w_dot, 4)
            dve.sem_inc(gemm_dve, 2)
            dve.sem_inc(gemm_act, 2)
            dve.sem_inc(maxed, 2)
            dve.sem_inc(fold_dve, 2)
            dve.sem_inc(p_low, RING)
            dve.sem_inc(ev_done, 2)

            def graph():
                chain = [0]

                def link(ins):
                    chain[0] += 1
                    ins.then_inc(step, 1)
                    dve.wait_ge(step, chain[0])

                link(nc.vector.memset(eps_col[:], EPS))
                link(nc.vector.memset(score_sum[:], 0.0))
                link(nc.vector.memset(src_col[:], 0.0))
                link(nc.vector.memset(dst_col[:], -1.0))
                dve.wait_ge(edges_in, 32)
                nc.vector.tensor_copy(e_flt[:], e_int[:]).then_inc(edges_flt, 1)
                dve.wait_ge(edges_turned, 1)
                for i, col in enumerate((src_col, dst_col)):
                    link(nc.vector.tensor_copy(col[:, SLACK:SLACK + EC].rearrange("p (q h) -> p h q", h=2),
                                               ps[:P, 4, i * EC:(i + 1) * EC].rearrange("p (h q) -> p h q", h=2)))
                dve.wait_ge(graph_const, 5)
                link(nc.vector.tensor_copy(iota[:], iota_i[:]))
                link(nc.vector.tensor_copy(lim[:], lim_i[:]))
                real = dst_col[:, SLACK:SLACK + EC]
                low = lim[:, 0, 2 * (PER - SLACK) - PER + SLACK:][:, 0:EC]
                high = lim[:, 1, 2 * SLACK:2 * SLACK + EC]
                link(nc.vector.tensor_tensor(out_of[:, 0, :], low, real, ALU.is_gt))
                link(nc.vector.tensor_tensor(out_of[:, 1, :], real, high, ALU.is_ge))
                nc.vector.tensor_reduce(bad[:], out_of[:].rearrange("p a c -> p (a c)"), AX.X, ALU.add
                                        ).then_inc(bad_ready, 1)
                dve.wait_ge(bad_summed, 1)
                link(nc.vector.tensor_scalar(par_f[:, 0:1], ps[0:1, 4, 0:1], 1.0, None, ALU.min))
                for j, (sorted_, all_) in enumerate((((WIN - 2) // OH, (ECP - 2) // OH), (PER, 0), (WIN, ECP))):
                    link(nc.vector.tensor_scalar(par_f[:, j + 1:j + 2], par_f[:, 0:1], float(all_ - sorted_),
                                                 float(sorted_), ALU.mult, ALU.add))
                nc.vector.tensor_copy(params[:], par_f[:]).then_inc(par_ready, 1)
                dve.wait_ge(par_ready, 1)
                turns = dve.value_load(params[0:1, 1:2], min_val=(WIN - 2) // OH, max_val=(ECP - 2) // OH)
                stride = dve.value_load(params[0:1, 2:3], min_val=0, max_val=PER)
                count = dve.value_load(params[0:1, 3:4], min_val=WIN, max_val=ECP)

                def one_hot(b, j, slot):
                    col = ds(nc.s_assert_within(stride * b + j, 0, ECP - 1, skip_runtime_bounds_check_because=
                                              "stride, turns and count come as (PER, ., WIN) or (0, ., ECP)"), 1)
                    dve.wait_ge(oh_used, count * b + j + 1)
                    nc.vector.tensor_scalar(oh_src[:, slot, :], iota[:], src_col[:, col], None, ALU.is_equal)
                    nc.vector.tensor_scalar(oh_dst[:, slot, :], iota[:, 0:P], dst_col[:, col], None,
                                            ALU.is_equal).then_inc(oh_ready, 1)

                with dve.Fori(0, T) as b:
                    one_hot(b, 0, 0)
                    with dve.Fori(0, turns) as i:
                        for k in range(OH):
                            one_hot(b, i * OH + 1 + k, (1 + k) % OH)
                    one_hot(b, count - 1, (WIN - 1) % OH)
                    dve.wait_ge(oh_ready, count * b + count)
                    nc.vector.tensor_scalar(dst_col[:], dst_col[:], float(-P), None, ALU.add).then_inc(step, 1)
                    dve.wait_ge(step, b + (chain[0] + 1))
                    dve.wait_ge(ct_loop, b + 1)
                    nc.vector.tensor_reduce(deg[:, ds(b, 1)], ct[:], AX.X, ALU.add).then_inc(ct_deg, 1)
                dve.wait_ge(ct_deg, T)
                nc.vector.tensor_scalar(many[:], deg[:], EXACT, None, ALU.is_gt).then_inc(step, 1)
                dve.wait_ge(step, chain[0] + T + 1)
                nc.vector.tensor_reduce(many_any[:], many[:], AX.X, ALU.add).then_inc(many_ready, 1)
                dve.wait_ge(many_summed, 1)
                nc.vector.tensor_scalar(par_f[:, 0:1], ps[0:1, 3, 0:1], 1.0, None, ALU.min).then_inc(step, 1)
                dve.wait_ge(step, chain[0] + T + 2)
                nc.vector.tensor_copy(params[:, 0:1], par_f[:, 0:1]).then_inc(low_ready, 1)
                dve.wait_ge(root, 1)
                nc.vector.reciprocal(dinv[:], dinv[:]).then_inc(dinv_ready, 1)
                assert chain[0] + T + 2 == GRAPH_STEPS, chain[0]

            def chain_from(semaphore, start):
                at_ = [start]

                def link(ins):
                    at_[0] = at_[0] + 1
                    ins.then_inc(semaphore, 1)
                    dve.wait_ge(semaphore, at_[0])
                return link

            def piece(n, name, hd, k):
                width = weights_of(name, hd)[1]
                if vectors_of(name, hd) is None:
                    return
                if k == 0:
                    dve.wait_ge(score_mm, n["sc"])
                    dve.wait_ge(a_in, 32 * n["av"] + 32)
                    dve.wait_ge(ev_scaled, n["f1"])
                dve.wait_ge(w_in[k % 2], 16 * (n["wp"] + k // 2 + 1))
                for j in range(2):
                    hold(dve, w_dot, 2 * (n["dot"] + k) + j + 4)
                    nc.vector.tensor_tensor_reduce(
                        out=r_row[:].bitcast(BF16)[:, 0:width], in0=ws[:, k % 2, 0:width], in1=a_row[:, j, 0:width],
                        scale=1.0, scalar=0.0, op0=ALU.mult, op1=ALU.add, accum_out=wa[:, k, j:j + 1]).then_inc(w_dot, 1)

            def weights(n, name, hd):
                for k in range(weights_of(name, hd)[0]):
                    piece(n, name, hd, k)

            def source_columns(link):
                link(nc.vector.tensor_scalar(s08[:], score[:, :, 0], 1.0 - SLOPE, None, ALU.mult))
                link(nc.vector.tensor_scalar(s02[:], score[:, :, 0], SLOPE, None, ALU.mult))

            def scores(n, kb, what):
                dve.wait_ge(score_mm, n["sc"] + 1)
                got = ps[:P, 4, 0:2 * T].rearrange("p (t j) -> p t j", j=2)
                if what == "add":
                    nc.vector.tensor_tensor(score_sum[:], score_sum[:], got, ALU.add).then_inc(score_ready, 1)
                else:
                    nc.vector.tensor_copy(score[:], got).then_inc(score_ready, 1)
                    dve.wait_ge(score_ready, n["sc"] + 1)
                    source_columns(chain_from(step, n["step"]))

            def masked_max(n, i, r):
                dve.wait_ge(maxed, 2 * (n["mp"] + i) + r + 2)
                dve.wait_ge(amax_ready, n["mp"] + i)
                hold(dve, mask_ld[r], 16 * (n["mp"] + i + 1))
                nc.vector.tensor_tensor_reduce(out=junk[:], in0=x_row[:P, :], in1=mask_in[r][:], scale=1.0, scalar=NONE,
                                               op0=ALU.add, op1=ALU.max, accum_out=pair_max[:, r:r + 1]).then_inc(maxed, 1)
                if r == 1:
                    dve.wait_ge(maxed, 2 * (n["mp"] + i) + 4)
                    nc.vector.tensor_copy(amax[:, ds(2 * i, 2)], pair_max[:]).then_inc(amax_ready, 1)

            def product(n, kb, width, maxima, scale, kind):
                dve.wait_ge(xt_ready, n["y"] + 2)
                dve.wait_ge(ev_done, n["f1"] + 2)
                if scale is not None:
                    dve.wait_ge(dinv_ready, 1)
                if maxima:
                    dve.wait_ge(p_low, n["tile"] + RING)
                    dve.wait_ge(acc_done, n["acc"] + RING)
                    dve.wait_ge(row_ready, n["rows"])

                def prepare(t, r):
                    q = n["q"] + t
                    dve.wait_ge(split_high, q + 1)
                    src_ = sources(kb)
                    for tile, k0 in src_:
                        kn = kb // len(src_)
                        last = nc.vector.tensor_tensor(ys_lo[:, r, k0:k0 + kn, :], tile[:, 0:kn, ds(t * P, P)],
                                                       ys_hi[:, r, k0:k0 + kn, :].bitcast(F32), ALU.subtract)
                    last.then_inc(split_low, 1)

                def finish(t, r, i):
                    q = n["q"] + t
                    dve.wait_ge(gemm_done, q + 3)
                    if kind == "sum":
                        dve.wait_ge(sum_added[r], 16 * (n["sp"] + i))
                        nc.vector.tensor_copy(ev[:P, r, HALF:D], ps[:P, 2 * r + 1, 0:HALF]).then_inc(gemm_dve, 1)
                    else:
                        dve.wait_ge(gemm_act, q + 3)
                        nc.vector.scalar_tensor_tensor(
                            out=h_block(h_lo, width, t), in0=ps_block(r, width),
                            scalar=1.0 if scale is None else scale[:, ds(t, 1)],
                            in1=h_block(h_hi, width, t).bitcast(F32), op0=ALU.mult, op1=ALU.subtract).then_inc(gemm_dve, 1)
                    if maxima:
                        masked_max(n, i, r)

                blocks_ahead(prepare, finish)(dve)

            def columns(n):
                link = chain_from(step, n["step"])
                dve.wait_ge(amax_ready, n["mp"])
                link(nc.vector.tensor_tensor(mcol[:], amax[:], score[:, :, 1], ALU.add))
                link(nc.vector.scalar_tensor_tensor(out=mcol[:], in0=mcol[:], scalar=SLOPE, in1=mcol[:],
                                                    op0=ALU.mult, op1=ALU.max))
                link(nc.vector.tensor_tensor(xcol[:], score[:, :, 1], mcol[:], ALU.subtract))
                nc.vector.scalar_tensor_tensor(out=ycol[:], in0=score[:, :, 1], scalar=SLOPE, in1=mcol[:],
                                               op0=ALU.mult, op1=ALU.subtract).then_inc(xy_ready, 1)

            def fold(n):
                dve.wait_ge(gemm_done, n["q"] + 2)
                link = chain_from(step, n["step"])
                nc.vector.memset(h_view(h_hi, D)[:, :, D:HW].bitcast(F32), 1.0).then_inc(ones_set, 1)
                nc.vector.memset(h_view(h_lo, D)[:, :, D:HW].bitcast(F32), 0.0).then_inc(ones_set, 1)
                dve.wait_ge(score_ready, n["sc"])
                link(nc.vector.tensor_copy(score[:], score_sum[:]))
                source_columns(link)
                dve.wait_ge(p_low, n["tile"] + RING)
                dve.wait_ge(acc_done, n["acc"] + RING)
                dve.wait_ge(row_ready, n["rows"] + 1)
                with dve.Fori(0, T // 2) as i:
                    for r in range(2):
                        dve.wait_ge(fold_act, 2 * i + r + 1)
                        nc.vector.tensor_tensor(h_block(h_lo, D, 2 * i + r), halves(ev[:P, r, :]),
                                                h_block(h_hi, D, 2 * i + r).bitcast(F32), ALU.subtract).then_inc(fold_dve, 1)
                        masked_max(n, i, r)

            def tiles(n, c, kind, width, off, sums, hook):
                t0, g, a = n["tile"] + c * T, n["gat"] + c * T, n["acc"] + c * T

                def larger(s):
                    dve.wait_ge(p_low, t0 + s + 1)
                    if sums:
                        dve.wait_ge(acc_done, a + s + 1)
                    nc.vector.scalar_tensor_tensor(out=tb[:, s % RING, 0:width], in0=x_row[:P, ds(off, width)],
                                                   scalar=s08[:, s:s + 1], in1=y_row[:, ds(off, width)],
                                                   op0=ALU.add, op1=ALU.max).then_inc(t_ready, 1)

                def count(s):
                    dve.wait_ge(e_ready, g + s + 1)
                    dve.wait_ge(c_ld[s % RING], 16 * (2 * (n["chunks"] + c) + s // RING + 1))
                    nc.vector.scalar_tensor_tensor(out=tb[:, s % RING, 0:width], in0=tb[:, s % RING, 0:width],
                                                   scalar=1.0, in1=c_in[:, s % RING, 0:width],
                                                   op0=ALU.min, op1=ALU.mult).then_inc(p_ready, 1)

                def low(s):
                    dve.wait_ge(p_high, t0 + s + 1)
                    tile = tb if kind == "gat" else c_in
                    nc.vector.tensor_tensor(p_lo[:, s % RING, 0:width], tile[:, s % RING, 0:width],
                                            p_hi[:, s % RING, 0:width].bitcast(F32), ALU.subtract).then_inc(p_low, 1)

                if kind == "gcn":
                    for s in range(T):
                        low(s)
                        hook(s)
                    return
                for s in range(T + 2):
                    if s < T:
                        larger(s)
                    if 1 <= s <= T:
                        count(s - 1)
                    if s >= 2:
                        low(s - 2)
                    hook(s)

            def hook_weights(n, following, s):
                if following is not None and 0 <= s - 2 < weights_of(*following)[0]:
                    piece(n, *following, s - 2)

            def across(n, kind, fb, what, bias, following, eps):
                dve.wait_ge(maxed, 2 * n["mp"] + 2)
                dve.wait_ge(row_ready, n["rows"])
                for r in range(2):
                    dve.wait_ge(stored[r], 16 * n["c2"])
                    dve.wait_ge(sum_added[r], 16 * n["sp"])

                dots = n["dot"] + (weights_of(*following)[0] if vectors_of(*following) else 0)

                def finish(c):
                    scale = r_row[:]
                    dve.wait_ge(w_dot, 2 * dots + 4)
                    dve.wait_ge(ev_scaled, n["f1"] + c * fb)
                    if kind == "gcn":
                        scale = x_row[:, ds(c * TS, TW)]
                    else:
                        dve.wait_ge(den_mm, n["den"] + c + 1)
                        total = ps[:, 7, 0:TW]
                        if eps:
                            link = chain_from(step, n["step"] + c)
                            link(nc.vector.tensor_scalar(r_row[:], total, eps, None, ALU.add))
                            total = r_row[:]
                        nc.vector.reciprocal(r_row[:], total).then_inc(r_ready, 1)
                        dve.wait_ge(r_ready, n["den"] + c + 1)

                    def unelu(f):
                        e = n["elu"] + c * fb + f
                        dve.wait_ge(ev_act, 2 * e + 2)
                        dve.wait_ge(ev_exp, e + 1)
                        nc.vector.tensor_tensor(ot[f // 2][:, f % 2, ds(c * TS, TW)], ev[:, f % 2, 0:TW],
                                                ev[:, 2 + f % 2, 0:TW], ALU.add).then_inc(ev_done, 1)

                    for f in range(fb):
                        v = n["f1"] + c * fb + f
                        dve.wait_ge(agg_mm, v + 1)
                        dve.wait_ge(ev_done, v + 1)
                        nc.vector.tensor_tensor(ev[:, f % 2, 0:TW], ps[:, f, 0:TW], scale, ALU.mult).then_inc(ev_scaled, 1)
                        if what == "elu" and f:
                            unelu(f - 1)
                    if what == "elu":
                        unelu(fb - 1)

                tiles(n, 0, kind, TW, 0, kind == "gat", lambda s: hook_weights(n, following, s))
                with dve.Fori(1, NC1) as c:
                    tiles(n, c, kind, TW, c * TS, kind == "gat", lambda s: finish(c - 1) if s == MID else None)
                finish(NC1 - 1)

            def along(n, kind, layer, following, eps):
                dve.wait_ge(maxed, 2 * n["mp"] + 2)
                dve.wait_ge(row_ready, n["rows"])

                def finish(c, bank):
                    link = chain_from(ln_step, n["ln"] + c * ln_links(kind, eps))
                    dve.wait_ge(y_ready, 2 * (n["c2"] + c))
                    for r in range(2):
                        b = 2 * (n["c2"] + c) + r
                        dve.wait_ge(agg2_mm, n["c2"] + c + 1)
                        if kind == "gat":
                            total = ps[:P, bank + 2 * r + 1, HALF:HALF + 1]
                            if eps:
                                link(nc.vector.tensor_scalar(rden[:, r, 0:1], total, eps, None, ALU.add))
                                total = rden[:, r, 0:1]
                            link(nc.vector.reciprocal(rden[:, r, 1:2], total))
                            by = rden[:, r, 1:2]
                        else:
                            by = dinv[:, ds(2 * c + r, 1)]
                        dve.wait_ge(res_ready, b + 1)
                        dve.wait_ge(stored[r], 16 * (n["c2"] + c))
                        dve.wait_ge(y_turned, n["y"] + (2 if layer == 3 else 2 * c + r + 1))
                        y = ev[:P, r, :]
                        nc.vector.scalar_tensor_tensor(out=halves(y), in0=ps[:P, bank + 2 * r:bank + 2 * r + 2, 0:HALF], scalar=by,
                                                       in1=halves(ev[:P, 2 + r, :]), op0=ALU.mult, op1=ALU.add
                                                       ).then_inc(agg2_read, 1)
                    for r in range(2):
                        dve.wait_ge(agg2_read, 2 * (n["c2"] + c) + r + 1)
                        for j in range(2):
                            link(nc.vector.bn_stats(stats[:, r, j, :], ev[:P, r, j * HALF:(j + 1) * HALF]))
                        dve.sem_inc(held, 1)
                        nc.vector.bn_aggr(mv[:, r, :], stats[:, r, :, :].rearrange("p a b -> p (a b)")).then_inc(var_ready, 1)
                    dve.wait_ge(var_ready, 2 * (n["c2"] + c) + 2)
                    dve.wait_ge(std_ready, n["c2"] + c + 1)
                    link(nc.vector.reciprocal(rstd[:], rstd[:]))
                    for r in range(2):
                        y = ev[:P, r, :]
                        nc.vector.tensor_scalar(y, y, mv[:, r, 0:1], rstd[:, r:r + 1], ALU.subtract, ALU.mult
                                                ).then_inc(y_ready, 1)

                tiles(n, 0, kind, BW, 0, False, lambda s: hook_weights(n, following, s))
                with dve.Fori(0, NC2 // 2) as i:
                    for k, bank in ((0, 0), (1, 4)):
                        c = 2 * i + k
                        tiles(n, c + 1, kind, BW, (c + 1) * BW, False, lambda s: finish(c, bank) if s == MID else None)
                finish(NC2 - 1, 0)

            def none(*_):
                pass

            program(dve, Stages(graph, none, weights, scores, product, columns, across, along, fold, none))

        @block.tensor
        def _(pe):
            pe.sem_inc(oh_used, OH)
            pe.sem_inc(y_turned, 2)
            pe.sem_inc(xt_ready, 2)
            pe.sem_inc(gemm_done, 2)
            pe.sem_inc(tile_used, RING)

            def graph():
                pe.wait_ge(graph_const, 1)
                pe.wait_ge(edges_flt, 1)
                for i in range(2):
                    for h in range(2):
                        o = i * EC + h * (EC // 2)
                        last = pe.transpose(ps[:P, 4, o:o + EC // 2], e_flt[:, i, h * P:(h + 1) * P],
                                            ident[0:EC // 2, 0:EC // 2])
                last.then_inc(edges_turned, 1)
                pe.wait_ge(bad_ready, 1)
                pe.matmul(ps[0:1, 4, 0:1], bad[:], ones[:, 0:1], start=True, stop=True).then_inc(bad_summed, 1)
                pe.wait_ge(par_ready, 1)
                turns = pe.value_load(params[0:1, 1:2], min_val=(WIN - 2) // OH, max_val=(ECP - 2) // OH)
                count = pe.value_load(params[0:1, 3:4], min_val=WIN, max_val=ECP)

                def add(b, j, slot, start, stop):
                    pe.wait_ge(oh_ready, count * b + j + 1)
                    for k in range(3):
                        o, w = (TW + TS * (k - 1), TS) if k else (0, TW)
                        last = pe.matmul(ps[:P, k, 0:w], oh_dst[:, slot, :], oh_src[:, slot, o:o + w],
                                         start=start, stop=stop)
                    last.then_inc(oh_used, 1)
                    return last

                with pe.Fori(0, T) as b:
                    pe.wait_ge(ct_out, b)
                    add(b, 0, 0, True, False)
                    with pe.Fori(0, turns) as i:
                        for k in range(OH):
                            add(b, i * OH + 1 + k, (1 + k) % OH, False, False)
                    add(b, count - 1, (WIN - 1) % OH, False, True)
                    pe.wait_ge(oh_used, count * b + count + OH)
                    pe.sem_inc(ct_summed, 1)
                    pe.wait_ge(ct_loop, b + 1)
                    pe.wait_ge(c_ready, b)
                    for j in range(T):
                        last = pe.transpose(ps[:P, 4 + j // 4, (j % 4) * P:(j % 4 + 1) * P], ct[:, j * P:(j + 1) * P],
                                            ident[:P, :P])
                    last.then_inc(ct_turned, 1)
                pe.wait_ge(many_ready, 1)
                pe.matmul(ps[0:1, 3, 0:1], many_any[:], ones[:, 0:1], start=True, stop=True).then_inc(many_summed, 1)

            def low_passes():
                pe.wait_ge(low_ready, 1)
                return pe.value_load(params[0:1, 0:1], min_val=0, max_val=1)

            def turn(y, r, bank):
                for k in range(KD):
                    last = pe.transpose(ps[:, bank + 2 * r + k // 3, (k % 3) * P:(k % 3 + 1) * P],
                                        ev[:P, r, k * 128:(k + 1) * 128], ident[:P, :P])
                last.then_inc(y_turned, 1)

            def turn_input():
                pe.wait_ge(c_ready, T)
                with pe.Fori(0, T // 2) as i:
                    for r in range(2):
                        pe.wait_ge(x_in[r], 16 * (i + 1))
                        pe.wait_ge(xt_ready, 2 * i + r + 1)
                        turn(2 * i + r, r, 4)

            def banks_free(n):
                pe.wait_ge(xt_ready, n["y"] + 2)
                pe.wait_ge(row_ready, n["rows"])
                pe.wait_ge(score_ready, n["sc"])
                pe.wait_ge(gemm_act, n["q"] + 2)
                pe.wait_ge(gemm_dve, n["q"] + 2)
                pe.wait_ge(ev_scaled, n["f1"])
                pe.wait_ge(r_ready, n["den"])
                pe.wait_ge(agg2_read, 2 * n["c2"])

            def row(n, k, col, parts):
                pe.wait_ge(row_ready, n["rows"] + k)
                for t in range(T):
                    last = pe.matmul(ps[:parts, 5 + t // 4, (t % 4) * P:(t % 4 + 1) * P],
                                     col(t).broadcast_to([P, parts]), ident[:P, :P], start=True, stop=True)
                last.then_inc(row_mm, 1)

            def scores(n, kb, what):
                banks_free(n)
                pe.wait_ge(ev_done, n["f1"] + 2)
                pe.wait_ge(w_dot, 2 * n["dot"] + 4)
                for t in range(T):
                    for k in range(kb):
                        last = pe.matmul(ps[:P, 4, 2 * t:2 * t + 2], source_block(kb, k, slice(t * P, (t + 1) * P)),
                                         wa[:, k, :], start=(k == 0), stop=(k == kb - 1))
                last.then_inc(score_mm, 1)
                if what == "use":
                    pe.wait_ge(score_ready, n["sc"] + 1)
                    row(n, 0, lambda t: score[:, t, 0:1], P)

            def product(n, kb, width, maxima, scale, kind):
                pe.wait_ge(agg2_read, 2 * n["c2"])
                pe.wait_ge(xt_ready, n["y"] + 2)
                pe.wait_ge(ev_scaled, n["f1"])
                hold(pe, w_low, 2 * n["wp"] + 2)
                banks = 1 if width == HID else 2
                bw = width // banks

                def one(q, r):
                    pe.wait_ge(split_high, q + 1)
                    pe.wait_ge(split_low, q + 1)
                    pe.wait_ge(gemm_act, q + 1)
                    pe.wait_ge(gemm_dve, q + 1)
                    for j in range(banks):
                        for k in range(kb):
                            for m, (a, b) in enumerate(PASSES):
                                o = k * width + j * bw
                                last = pe.matmul(ps[:P, 2 * r + j, 0:bw], (ys_hi, ys_lo)[a][:, r, k, :],
                                                 (w_hi, w_lo)[b][:, o:o + bw], start=(k == 0 and m == 0),
                                                 stop=(k == kb - 1 and m == 2))
                    last.then_inc(gemm_done, 1)

                with pe.Fori(0, T // 2) as i:
                    for r in range(2):
                        one(n["q"] + 2 * i + r, r)

            def columns(n):
                pe.wait_ge(xy_ready, n["xy"] + 1)
                row(n, 0, lambda t: xcol[:, t:t + 1], P)
                row(n, 1, lambda t: ycol[:, t:t + 1], P)

            def degree_row(n):
                pe.wait_ge(dinv_ready, 1)
                row(n, 0, lambda t: dinv[:, t:t + 1], 128)

            def fold(n):
                pe.wait_ge(score_ready, n["sc"])
                banks_free(n)
                row(n, 0, lambda t: score_sum[:, t, 0:1], P)
                pe.wait_ge(fold_act, T)
                pe.wait_ge(fold_dve, T + 2)
                pe.wait_ge(ones_set, 2)

            def across(n, kind, fb, what, bias, following, eps):
                banks_free(n)
                width = HID if fb == KH else D

                low = low_passes() if kind == "gcn" else None

                def chunk(c, first):
                    t0 = n["tile"] + c * T
                    for s in range(T):
                        pe.wait_ge(p_high, t0 + s + 1)
                        pe.wait_ge(p_low, t0 + s + 1 + RING)

                        def products(f, passes, start, stop):
                            for m, (a, b) in enumerate(passes):
                                last = pe.matmul(ps[:, f, 0:TW],
                                                 h_view((h_hi, h_lo)[a], width)[:, s, f * 128:(f + 1) * 128],
                                                 (p_hi, p_lo)[b][:, s % RING, :], start=(start and m == 0),
                                                 stop=(stop and m == len(passes) - 1))
                            return last

                        def free(f):
                            if s == 0 and not first:
                                pe.wait_ge(ev_scaled, n["f1"] + (c - 1) * fb + f + 1)

                        if kind == "gcn":
                            for f in range(fb):
                                free(f)
                                products(f, PASSES[0:1], s == 0, False)
                            with pe.If(low > 0):
                                for f in range(fb):
                                    products(f, PASSES[1:2], False, False)
                        for f in range(fb):
                            if kind == "gat":
                                free(f)
                                last = products(f, PASSES, s == 0, s == T - 1)
                            else:
                                last = products(f, PASSES[2:3], False, s == T - 1)
                            if s == T - 1:
                                last.then_inc(agg_mm, 1)
                            if s == T - 1 and kind == "gat" and f == fb // 2 - 1:
                                pe.wait_ge(acc_done, n["acc"] + c * T + T + RING)
                                pe.wait_ge(r_ready, n["den"] + c)
                                pe.matmul(ps[:, 7, 0:TW], ones[:].broadcast_to([P, 128]), acc[:],
                                          start=True, stop=True).then_inc(den_mm, 1)
                        if s == T - 1:
                            pe.wait_ge(agg_mm, n["f1"] + c * fb + fb)
                            pe.sem_inc(tile_used, 1)
                        else:
                            last.then_inc(tile_used, 1)

                chunk(0, True)
                with pe.Fori(1, NC1) as c:
                    chunk(c, False)

            def along(n, kind, layer, following, eps):
                banks_free(n)

                low = low_passes() if kind == "gcn" else None

                def chunk(c, bank, hook):
                    t0 = n["tile"] + c * T
                    for s in range(T):
                        pe.wait_ge(p_high, t0 + s + 1)
                        pe.wait_ge(p_low, t0 + s + 1 + RING)

                        def products(passes, start, stop):
                            for r in range(2):
                                for m, (a, b) in enumerate(passes):
                                    for j, w in enumerate((HALF, HALF + 2)):
                                        last = pe.matmul(ps[:P, bank + 2 * r + j, 0:w],
                                                         (p_hi, p_lo)[a][:, s % RING, r * P:(r + 1) * P],
                                                         h_view((h_hi, h_lo)[b], D)[:, s, j * HALF:j * HALF + w],
                                                         start=(start and m == 0), stop=(stop and m == len(passes) - 1))
                            return last

                        if kind == "gat":
                            last = products(PASSES, s == 0, s == T - 1)
                        else:
                            products(PASSES[0:1], s == 0, False)
                            with pe.If(low > 0):
                                products(PASSES[2:3], False, False)
                            last = products(PASSES[1:2], False, s == T - 1)
                        last.then_inc(tile_used, 1)
                        hook(s)
                    pe.wait_ge(tile_used, t0 + T + RING)
                    pe.sem_inc(agg2_mm, 1)

                def turned(c, bank):
                    for r in range(2):
                        pe.wait_ge(y_ready, 2 * (n["c2"] + c) + r + 1)
                        turn(n["y"] + 2 * c + r, r, bank)

                def banks_used(c):
                    pe.wait_ge(agg2_read, 2 * (n["c2"] + c - 1))
                    if layer < 3:
                        pe.wait_ge(xt_ready, n["y"] + 2 * (c - 1) + 2)

                chunk(0, 0, lambda s: None)
                with pe.Fori(0, NC2 // 2) as i:
                    for k, bank in ((1, 4), (2, 0)):
                        banks_used(2 * i + k)
                        chunk(2 * i + k, bank, lambda s: turned(2 * i + k - 1, 4 - bank) if s == TURN_AT and layer < 3 else None)
                if layer < 3:
                    turned(NC2 - 1, 0)

            def none(*_):
                pass

            program(pe, Stages(graph, turn_input, none, scores, product, columns, across, along, fold, degree_row))


_INS = ['x', 'src', 'dst', 'L0_gnn_W1', 'L0_gnn_a1_src', 'L0_gnn_a1_dst', 'L0_gnn_b1', 'L0_gnn_W2', 'L0_gnn_a2_src',
        'L0_gnn_a2_dst', 'L0_gnn_b2', 'L1_gnn_W', 'L1_gnn_b', 'L2_gnn_W1', 'L2_gnn_att_src1', 'L2_gnn_att_dst1',
        'L2_gnn_b1', 'L2_gnn_W2', 'L2_gnn_att_src2', 'L2_gnn_att_dst2', 'L2_gnn_b2', 'L3_gnn_W1', 'L3_gnn_b1',
        'L3_gnn_W2', 'L3_gnn_b2']
_OUTS = [((N, D), 'float32')]


def kernel(**inputs):
    import numpy as _np
    import concourse.bacc as _bacc
    from concourse import mybir as _mybir
    from concourse.bass_utils import run_bass_kernel_spmd as _run

    nc = _bacc.Bacc("TRN2", target_bir_lowering=False, num_devices=1)
    arrays, args = {}, []
    for name in _INS:
        a = _np.ascontiguousarray(inputs[name])
        arrays[f"in_{name}_dram"] = a
        args.append(nc.dram_tensor(f"in_{name}_dram", a.shape, _mybir.dt.from_np(a.dtype), kind="ExternalInput").ap())
    for i, (shape, dtype) in enumerate(_OUTS):
        dt = _mybir.dt.from_np(_np.dtype(dtype))
        args.append(nc.dram_tensor(f"out_{i}_dram", shape, dt, kind="ExternalOutput").ap())
    build(nc, *args)
    r = _run(nc, [arrays], core_ids=[0])
    return r.results[0]["out_0_dram"]
```

```python
from collections import namedtuple
from contextlib import ExitStack

import concourse.bass as bass
from concourse import mybir

F32, F32R, BF16, F16 = mybir.dt.float32, mybir.dt.float32r, mybir.dt.bfloat16, mybir.dt.float16
I32, I16 = mybir.dt.int32, mybir.dt.int16
ALU = mybir.AluOpType
ACT = mybir.ActivationFunctionType
AX = mybir.AxisListType
ds = bass.ds

N, D, E = 1250, 768, 20000
HEADS, HID = 4, 512
P = 125
T = N // P
KD = D // 128
KH = HID // 128
HALF = D // 2
HW = D + 2
TW, TS = 418, 416
NC1 = 3
BW = 2 * P
NC2 = T // 2
RING = 5
SLOPE = 0.2
EPS = 1e-5
EXACT = 4096.0
NONE = -1e30

EC = E // P
PER = EC // T
SLACK = 3
WIN = PER + 2 * SLACK
ECP = EC + 2 * SLACK
OH = 4
W1_PIECES = 3
TURN_AT = 8


def late(kind):
    return 2 if kind == "gat" else 0


def chunk_ends(kind):
    return RING - 2 + late(kind)


GRAPH_STEPS = 3 + 2 + 2 + 2 + 4 + T + 2

Stages = namedtuple("Stages", "graph turn_input head_scores maxima product_sum scores product columns across along fold "
                    "degree_row")

assert NC2 % 2 == 1 and T % 2 == 0 and T % RING == 0 and (WIN - 2) % OH == 0 and (ECP - 2) % OH == 0
assert TS * (NC1 - 1) + TW == N and EC * P == E and EC % 2 == 0 and PER * T == EC


def build(nc, x, src, dst, L0_W1, L0_a1s, L0_a1d, L0_b1, L0_W2, L0_a2s, L0_a2d, L0_b2, L1_W, L1_b,
          L2_W1, L2_a1s, L2_a1d, L2_b1, L2_W2, L2_a2s, L2_a2d, L2_b2, L3_W1, L3_b1, L3_W2, L3_b2, out):
    counts_dram = nc.dram_tensor("counts_dram", (T, P, N), I16, kind="Internal").ap()
    masks_dram = nc.dram_tensor("masks_dram", (T, P, N), BF16, kind="Internal").ap()
    heads_dram = nc.dram_tensor("heads_dram", (T, P, D), F32, kind="Internal").ap()
    y_dram = [nc.dram_tensor(f"y{n}_dram", (T, P, D), F32, kind="Internal").ap() for n in range(3)]
    x_blocks = x.rearrange("(t p) f -> t p f", p=P)
    out_blocks = out.rearrange("(t p) f -> t p f", p=P)

    with ExitStack() as ctx:
        place = [0]

        def at(name, shape, dt, offset=None):
            size = mybir.dt.size(dt)
            for n in shape[1:]:
                size *= n
            if offset is None:
                offset = place[0]
                place[0] += (size + 31) // 32 * 32
            return nc.alloc_sbuf_tensor_at(name, shape, dt, offset=offset)

        base0 = nc.sbuf_base
        place[0] = (base0 + 31) // 32 * 32

        def sem(name):
            return ctx.enter_context(nc.semaphore(name))

        XT = at("XT", [128, KD, N], F32)
        ys_hi = at("ys_hi", [128, 2, KD, P], F32R)
        ys_lo = at("ys_lo", [128, 2, KD, P], F32R)
        h_at = place[0]
        h_hi = at("h_hi", [P, T * HW], F32R)
        h_lo_at = place[0]
        h_lo = at("h_lo", [P, T * HW], F32R)
        w_at = place[0]
        w_hi = at("w_hi", [128, KD * D], F32R)
        w_lo = at("w_lo", [128, KD * D], F32R)
        p_hi = at("p_hi", [P, RING, TW], F32R)
        p_lo = at("p_lo", [P, RING, TW], F32R)
        x_row = at("x_row", [128, N], F32)
        y_row = at("y_row", [P, N], F32)
        tb_at = place[0]
        tb = at("tb", [P, RING, TW], F32)
        c_in = at("c_in", [P, RING, TW], I16)
        acc = at("acc", [P, TW], F32)
        r_row = at("r_row", [128, TW], F32)
        ws = at("ws", [128, 2, D], F32)
        ev = at("ev", [128, 4, D], F32)
        bias_at = place[0]
        bias_row = at("bias_row", [P, D], F32)
        a_row = at("a_row", [128, 2, D], F32)
        ident = at("ident", [128, 128], F32)
        ones = at("ones", [P, 1], F32)
        wa = at("wa", [128, KD, 2], F32)
        score = at("score", [P, T, 2], F32)
        score_sum = at("score_sum", [P, T, 2], F32)
        s08 = at("s08", [P, T], F32)
        s02 = at("s02", [P, T], F32)
        pair_max = at("pair_max", [P, 2], F32)
        amax = at("amax", [P, T], F32)
        mcol = at("mcol", [P, T], F32)
        xcol = at("xcol", [P, T], F32)
        ycol = at("ycol", [P, T], F32)
        deg = at("deg", [P, T], F32)
        dinv = at("dinv", [P, T], F32)
        b_col = at("b_col", [128, HEADS * KH + 2 * KD], F32)
        rden = at("rden", [P, 2, 2], F32)
        stats = at("stats", [P, 2, 2, 6], F32)
        mv = at("mv", [P, 2, 2], F32)
        rstd = at("rstd", [P, 2], F32)
        eps_col = at("eps_col", [P, 1], F32)
        params = at("params", [1, 4], I32)
        assert place[0] <= nc.sbuf_usable_end, (place[0], nc.sbuf_usable_end)

        w2 = [at(f"w2_{part}", [128, KH, HW], F32R, offset=w_at + i * KH * HW * 4) for i, part in enumerate(("hi", "lo"))]
        w1 = [at(f"w1_{part}", [128, KD * HID], F32R, offset=w_at + 2 * KH * HW * 4 + i * KD * HID * 4)
              for i, part in enumerate(("hi", "lo"))]
        assert 2 * KH * HW + 2 * KD * HID <= 2 * KD * D + 2 * RING * TW
        w1_rows = at("w1_rows", [128, 2, HEADS * HID], F32, offset=w_at)
        a1_row = at("a1_row", [128, 2 * HEADS, HID], F32, offset=w_at + 2 * HEADS * HID * 4)
        wa8 = at("wa8", [128, KD, 2 * HEADS], F32, offset=h_at + 2 * T * HW * 4 - KD * 2 * HEADS * 4)
        score8 = at("score8", [P, T, 2 * HEADS], F32, offset=bias_at)
        w1_in = at("w1_in", [128, KD * HID], F32, offset=h_at)
        add = at("add", [P, 2, D], F32, offset=h_at + KD * HID * 4)
        assert KD * HID + 2 * D <= T * HID
        ev_flat = ev[:].rearrange("p a f -> p (a f)")

        def z_tile(f):
            return ev_flat[:, f * TW:(f + 1) * TW]

        def e_tile(f):
            return z_tile(KH + f) if f < KH - 1 else r_row[:]

        ot = [at(f"ot{i}", [128, KH // 2, N], F32, offset=o + T * HID * 4) for i, o in enumerate((h_at, h_lo_at))]
        junk = at("junk", [P, N], BF16, offset=tb_at)
        mask_in = [at(f"mask_in{i}", [P, N], BF16, offset=tb_at + 2528 * (i + 1)) for i in range(2)]
        g = [h_at]

        def graph(name, shape, dt):
            size = mybir.dt.size(dt)
            for n in shape[1:]:
                size *= n
            g[0] += (size + 31) // 32 * 32
            return at(name, shape, dt, offset=g[0] - (size + 31) // 32 * 32)

        iota_i = graph("iota_i", [P, N], I32)
        iota = graph("iota", [P, N], F16)
        oh_src = graph("oh_src", [P, OH, N], BF16)
        oh_dst = graph("oh_dst", [P, OH, P], BF16)
        ct = graph("ct", [P, N], F32)
        c_out = graph("c_out", [P, T, P], I16)
        m_out = graph("m_out", [P, N], BF16)
        e_int = graph("e_int", [EC // 2, 2, BW], I32)
        e_flt = graph("e_flt", [EC // 2, 2, BW], F32)
        src_col = graph("src_col", [P, ECP], F32)
        dst_col = graph("dst_col", [P, ECP], F32)
        lim_i = graph("lim_i", [P, 2, 12 * PER], I32)
        lim = graph("lim", [P, 2, 12 * PER], F32)
        out_of = graph("out_of", [P, 2, EC], F32)
        bad = graph("bad", [P, 1], F32)
        many = graph("many", [P, T], F32)
        many_any = graph("many_any", [P, 1], F32)
        par_f = graph("par_f", [1, 4], F32)
        zeros = graph("zeros", [P, D], F32)
        assert g[0] <= h_at + 2 * T * HW * 4 - KD * 2 * HEADS * 4

        ps = ctx.enter_context(nc.psum_tensor("ps", [128, 8, 512], F32))

        edges_in, graph_const, graph_step = sem("edges_in"), sem("graph_const"), sem("graph_step")
        edges_flt, edges_turned, edges_col = sem("edges_flt"), sem("edges_turned"), sem("edges_col")
        bad_ready, bad_summed, par_ready = sem("bad_ready"), sem("bad_summed"), sem("par_ready")
        oh_ready, oh_used, ct_summed, ct_out = sem("oh_ready"), sem("oh_used"), sem("ct_summed"), sem("ct_out")
        ct_loop, ct_deg, ct_turned, c_ready = sem("ct_loop"), sem("ct_deg"), sem("ct_turned"), sem("c_ready")
        m_ready, c_stored, m_stored = sem("m_ready"), sem("c_stored"), sem("m_stored")
        many_ready, many_summed, low_ready = sem("many_ready"), sem("many_summed"), sem("low_ready")
        root, dinv_ready, zeroed = sem("root"), sem("dinv_ready"), sem("zeroed")
        held = sem("held")
        x_in = [sem(f"x_in{i}") for i in range(2)]
        y_ready, y_turned, xt_ready = sem("y_ready"), sem("y_turned"), sem("xt_ready")
        w_in = [sem(f"w_in{i}") for i in range(2)]
        a_in, w_high, w_low, w_dot = sem("a_in"), sem("w_high"), sem("w_low"), sem("w_dot")
        split_high, split_low, gemm_done = sem("split_high"), sem("split_low"), sem("gemm_done")
        gemm_act, gemm_dve = sem("gemm_act"), sem("gemm_dve")
        fold_act, fold_dve = sem("fold_act"), sem("fold_dve")
        sum_in, sum_added = [sem(f"sum_in{i}") for i in range(2)], [sem(f"sum_added{i}") for i in range(2)]
        a1_in, rows_in, head_dot = sem("a1_in"), [sem(f"rows_in{i}") for i in range(2)], sem("head_dot")
        rows_more = [sem(f"rows_more{i}") for i in range(2)]
        w1_ld, w1_high, w1_low = sem("w1_ld"), sem("w1_high"), sem("w1_low")
        wa_high, wa_low, summed = sem("wa_high"), sem("wa_low"), sem("summed")
        ones_set = sem("ones_set")
        score_mm, score_ready, row_mm, row_ready = sem("score_mm"), sem("score_ready"), sem("row_mm"), sem("row_ready")
        mask_ld = [sem(f"mask_ld{i}") for i in range(2)]
        maxed, step, xy_ready, amax_ready = sem("maxed"), sem("step"), sem("xy_ready"), sem("amax_ready")
        c_ld = [sem(f"c_ld{i}") for i in range(RING)]
        t_ready, e_ready, p_ready = sem("t_ready"), sem("e_ready"), sem("p_ready")
        p_high, p_low, tile_used, acc_done = sem("p_high"), sem("p_low"), sem("tile_used"), sem("acc_done")
        den_mm, r_ready, agg_mm = sem("den_mm"), sem("r_ready"), sem("agg_mm")
        ev_scaled, ev_act, ev_exp, ev_done = sem("ev_scaled"), sem("ev_act"), sem("ev_exp"), sem("ev_done")
        b_in = sem("b_in")
        agg2_mm, agg2_read, res_in, res_ready = sem("agg2_mm"), sem("agg2_read"), [sem(f"res_in{i}") for i in range(2)], sem("res_ready")
        bias_in, var_ready, std_ready, ln_step = sem("bias_in"), sem("var_ready"), sem("std_ready"), sem("ln_step")
        stored = [sem(f"stored{i}") for i in range(2)]

        START = dict(wp=0, dot=0, av=0, q=0, sp=0, sc=1, rows=1, mp=T // 2, step=GRAPH_STEPS + 6, xy=1, tile=0, gat=0,
                     acc=0, c1=0, f1=0, den=0, elu=0, c2=0, y=T, ln=0, chunks=0)
        HEAD = dict(wp=KH // 2, dot=KH, av=1, q=2 * T, sp=T // 2, sc=0, rows=3, mp=T // 2,
                    step=6 + NC1, xy=1, tile=T * NC1, gat=T * NC1, acc=T * NC1, c1=NC1, f1=KH * NC1, den=NC1,
                    elu=KH * NC1, c2=0, y=0, ln=0, chunks=NC1)

        def in_head(hd):
            return {k: START[k] + HEAD[k] * hd for k in START}

        def after_heads():
            n = {k: START[k] + HEAD[k] * HEADS for k in START}
            return dict(n, rows=n["rows"] - 1, mp=n["mp"] - T // 2, step=n["step"] - 6, xy=n["xy"] - 1)

        def weights_of(name, hd=None):
            if name == "L0_W2":
                return KH, D, lambda k: L0_W2[ds(hd * HID + k * 128, 128), :]
            w = {"L1_W": L1_W, "L2_W1": L2_W1, "L2_W2": L2_W2, "L3_W1": L3_W1, "L3_W2": L3_W2}[name]
            return KD, D, lambda k: w[k * 128:(k + 1) * 128, :]

        def vectors_of(name, hd=None):
            if name == "L0_W2":
                return L0_a2s, L0_a2d
            if name == "L2_W1":
                return L2_a1s.rearrange("(a f) -> a f", a=1), L2_a1d.rearrange("(a f) -> a f", a=1)
            if name == "L2_W2":
                return L2_a2s.rearrange("(a f) -> a f", a=1), L2_a2d.rearrange("(a f) -> a f", a=1)
            return None

        def sources(kb):
            return [(XT, 0)] if kb == KD else [(ot[0], 0), (ot[1], KH // 2)]

        def source_block(kb, k, cols):
            return XT[:, k, cols] if kb == KD else ot[k // (KH // 2)][:, k % (KH // 2), cols]

        def h_view(h, width):
            return (h[:, 0:T * HID].rearrange("p (t f) -> p t f", f=HID) if width == HID
                    else h[:].rearrange("p (t f) -> p t f", f=HW))

        def h_block(h, width, t):
            v = h_view(h, width)[:, ds(t, 1), 0:width]
            return (v.rearrange("p t f -> p (t f)") if width == HID
                    else v.rearrange("p t (b f) -> p (t b) f", b=2))

        def ps_block(r, width):
            return ps[:P, 2 * r, 0:HID] if width == HID else ps[:P, 2 * r:2 * r + 2, 0:HALF]

        def halves(tile):
            return tile.rearrange("p (b f) -> p b f", b=2)

        def w_place(tiles_, name, k):
            def part(i):
                return w2[i][:, k, 0:D] if name == "L0_W2" else (w_hi, w_lo)[i][:, k * D:(k + 1) * D]
            return part(tiles_)

        def in_segments(eng, pair, last, hooks):
            at_ = 0
            for stop in [k for k in sorted(hooks) if k < last] + [last]:
                if stop - at_ == 1:
                    pair(at_)
                else:
                    with eng.Fori(at_, stop) as i:
                        pair(i)
                if stop in hooks:
                    hooks[stop]()
                at_ = stop

        def blocks_ahead(eng, prepare, finish, started=lambda: None, hooks={}):
            prepare(0, 0)
            prepare(1, 1)
            started()

            def pair(i):
                for r in range(2):
                    finish(2 * i + r, r, i)
                    prepare(2 * i + r + 2, r)

            in_segments(eng, pair, T // 2 - 1, hooks)
            finish(T - 2, 0, T // 2 - 1)
            finish(T - 1, 1, T // 2 - 1)

        def first_bank(fb, c):
            return 4 * (c % 2) if fb == KH else 0

        def sum_bank(fb, c):
            return first_bank(fb, c + 1) + KH - 1 if fb == KH else 7

        def other_chunks(eng, fb, chunk):
            if fb == KH:
                for c in range(1, NC1):
                    chunk(c)
            else:
                with eng.Fori(1, NC1) as c:
                    chunk(c)

        def program(eng, do):
            do.graph()
            do.turn_input()
            do.head_scores()
            do.maxima(dict(START, rows=1, mp=0, step=GRAPH_STEPS + 3, xy=0))

            def head(hd, more):
                n = in_head(hd)
                do.product(n, KD, HID, False, None, "h", hd)
                n = dict(n, q=n["q"] + T, rows=n["rows"] + 2)
                do.across(n, "gat", KH, "elu", hd * KH, ("L0_W2", hd), 1e-16)
                before = n
                n = dict(n, wp=n["wp"] + KH // 2, dot=n["dot"] + KH, av=n["av"] + 1, chunks=n["chunks"] + NC1, tile=n["tile"] + T * NC1,
                         gat=n["gat"] + T * NC1, acc=n["acc"] + T * NC1, c1=n["c1"] + NC1, den=n["den"] + NC1,
                         f1=n["f1"] + KH * NC1, elu=n["elu"] + KH * NC1, step=n["step"] + NC1)
                do.product_sum(before, n, hd, more)

            with eng.Fori(0, HEADS - 1) as hd:
                head(hd, True)
            head(HEADS - 1, False)
            n = after_heads()
            do.fold(n)
            n = dict(n, mp=n["mp"] + T // 2, step=n["step"] + 3, rows=n["rows"] + 1)
            do.columns(n)
            n = dict(n, xy=n["xy"] + 1, rows=n["rows"] + 2, step=n["step"] + 3)
            do.along(n, "gat", 0, ("L1_W", None), 1e-16)
            n = after_along(n, "gat", "L1_W", 1e-16)

            do.product(n, KD, D, False, dinv, "h")
            n = dict(n, q=n["q"] + T)
            do.along(n, "gcn", 1, ("L2_W1", None), 0.0)
            n = after_along(n, "gcn", "L2_W1", 0.0)

            do.scores(n, KD, "use")
            n = dict(n, sc=n["sc"] + 1, rows=n["rows"] + 1, step=n["step"] + 2)
            do.product(n, KD, D, True, None, "h")
            n = dict(n, q=n["q"] + T, mp=n["mp"] + T // 2)
            do.columns(n)
            n = dict(n, xy=n["xy"] + 1, rows=n["rows"] + 2, step=n["step"] + 3)
            do.across(n, "gat", KD, "relu", HEADS * KH, ("L2_W2", None), 0.0)
            n = dict(n, wp=n["wp"] + KD // 2, dot=n["dot"] + KD, av=n["av"] + 1, chunks=n["chunks"] + NC1, tile=n["tile"] + T * NC1,
                     gat=n["gat"] + T * NC1, acc=n["acc"] + T * NC1, c1=n["c1"] + NC1, den=n["den"] + NC1,
                     f1=n["f1"] + KD * NC1)
            do.scores(n, KD, "use")
            n = dict(n, sc=n["sc"] + 1, rows=n["rows"] + 1, step=n["step"] + 2)
            do.product(n, KD, D, True, None, "h")
            n = dict(n, q=n["q"] + T, mp=n["mp"] + T // 2)
            do.columns(n)
            n = dict(n, xy=n["xy"] + 1, rows=n["rows"] + 2, step=n["step"] + 3)
            do.along(n, "gat", 2, ("L3_W1", None), 0.0)
            n = after_along(n, "gat", "L3_W1", 0.0)

            do.product(n, KD, D, False, dinv, "h")
            n = dict(n, q=n["q"] + T)
            do.degree_row(n)
            n = dict(n, rows=n["rows"] + 1)
            do.across(n, "gcn", KD, "relu", HEADS * KH + KD, ("L3_W2", None), 0.0)
            n = dict(n, wp=n["wp"] + KD // 2, chunks=n["chunks"] + NC1, tile=n["tile"] + T * NC1, c1=n["c1"] + NC1, f1=n["f1"] + KD * NC1)
            do.product(n, KD, D, False, dinv, "h")
            n = dict(n, q=n["q"] + T)
            do.along(n, "gcn", 3, None, 0.0)
        def ln_links(kind, eps):
            return (0 if kind == "gcn" else 4 if eps else 2) + 5

        def after_along(n, kind, following, eps):
            n = dict(n, chunks=n["chunks"] + NC2, tile=n["tile"] + T * NC2, c2=n["c2"] + NC2, y=n["y"] + T, wp=n["wp"] + KD // 2,
                     ln=n["ln"] + NC2 * ln_links(kind, eps))
            if kind == "gat":
                n["gat"] += T * NC2
            if vectors_of(following) is not None:
                n = dict(n, dot=n["dot"] + KD, av=n["av"] + 1)
            return n

        C_T = counts_dram.rearrange("t p n -> p t n")
        PASSES = ((0, 0), (0, 1), (1, 0))

        def hold(eng, semaphore, value):
            eng.wait_ge(semaphore, value)
            eng.sem_inc(held, 1)

        block = ctx.enter_context(nc.Block())

        @block.sync
        def _(sp):
            def graph():
                for i, e in enumerate((src, dst)):
                    sp.dma_start(e_int[:, i, :], e.rearrange("(q c) -> q c", c=BW)).then_inc(edges_in, 16)
                for i, (b, o, k) in enumerate(((L0_b1, 0, HEADS * KH), (L2_b1, HEADS * KH, KD),
                                               (L3_b1, HEADS * KH + KD, KD))):
                    sp.dma_start(b_col[:, o:o + k], b.rearrange("(k p) -> p k", p=128),
                                 allow_slow_non_contiguous=True).then_inc(b_in, 16)
                for j, a in enumerate((L0_a1s, L0_a1d)):
                    sp.dma_start(a1_row[:, j * HEADS:(j + 1) * HEADS, :].rearrange("p h f -> p (h f)"),
                                 a.rearrange("(a h) f -> a (h f)", a=1).broadcast_to([128, HEADS * HID])).then_inc(a1_in, 16)
                for k in range(2):
                    sp.dma_start(w1_rows[:, k, :], L0_W1[k * 128:(k + 1) * 128, :]).then_inc(rows_in[k], 16)
                sp.wait_ge(graph_const, 2)
                for t in range(T):
                    sp.dma_start(heads_dram[t], zeros[:]).then_inc(zeroed, 16)
                with sp.Fori(0, T) as b:
                    hold(sp, m_ready, b + 1)
                    sp.dma_start(masks_dram[ds(b, 1)].rearrange("b p n -> (b p) n"), m_out[:]).then_inc(m_stored, 16)
                    hold(sp, c_ready, b + 1)
                    sp.dma_start(C_T[:, :, ds(b * P, P)], c_out[:]).then_inc(c_stored, 16)

            def turn_input():
                with sp.Fori(0, T // 2) as i:
                    for r in range(2):
                        hold(sp, y_turned, 2 * i + r + 1)
                        sp.dma_start(ev[:P, r, :], x_blocks[ds(2 * i + r, 1)].rearrange("t p f -> (t p) f")
                                     ).then_inc(x_in[r], 16)
                sp.wait_ge(c_stored, 16 * T)
                sp.wait_ge(m_stored, 16 * T)
                sp.wait_ge(zeroed, 16 * T)

            def load_w1(n, hd):
                sp.dma_start(w1_in[:].rearrange("p (k f) -> p k f", f=HID),
                             L0_W1[:, ds(hd * HID, HID)].rearrange("(k p) f -> p k f", p=128)).then_inc(w1_ld, 16)

            def head_scores():
                sp.wait_ge(dinv_ready, 1)
                load_w1(START, 0)

            def maxima(n):
                with sp.Fori(0, T // 2) as i:
                    for r in range(2):
                        mask(n, i, r)

            def product_sum(before, n, hd, more):
                if more:
                    hold(sp, tile_used, n["tile"] + RING)
                    load_w1(n, hd + 1)
                    masks_free(n)
                    maxima(n)

            def vectors(n, name, hd):
                hold(sp, w_dot, 2 * n["dot"] + 4)
                for j, a in enumerate(vectors_of(name, hd)):
                    width = a.shape[1]
                    sp.dma_start(a_row[:, j, 0:width], a.broadcast_to([128, width])).then_inc(a_in, 16)

            def piece(n, name, hd, k):
                kb, width, rows = weights_of(name, hd)
                if k == 0 and vectors_of(name, hd) is not None:
                    vectors(n, name, hd)
                hold(sp, w_low, 2 * n["wp"] + k + 1)
                hold(sp, w_dot, 2 * n["dot"] + (4 if vectors_of(name, hd) is None else 2 * k + 2))
                sp.dma_start(ws[:, k % 2, 0:width], rows(k)).then_inc(w_in[k % 2], 16)

            def masks_free(n):
                hold(sp, p_low, n["tile"] + RING)
                hold(sp, acc_done, n["acc"] + RING)

            def mask(n, i, r):
                hold(sp, maxed, 2 * n["mp"] + 2 * i + r + 1)
                sp.dma_start(mask_in[r][:], masks_dram[ds(2 * i + r, 1)].rearrange("t p n -> (t p) n")
                             ).then_inc(mask_ld[r], 16)

            def product(n, kb, width, with_max, scale, kind, hd=None):
                if with_max:
                    masks_free(n)
                    with sp.Fori(0, T // 2) as i:
                        for r in range(2):
                            mask(n, i, r)

            def fold(n):
                masks_free(n)
                with sp.Fori(0, T // 2) as i:
                    for r in range(2):
                        if r == 0:
                            for q in range(2):
                                hold(sp, sum_added[q], 16 * n["sp"])
                        hold(sp, fold_dve, 2 * i + r + 1)
                        sp.dma_start(ev[:P, r, :], heads_dram[ds(2 * i + r, 1)].rearrange("t p f -> (t p) f")
                                     ).then_inc(sum_in[r], 16)
                        mask(n, i, r)

            def counts(n, c, cstat, width, off, hook):
                tile = n["tile"] + c * T
                for s in range(T):
                    hold(sp, p_low, tile + s + 1)
                    sp.dma_start(c_in[:, s % RING, 0:width], counts_dram[s][:, ds(off, width)]
                                 ).then_inc(c_ld[s % RING], 16)
                    hook(s)

            def hook_weights(n, following):
                def hook(s):
                    if following is not None and 0 <= s - 2 < weights_of(*following)[0]:
                        piece(n, *following, s - 2)
                return hook

            def across(n, kind, fb, act, bias, following, eps):
                counts(n, 0, 0, TW, 0, hook_weights(n, following))
                with sp.Fori(1, NC1) as c:
                    counts(n, c, 1, TW, c * TS, lambda s: None)

            def along(n, kind, layer, following, eps):
                hold(sp, ev_done, n["f1"] + 2)
                if layer:
                    for r in range(2):
                        hold(sp, stored[r], 16 * n["c2"])
                res = x_blocks if layer == 0 else y_dram[layer - 1]
                hold(sp, res_ready, 2 * n["c2"])
                last_bias = (L0_b2, L1_b, L2_b2, L3_b2)[layer]
                sp.dma_start(bias_row[:], last_bias.rearrange("(a f) -> a f", a=1).broadcast_to([P, D])
                             ).then_inc(bias_in, 16)

                def residual(c):
                    for r in range(2):
                        hold(sp, agg2_read, 2 * n["c2"] + 2 * c)
                        sp.dma_start(ev[:P, 2 + r, :], res[ds(2 * c + r, 1)].rearrange("t p f -> (t p) f")
                                     ).then_inc(res_in[r], 16)

                residual(0)
                counts(n, 0, 0, BW, 0, hook_weights(n, following))
                with sp.Fori(1, NC2) as c:
                    counts(n, c, 1, BW, c * BW, lambda s: residual(c) if s == 8 else None)

            def none(*_):
                pass

            program(sp, Stages(graph, turn_input, head_scores, maxima, product_sum, none, product, none, across, along, fold, none))

        @block.gpsimd
        def _(pool):
            pool.sem_inc(w_low, 2)
            pool.sem_inc(acc_done, RING)

            def graph():
                nc.gpsimd.memset(ident[:], 0.0).then_inc(graph_step, 1)
                nc.gpsimd.memset(ones[:], 1.0).then_inc(graph_step, 1)
                pool.wait_ge(graph_step, 2)
                nc.gpsimd.affine_select(out=ident[:], in_=ident[:], compare_op=ALU.not_equal, fill=1.0, base=0,
                                        pattern=[[-1, 128]], channel_multiplier=1).then_inc(graph_const, 1)
                nc.gpsimd.memset(zeros[:], 0.0).then_inc(graph_const, 1)
                nc.gpsimd.iota(iota_i[:], pattern=[[1, N]], base=0, channel_multiplier=0).then_inc(graph_const, 1)
                nc.gpsimd.iota(lim_i[:, 0, :], pattern=[[P, 12], [0, PER]], base=-P,
                               channel_multiplier=0).then_inc(graph_const, 1)
                nc.gpsimd.iota(lim_i[:, 1, :], pattern=[[P, 12], [0, PER]], base=P,
                               channel_multiplier=0).then_inc(graph_const, 1)
                with pool.Fori(0, T) as b:
                    pool.wait_ge(ct_out, b + 1)
                    diagonal = ct[:, ds(b * P, P)]
                    nc.gpsimd.tensor_tensor(diagonal, diagonal, ident[:P, :P], ALU.add).then_inc(ct_loop, 1)
                    pool.wait_ge(ct_loop, b + 1)
                    hold(pool, m_stored, 16 * b)
                    nc.gpsimd.tensor_scalar(m_out[:], ct[:], 0.0, NONE, ALU.is_equal, ALU.mult).then_inc(m_ready, 1)

            def piece(n, name, hd, k):
                pool.wait_ge(w_high, 2 * n["wp"] + k + 1)
                nc.gpsimd.tensor_tensor(w_place(1, name, k), ws[:, k % 2, :], w_place(0, name, k).bitcast(F32),
                                        ALU.subtract).then_inc(w_low, 1)
                if name == "L0_W2" and k == KH - 1:
                    pool.wait_ge(wa_high, n["av"] + 1)
                    nc.gpsimd.tensor_tensor(w2[1][:, :, D:HW], wa[:, 0:KH, :], w2[0][:, :, D:HW].bitcast(F32),
                                            ALU.subtract).then_inc(wa_low, 1)

            def split_w1(hd):
                for k in range(W1_PIECES):
                    cols = slice(k * KD * HID // W1_PIECES, (k + 1) * KD * HID // W1_PIECES)
                    pool.wait_ge(w1_high, W1_PIECES * hd + k + 1)
                    nc.gpsimd.tensor_tensor(w1[1][:, cols], w1_in[:, cols], w1[0][:, cols].bitcast(F32),
                                            ALU.subtract).then_inc(w1_low, 1)

            def head_scores():
                for k in range(2, KD):
                    pool.wait_ge(head_dot, 2 * HEADS * (k - 1))
                    pool.dma_start(w1_rows[:, k % 2, :], L0_W1[k * 128:(k + 1) * 128, :]).then_inc(rows_more[k % 2], 16)
                split_w1(0)

            def product_sum(before, n, hd, more):
                elu_part(before, NC1 - 1, KH)
                pool.wait_ge(zeroed, 16 * T)

                def pair(i):
                    for r in range(2):
                        q = n["q"] + 2 * i + r
                        pool.wait_ge(gemm_act, q + 3)
                        pool.wait_ge(gemm_dve, q + 3)
                        pool.dma_start(heads_dram[ds(2 * i + r, 1)].rearrange("t p f -> (t p) f"), add[:, r, :],
                                       accum_op=ALU.add).then_inc(sum_added[r], 16)

                in_segments(pool, pair, T // 2, {3: lambda: split_w1(hd + 1)} if more else {})

            def hook_weights(n, following, s):
                if following is not None and 0 <= s - 2 < weights_of(*following)[0]:
                    piece(n, *following, s - 2)

            def sum_tiles(n, c, hook):
                g, a = n["gat"] + c * T, n["acc"] + c * T
                for s in range(T):
                    pool.wait_ge(p_ready, g + s + 1)
                    if s == 0:
                        hold(pool, den_mm, n["den"] + c)
                        nc.gpsimd.tensor_copy(acc[:], tb[:, 0, :]).then_inc(acc_done, 1)
                    else:
                        pool.wait_ge(acc_done, a + s + RING)
                        nc.gpsimd.tensor_tensor(acc[:], acc[:], tb[:, s % RING, :], ALU.add).then_inc(acc_done, 1)
                    hook(s)

            def elu_part(n, c, fb):
                for f in range(fb):
                    e = n["elu"] + c * fb + f
                    hold(pool, ev_act, 2 * e + 1)
                    nc.gpsimd.tensor_scalar(e_tile(f), e_tile(f), 1.0, -1.0,
                                            ALU.min, ALU.add).then_inc(ev_exp, 1)

            def across(n, kind, fb, act, bias, following, eps):
                if kind == "gat":
                    sum_tiles(n, 0, lambda s: hook_weights(n, following, s))
                else:
                    for s in range(T):
                        hook_weights(n, following, s)
                with pool.Fori(1, NC1) as c:
                    if kind == "gat":
                        sum_tiles(n, c, lambda s: elu_part(n, c - 1, fb) if s == chunk_ends(kind) + 1 and act == "elu" else None)

            def along(n, kind, layer, following, eps):
                dest = out_blocks if layer == 3 else y_dram[layer]

                def residual(c):
                    for r in range(2):
                        pool.wait_ge(bias_in, 16 * (layer + 1))
                        pool.wait_ge(res_in[r], 16 * (n["c2"] + c + 1))
                        nc.gpsimd.tensor_tensor(ev[:P, 2 + r, :], ev[:P, 2 + r, :], bias_row[:],
                                                ALU.add).then_inc(res_ready, 1)

                def store(c):
                    for r in range(2):
                        pool.wait_ge(y_ready, 2 * (n["c2"] + c) + r + 1)
                        pool.dma_start(dest[ds(2 * c + r, 1)].rearrange("t p f -> (t p) f"), ev[:P, r, :]
                                       ).then_inc(stored[r], 16)

                residual(0)
                for s in range(T):
                    hook_weights(n, following, s)
                with pool.Fori(1, NC2) as c:
                    store(c - 1)
                    residual(c)
                store(NC2 - 1)
                if layer == 3:
                    for r in range(2):
                        pool.wait_ge(stored[r], 16 * (n["c2"] + NC2))

            def none(*_):
                pass

            program(pool, Stages(graph, none, head_scores, none, product_sum, none, none, none, across, along, none, none))

        @block.scalar
        def _(act):
            def graph():
                with act.Fori(0, T) as b:
                    act.wait_ge(ct_summed, b + 1)
                    act.wait_ge(ct_turned, b)
                    act.wait_ge(m_ready, b)
                    act.wait_ge(ct_deg, b)
                    for j in range(3):
                        o, w = (TW + TS * (j - 1), TS) if j else (0, TW)
                        last = nc.scalar.activation(ct[:, o:o + w], ps[:P, j, 0:w], ACT.Copy)
                    last.then_inc(ct_out, 1)
                    act.wait_ge(ct_turned, b + 1)
                    act.wait_ge(c_stored, 16 * b)
                    for j in range(3):
                        k = min(4, T - 4 * j)
                        last = nc.scalar.activation(c_out[:, 4 * j:4 * j + k, :],
                                                    ps[:P, 4 + j, 0:k * P].rearrange("p (k q) -> p k q", q=P), ACT.Copy)
                    last.then_inc(c_ready, 1)
                act.wait_ge(ct_deg, T)
                nc.scalar.activation(dinv[:], deg[:], ACT.Sqrt).then_inc(root, 1)

            def turned(y, t, r, bank):
                act.wait_ge(y_turned, y + 3)
                for j in range(2):
                    last = nc.scalar.activation(XT[:, 3 * j:3 * j + 3, ds(t * P, P)],
                                                ps[:, bank + 2 * r + j, 0:3 * P].rearrange("p (k q) -> p k q", q=P), ACT.Copy)
                last.then_inc(xt_ready, 1)

            def turn_input():
                with act.Fori(0, T // 2) as i:
                    for r in range(2):
                        turned(2 * i + r, 2 * i + r, r, 4)

            def piece(n, name, hd, k):
                if k == 0:
                    act.wait_ge(gemm_done, n["q"] + 2)
                act.wait_ge(w_in[k % 2], 16 * (n["wp"] + k // 2 + 1))
                nc.scalar.activation(w_place(0, name, k), ws[:, k % 2, :], ACT.Copy).then_inc(w_high, 1)

            def split_w1(hd):
                act.wait_ge(w1_ld, 16 * (hd + 1))
                for k in range(W1_PIECES):
                    cols = slice(k * KD * HID // W1_PIECES, (k + 1) * KD * HID // W1_PIECES)
                    nc.scalar.activation(w1[0][:, cols], w1_in[:, cols], ACT.Copy).then_inc(w1_high, 1)

            def head_scores():
                act.wait_ge(head_dot, 2 * HEADS * KD)
                split_w1(0)
                row(x_row, P, dict(START, rows=0), 0)

            def product_sum(before, n, hd, more):
                act.wait_ge(ev_done, n["f1"] - KH + 2)

                def finish(t, r, i):
                    act.wait_ge(gemm_done, n["q"] + t + 3)
                    act.wait_ge(sum_added[r], 16 * (n["sp"] + i))
                    nc.scalar.activation(add[:, r, 0:HALF], ps[:P, 4 + 2 * r, 0:HALF], ACT.Copy).then_inc(gemm_act, 1)

                def started():
                    finish_across(before, NC1 - 1, KH, "elu", hd * KH)
                    if more:
                        act.wait_ge(t_ready, n["gat"])
                        row(x_row, P, n, 0, 0)

                def last_chunk():
                    act.wait_ge(ev_done, n["f1"] + 2)
                    act.sem_inc(held, 1)

                hooks = {1: last_chunk}
                if more:
                    hooks[3] = lambda: split_w1(hd + 1)
                blocks_ahead(act, lambda t, r: split_block(n, KH, t, r), finish, started, hooks)

            def row(dest, parts, n, k, bank=5):
                act.wait_ge(row_mm, n["rows"] + k + 1)
                for j in range(3):
                    w = min(4, T - 4 * j) * P
                    last = nc.scalar.activation(dest[:parts, 4 * P * j:4 * P * j + w], ps[:parts, bank + j, 0:w], ACT.Copy)
                last.then_inc(row_ready, 1)

            def scores(n, kb, what):
                if what == "use":
                    act.wait_ge(t_ready, n["gat"])
                    row(x_row, P, n, 0)

            def split_block(n, kb, t, r):
                act.wait_ge(gemm_done, n["q"] + t + 1)
                src_ = sources(kb)
                for tile, k0 in src_:
                    kn = kb // len(src_)
                    last = nc.scalar.activation(ys_hi[:, r, k0:k0 + kn, :], tile[:, 0:kn, ds(t * P, P)], ACT.Copy)
                last.then_inc(split_high, 1)

            def product(n, kb, width, with_max, scale, kind, hd=None):
                act.wait_ge(xt_ready, n["y"] + 2)
                act.wait_ge(ev_done, n["f1"] + 2)

                def finish(t, r, i):
                    act.wait_ge(gemm_done, n["q"] + t + 3)
                    nc.scalar.activation(h_block(h_hi, width, t), ps_block(r, width), ACT.Copy,
                                         scale=1.0 if scale is None else scale[:, ds(t, 1)]).then_inc(gemm_act, 1)

                def started():
                    if scale is not None:
                        act.wait_ge(dinv_ready, 1)
                    if hd is not None:
                        for r in range(2):
                            act.wait_ge(sum_added[r], 16 * n["sp"])

                def x_out():
                    act.wait_ge(maxed, 2 * n["mp"] + 2)
                    row(x_row, P, n, 0)
                    act.sem_inc(held, 1)

                def y_out():
                    act.wait_ge(t_ready, n["gat"])
                    row(y_row, P, n, 1)

                blocks_ahead(act, lambda t, r: split_block(n, kb, t, r), finish, started,
                             {} if hd is None else {1: x_out, 3: y_out})

            def maxima(n):
                pass

            def columns(n):
                act.wait_ge(maxed, 2 * n["mp"] + 2)
                row(x_row, P, n, 0)
                act.wait_ge(t_ready, n["gat"])
                row(y_row, P, n, 1)

            def degree_row(n):
                row(x_row, 128, n, 0)

            def fold(n):
                act.wait_ge(t_ready, n["gat"])
                row(x_row, P, n, 0)
                with act.Fori(0, T // 2) as i:
                    for r in range(2):
                        act.wait_ge(sum_in[r], 16 * (i + 1))
                        nc.scalar.activation(h_block(h_hi, D, 2 * i + r), halves(ev[:P, r, :]), ACT.Copy).then_inc(fold_act, 1)

            def tiles(n, c, kind, width, hook):
                t0, g = n["tile"] + c * T, n["gat"] + c * T

                def exp(s):
                    act.wait_ge(t_ready, g + s + 1)
                    nc.scalar.activation(tb[:, s % RING, 0:width], tb[:, s % RING, 0:width], ACT.Exp,
                                         bias=s02[:, s:s + 1]).then_inc(e_ready, 1)

                def high(s):
                    if kind == "gat":
                        act.wait_ge(p_ready, g + s + 1)
                        tile = tb[:, s % RING, 0:width]
                    else:
                        act.wait_ge(c_ld[s % RING], 16 * (2 * (n["chunks"] + c) + s // RING + 1))
                        tile = c_in[:, s % RING, 0:width]
                    act.wait_ge(tile_used, t0 + s + 1)
                    nc.scalar.activation(p_hi[:, s % RING, 0:width], tile, ACT.Copy).then_inc(p_high, 1)

                for s in range(T + 1):
                    if s < T and kind == "gat":
                        exp(s)
                    if s < T and kind == "gcn":
                        high(s)
                    if s >= 1 and kind == "gat":
                        high(s - 1)
                    hook(s)

            def hook_weights(n, following, s):
                if following is not None and 0 <= s - 2 < weights_of(*following)[0]:
                    piece(n, *following, s - 2)

            def finish_across(n, c, fb, what, bias):
                for f in range(fb):
                    v = n["f1"] + c * fb + f
                    act.wait_ge(ev_scaled, v + 1)
                    z, b = z_tile(f), b_col[:, ds(bias + f, 1)]
                    if what == "elu":
                        nc.scalar.activation(e_tile(f), z, ACT.Exp, bias=b).then_inc(ev_act, 1)
                        hold(act, ev_act, 2 * (n["elu"] + c * fb + f) + 1)
                        nc.scalar.activation(z, z, ACT.Relu, bias=b).then_inc(ev_act, 1)
                    else:
                        nc.scalar.activation(XT[:, f, ds(c * TS, TW)], z, ACT.Relu, bias=b).then_inc(ev_done, 1)

            def across(n, kind, fb, what, bias, following, eps):
                act.wait_ge(b_in, 48)
                act.wait_ge(gemm_done, n["q"] + 2)

                def hook(s):
                    hook_weights(n, following, s)
                    if following[0] == "L0_W2" and s == T:
                        act.wait_ge(w_dot, 2 * (n["dot"] + KH) + 4)
                        nc.scalar.activation(w2[0][:, :, D:HW], wa[:, 0:KH, :], ACT.Copy).then_inc(wa_high, 1)

                tiles(n, 0, kind, TW, hook)
                with act.Fori(1, NC1) as c:
                    tiles(n, c, kind, TW, lambda s: finish_across(n, c - 1, fb, what, bias)
                          if s == chunk_ends(kind) + (1 if kind == "gcn" or what == "elu" else 0) else None)
                if what != "elu":
                    finish_across(n, NC1 - 1, fb, what, bias)

            def along(n, kind, layer, following, eps):
                def deviation(c):
                    act.wait_ge(var_ready, 2 * (n["c2"] + c) + 2)
                    nc.scalar.activation(rstd[:], mv[:, :, 1], ACT.Sqrt, bias=eps_col[:, 0:1]).then_inc(std_ready, 1)

                def turn(c, bank):
                    if layer < 3:
                        for r in range(2):
                            turned(n["y"] + 2 * c + r, 2 * c + r, r, bank)

                tiles(n, 0, kind, BW, lambda s: hook_weights(n, following, s))
                with act.Fori(0, NC2 // 2) as i:
                    for k, bank in ((0, 0), (1, 4)):
                        c = 2 * i + k
                        tiles(n, c + 1, kind, BW,
                              lambda s: deviation(c) if s == chunk_ends(kind) + 2
                              else turn(c, bank) if s == T else None)
                deviation(NC2 - 1)
                turn(NC2 - 1, 0)

            program(act, Stages(graph, turn_input, head_scores, maxima, product_sum, scores, product, columns, across, along,
                                fold, degree_row))

        @block.vector
        def _(dve):
            dve.sem_inc(w_dot, 4)
            dve.sem_inc(gemm_dve, 2)
            dve.sem_inc(gemm_act, 2)
            dve.sem_inc(maxed, 2)
            dve.sem_inc(fold_dve, 2)
            dve.sem_inc(p_low, RING)
            dve.sem_inc(ev_done, 2)

            def graph():
                chain = [0]

                def link(ins):
                    chain[0] += 1
                    ins.then_inc(step, 1)
                    dve.wait_ge(step, chain[0])

                link(nc.vector.memset(eps_col[:], EPS))
                nc.vector.memset(score_sum[:], 0.0).then_inc(summed, 1)
                link(nc.vector.memset(src_col[:], 0.0))
                link(nc.vector.memset(dst_col[:], -1.0))
                dve.wait_ge(edges_in, 32)
                nc.vector.tensor_copy(e_flt[:], e_int[:]).then_inc(edges_flt, 1)
                dve.wait_ge(edges_turned, 1)
                for i, col in enumerate((src_col, dst_col)):
                    link(nc.vector.tensor_copy(col[:, SLACK:SLACK + EC].rearrange("p (q h) -> p h q", h=2),
                                               ps[:P, 4, i * EC:(i + 1) * EC].rearrange("p (h q) -> p h q", h=2)))
                dve.wait_ge(graph_const, 5)
                link(nc.vector.tensor_copy(iota[:], iota_i[:]))
                link(nc.vector.tensor_copy(lim[:], lim_i[:]))
                real = dst_col[:, SLACK:SLACK + EC]
                low = lim[:, 0, 2 * (PER - SLACK) - PER + SLACK:][:, 0:EC]
                high = lim[:, 1, 2 * SLACK:2 * SLACK + EC]
                link(nc.vector.tensor_tensor(out_of[:, 0, :], low, real, ALU.is_gt))
                link(nc.vector.tensor_tensor(out_of[:, 1, :], real, high, ALU.is_ge))
                nc.vector.tensor_reduce(bad[:], out_of[:].rearrange("p a c -> p (a c)"), AX.X, ALU.add
                                        ).then_inc(bad_ready, 1)
                dve.wait_ge(bad_summed, 1)
                link(nc.vector.tensor_scalar(par_f[:, 0:1], ps[0:1, 4, 0:1], 1.0, None, ALU.min))
                for j, (sorted_, all_) in enumerate((((WIN - 2) // OH, (ECP - 2) // OH), (PER, 0), (WIN, ECP))):
                    link(nc.vector.tensor_scalar(par_f[:, j + 1:j + 2], par_f[:, 0:1], float(all_ - sorted_),
                                                 float(sorted_), ALU.mult, ALU.add))
                nc.vector.tensor_copy(params[:], par_f[:]).then_inc(par_ready, 1)
                dve.wait_ge(par_ready, 1)
                turns = dve.value_load(params[0:1, 1:2], min_val=(WIN - 2) // OH, max_val=(ECP - 2) // OH)
                stride = dve.value_load(params[0:1, 2:3], min_val=0, max_val=PER)
                count = dve.value_load(params[0:1, 3:4], min_val=WIN, max_val=ECP)

                def one_hot(b, j, slot):
                    col = ds(nc.s_assert_within(stride * b + j, 0, ECP - 1, skip_runtime_bounds_check_because=
                                              "stride, turns and count come as (PER, ., WIN) or (0, ., ECP)"), 1)
                    dve.wait_ge(oh_used, count * b + j + 1)
                    nc.vector.tensor_scalar(oh_src[:, slot, :], iota[:], src_col[:, col], None, ALU.is_equal)
                    nc.vector.tensor_scalar(oh_dst[:, slot, :], iota[:, 0:P], dst_col[:, col], None,
                                            ALU.is_equal).then_inc(oh_ready, 1)

                with dve.Fori(0, T) as b:
                    one_hot(b, 0, 0)
                    with dve.Fori(0, turns) as i:
                        for k in range(OH):
                            one_hot(b, i * OH + 1 + k, (1 + k) % OH)
                    one_hot(b, count - 1, (WIN - 1) % OH)
                    dve.wait_ge(oh_ready, count * b + count)
                    nc.vector.tensor_scalar(dst_col[:], dst_col[:], float(-P), None, ALU.add).then_inc(step, 1)
                    dve.wait_ge(step, b + (chain[0] + 1))
                    dve.wait_ge(ct_loop, b + 1)
                    nc.vector.tensor_reduce(deg[:, ds(b, 1)], ct[:], AX.X, ALU.add).then_inc(ct_deg, 1)
                dve.wait_ge(ct_deg, T)
                nc.vector.tensor_scalar(many[:], deg[:], EXACT, None, ALU.is_gt).then_inc(step, 1)
                dve.wait_ge(step, chain[0] + T + 1)
                nc.vector.tensor_reduce(many_any[:], many[:], AX.X, ALU.add).then_inc(many_ready, 1)
                dve.wait_ge(many_summed, 1)
                nc.vector.tensor_scalar(par_f[:, 0:1], ps[0:1, 3, 0:1], 1.0, None, ALU.min).then_inc(step, 1)
                dve.wait_ge(step, chain[0] + T + 2)
                nc.vector.tensor_copy(params[:, 0:1], par_f[:, 0:1]).then_inc(low_ready, 1)
                dve.wait_ge(root, 1)
                nc.vector.reciprocal(dinv[:], dinv[:]).then_inc(dinv_ready, 1)
                assert chain[0] + T + 2 == GRAPH_STEPS, chain[0]

            def chain_from(semaphore, start):
                at_ = [start]

                def link(ins):
                    at_[0] = at_[0] + 1
                    ins.then_inc(semaphore, 1)
                    dve.wait_ge(semaphore, at_[0])
                return link

            def piece(n, name, hd, k):
                width = weights_of(name, hd)[1]
                if vectors_of(name, hd) is None:
                    return
                if k == 0:
                    dve.wait_ge(score_mm, n["sc"])
                    dve.wait_ge(a_in, 32 * n["av"] + 32)
                    dve.wait_ge(ev_scaled, n["f1"])
                    dve.wait_ge(ev_done, n["f1"] + 2)
                dve.wait_ge(w_in[k % 2], 16 * (n["wp"] + k // 2 + 1))
                for j in range(2):
                    hold(dve, w_dot, 2 * (n["dot"] + k) + j + 4)
                    nc.vector.tensor_tensor_reduce(
                        out=r_row[:].bitcast(BF16)[:, 0:width], in0=ws[:, k % 2, 0:width], in1=a_row[:, j, 0:width],
                        scale=1.0, scalar=0.0, op0=ALU.mult, op1=ALU.add, accum_out=wa[:, k, j:j + 1]).then_inc(w_dot, 1)

            def head_scores():
                dve.wait_ge(a1_in, 32)
                for k in range(KD):
                    dve.wait_ge(*((rows_in[k], 16) if k < 2 else (rows_more[k % 2], 16 * (k // 2))))
                    for hd in range(HEADS):
                        for j in range(2):
                            at_ = 2 * (HEADS * k + hd) + j
                            if at_:
                                dve.wait_ge(head_dot, at_)
                            nc.vector.tensor_tensor_reduce(
                                out=r_row[:].bitcast(BF16)[:, 0:HID], in0=w1_rows[:, k % 2, hd * HID:(hd + 1) * HID],
                                in1=a1_row[:, j * HEADS + hd, :], scale=1.0, scalar=0.0, op0=ALU.mult, op1=ALU.add,
                                accum_out=wa8[:, k, 2 * hd + j:2 * hd + j + 1]).then_inc(head_dot, 1)
                dve.wait_ge(score_mm, 1)
                nc.vector.tensor_copy(score8[:], ps[:P, 4, 0:2 * HEADS * T].rearrange("p (t j) -> p t j", j=2 * HEADS)
                                      ).then_inc(score_ready, 1)
                dve.wait_ge(score_ready, 1)
                take_scores(dict(START, step=GRAPH_STEPS), 0)

            def take_scores(n, hd):
                link = chain_from(step, n["step"])
                link(nc.vector.tensor_copy(score[:], score8[:, :, ds(2 * hd, 2)]))
                source_columns(link)

            def maxima(n):
                dve.wait_ge(row_ready, n["rows"])
                with dve.Fori(0, T // 2) as i:
                    for r in range(2):
                        masked_max(n, i, r)
                n = dict(n, mp=n["mp"] + T // 2)
                columns(n)

            def product_sum(before, n, hd, more):
                def finish(t, r, i):
                    dve.wait_ge(gemm_done, n["q"] + t + 3)
                    scores_ = ps[:P, 5 + 2 * r, HALF:HALF + 2]
                    nc.vector.tensor_tensor(score_sum[:, ds(t, 1), :].rearrange("p t j -> p (t j)"),
                                            score_sum[:, ds(t, 1), :].rearrange("p t j -> p (t j)"), scores_,
                                            ALU.add).then_inc(summed, 1)
                    dve.wait_ge(sum_added[r], 16 * (n["sp"] + i))
                    nc.vector.tensor_copy(add[:, r, HALF:D], ps[:P, 5 + 2 * r, 0:HALF]).then_inc(gemm_dve, 1)
                    if more:
                        masked_max(n, i, r)

                def started():
                    weights_summed(before, NC1 - 1, "gat", ("L0_W2", hd), 1e-16)
                    scaled(before, NC1 - 1, "gat", KH)
                    if more:
                        dve.wait_ge(e_ready, n["gat"])
                        dve.wait_ge(xy_ready, n["xy"])
                        take_scores(n, hd + 1)
                    elu_sum(before, NC1 - 1, KH)
                    if more:
                        dve.wait_ge(p_low, n["tile"] + RING)
                        dve.wait_ge(acc_done, n["acc"] + RING)
                        dve.wait_ge(row_ready, n["rows"] + 1)
                    hold(dve, summed, 2 * n["sp"] + 1)

                blocks_ahead(dve, lambda t, r: split_block(n, KH, t, r), finish, started)
                if more:
                    columns(dict(n, mp=n["mp"] + T // 2, step=n["step"] + 3))

            def source_columns(link):
                link(nc.vector.tensor_scalar(s08[:], score[:, :, 0], 1.0 - SLOPE, None, ALU.mult))
                link(nc.vector.tensor_scalar(s02[:], score[:, :, 0], SLOPE, None, ALU.mult))

            def scores(n, kb, what):
                dve.wait_ge(score_mm, n["sc"] + 1)
                got = ps[:P, 4, 0:2 * T].rearrange("p (t j) -> p t j", j=2)
                nc.vector.tensor_copy(score[:], got).then_inc(score_ready, 1)
                dve.wait_ge(score_ready, n["sc"] + 1)
                source_columns(chain_from(step, n["step"]))

            def masked_max(n, i, r):
                dve.wait_ge(maxed, 2 * (n["mp"] + i) + r + 2)
                dve.wait_ge(amax_ready, n["mp"] + i)
                hold(dve, mask_ld[r], 16 * (n["mp"] + i + 1))
                nc.vector.tensor_tensor_reduce(out=junk[:], in0=x_row[:P, :], in1=mask_in[r][:], scale=1.0, scalar=NONE,
                                               op0=ALU.add, op1=ALU.max, accum_out=pair_max[:, r:r + 1]).then_inc(maxed, 1)
                if r == 1:
                    dve.wait_ge(maxed, 2 * (n["mp"] + i) + 4)
                    nc.vector.tensor_copy(amax[:, ds(2 * i, 2)], pair_max[:]).then_inc(amax_ready, 1)

            def split_block(n, kb, t, r):
                dve.wait_ge(split_high, n["q"] + t + 1)
                src_ = sources(kb)
                for tile, k0 in src_:
                    kn = kb // len(src_)
                    last = nc.vector.tensor_tensor(ys_lo[:, r, k0:k0 + kn, :], tile[:, 0:kn, ds(t * P, P)],
                                                   ys_hi[:, r, k0:k0 + kn, :].bitcast(F32), ALU.subtract)
                last.then_inc(split_low, 1)

            def product(n, kb, width, with_max, scale, kind, hd=None):
                dve.wait_ge(xt_ready, n["y"] + 2)
                dve.wait_ge(ev_done, n["f1"] + 2)
                if scale is not None:
                    dve.wait_ge(dinv_ready, 1)

                def started():
                    if with_max:
                        dve.wait_ge(p_low, n["tile"] + RING)
                        dve.wait_ge(acc_done, n["acc"] + RING)
                        dve.wait_ge(row_ready, n["rows"])

                def finish(t, r, i):
                    q = n["q"] + t
                    dve.wait_ge(gemm_done, q + 3)
                    dve.wait_ge(gemm_act, q + 3)
                    nc.vector.scalar_tensor_tensor(
                        out=h_block(h_lo, width, t), in0=ps_block(r, width),
                        scalar=1.0 if scale is None else scale[:, ds(t, 1)],
                        in1=h_block(h_hi, width, t).bitcast(F32), op0=ALU.mult, op1=ALU.subtract).then_inc(gemm_dve, 1)
                    if with_max:
                        masked_max(n, i, r)

                blocks_ahead(dve, lambda t, r: split_block(n, kb, t, r), finish, started)

            def columns(n):
                link = chain_from(step, n["step"])
                dve.wait_ge(amax_ready, n["mp"])
                link(nc.vector.tensor_tensor(mcol[:], amax[:], score[:, :, 1], ALU.add))
                link(nc.vector.scalar_tensor_tensor(out=mcol[:], in0=mcol[:], scalar=SLOPE, in1=mcol[:],
                                                    op0=ALU.mult, op1=ALU.max))
                link(nc.vector.tensor_tensor(xcol[:], score[:, :, 1], mcol[:], ALU.subtract))
                nc.vector.scalar_tensor_tensor(out=ycol[:], in0=score[:, :, 1], scalar=SLOPE, in1=mcol[:],
                                               op0=ALU.mult, op1=ALU.subtract).then_inc(xy_ready, 1)

            def fold(n):
                dve.wait_ge(gemm_done, n["q"] + 2)
                for r in range(2):
                    dve.wait_ge(sum_added[r], 16 * n["sp"])
                dve.wait_ge(summed, 2 * n["sp"] + 1)
                link = chain_from(step, n["step"])
                nc.vector.memset(h_view(h_hi, D)[:, :, D:HW].bitcast(F32), 1.0).then_inc(ones_set, 1)
                nc.vector.memset(h_view(h_lo, D)[:, :, D:HW].bitcast(F32), 0.0).then_inc(ones_set, 1)
                link(nc.vector.tensor_copy(score[:], score_sum[:]))
                source_columns(link)
                dve.wait_ge(p_low, n["tile"] + RING)
                dve.wait_ge(acc_done, n["acc"] + RING)
                dve.wait_ge(row_ready, n["rows"] + 1)
                with dve.Fori(0, T // 2) as i:
                    for r in range(2):
                        dve.wait_ge(fold_act, 2 * i + r + 1)
                        nc.vector.tensor_tensor(h_block(h_lo, D, 2 * i + r), halves(ev[:P, r, :]),
                                                h_block(h_hi, D, 2 * i + r).bitcast(F32), ALU.subtract).then_inc(fold_dve, 1)
                        masked_max(n, i, r)

            def tiles(n, c, kind, width, off, sums, hook):
                t0, g, a = n["tile"] + c * T, n["gat"] + c * T, n["acc"] + c * T

                def larger(s):
                    dve.wait_ge(p_low, t0 + s + 1)
                    if sums:
                        dve.wait_ge(acc_done, a + s + 1)
                    nc.vector.scalar_tensor_tensor(out=tb[:, s % RING, 0:width], in0=x_row[:P, ds(off, width)],
                                                   scalar=s08[:, s:s + 1], in1=y_row[:, ds(off, width)],
                                                   op0=ALU.add, op1=ALU.max).then_inc(t_ready, 1)

                def count(s):
                    dve.wait_ge(e_ready, g + s + 1)
                    dve.wait_ge(c_ld[s % RING], 16 * (2 * (n["chunks"] + c) + s // RING + 1))
                    nc.vector.scalar_tensor_tensor(out=tb[:, s % RING, 0:width], in0=tb[:, s % RING, 0:width],
                                                   scalar=1.0, in1=c_in[:, s % RING, 0:width],
                                                   op0=ALU.min, op1=ALU.mult).then_inc(p_ready, 1)

                def low(s):
                    dve.wait_ge(p_high, t0 + s + 1)
                    tile = tb if kind == "gat" else c_in
                    nc.vector.tensor_tensor(p_lo[:, s % RING, 0:width], tile[:, s % RING, 0:width],
                                            p_hi[:, s % RING, 0:width].bitcast(F32), ALU.subtract).then_inc(p_low, 1)

                if kind == "gcn":
                    for s in range(T):
                        low(s)
                        hook(s)
                    return
                for s in range(T + 2):
                    if s < T:
                        larger(s)
                    if 1 <= s <= T:
                        count(s - 1)
                    if s >= 2:
                        low(s - 2)
                    hook(s)

            def hook_weights(n, following, s):
                if following is not None and 0 <= s - 2 < weights_of(*following)[0]:
                    piece(n, *following, s - 2)

            def weights_summed(n, c, kind, following, eps):
                dots = n["dot"] + (weights_of(*following)[0] if vectors_of(*following) else 0)
                dve.wait_ge(w_dot, 2 * dots + 4)
                if kind == "gcn":
                    return
                fb = KH if eps else KD
                dve.wait_ge(ev_scaled, n["f1"] + c * fb)
                dve.wait_ge(ev_done, n["f1"] + c * fb + 2)
                dve.wait_ge(den_mm, n["den"] + c + 1)
                total = ps[:, sum_bank(fb, c), 0:TW]
                if eps:
                    link = chain_from(step, n["step"] + c)
                    link(nc.vector.tensor_scalar(r_row[:], total, eps, None, ALU.add))
                    total = r_row[:]
                nc.vector.reciprocal(r_row[:], total).then_inc(r_ready, 1)

            def scaled(n, c, kind, fb):
                dve.wait_ge(ev_done, n["f1"] + c * fb + 2)
                if kind == "gat":
                    dve.wait_ge(r_ready, n["den"] + c + 1)
                scale = r_row[:] if kind == "gat" else x_row[:, ds(c * TS, TW)]
                for f in range(fb):
                    dve.wait_ge(agg_mm, n["f1"] + c * fb + f + 1)
                    nc.vector.tensor_tensor(z_tile(f), ps[:, first_bank(fb, c) + f, 0:TW], scale, ALU.mult
                                            ).then_inc(ev_scaled, 1)

            def elu_sum(n, c, fb):
                for f in range(fb):
                    e = n["elu"] + c * fb + f
                    dve.wait_ge(ev_act, 2 * e + 2)
                    dve.wait_ge(ev_exp, e + 1)
                    nc.vector.tensor_tensor(ot[f // 2][:, f % 2, ds(c * TS, TW)], z_tile(f), e_tile(f),
                                            ALU.add).then_inc(ev_done, 1)

            def across(n, kind, fb, what, bias, following, eps):
                dve.wait_ge(maxed, 2 * n["mp"] + 2)
                dve.wait_ge(row_ready, n["rows"])
                dve.wait_ge(gemm_done, n["q"] + 2)
                if kind == "gcn" or fb == KD:
                    for r in range(2):
                        dve.wait_ge(stored[r], 16 * n["c2"])

                tiles(n, 0, kind, TW, 0, kind == "gat", lambda s: hook_weights(n, following, s))

                def hook(c, s):
                    if s == chunk_ends(kind):
                        weights_summed(n, c, kind, following, eps)
                    if s == chunk_ends(kind) + (1 if what == "elu" else 0):
                        scaled(n, c, kind, fb)
                    if s == chunk_ends(kind) + 3 and what == "elu":
                        elu_sum(n, c, fb)

                other_chunks(dve, fb, lambda c: tiles(n, c, kind, TW, c * TS, kind == "gat", lambda s: hook(c - 1, s)))
                if what != "elu":
                    weights_summed(n, NC1 - 1, kind, following, eps)
                    scaled(n, NC1 - 1, kind, fb)

            def along(n, kind, layer, following, eps):
                dve.wait_ge(maxed, 2 * n["mp"] + 2)
                dve.wait_ge(row_ready, n["rows"])

                def statistics(c, bank):
                    link = chain_from(ln_step, n["ln"] + c * ln_links(kind, eps))
                    dve.wait_ge(y_ready, 2 * (n["c2"] + c))
                    for r in range(2):
                        b = 2 * (n["c2"] + c) + r
                        dve.wait_ge(agg2_mm, n["c2"] + c + 1)
                        if kind == "gat":
                            total = ps[:P, bank + 2 * r + 1, HALF:HALF + 1]
                            if eps:
                                link(nc.vector.tensor_scalar(rden[:, r, 0:1], total, eps, None, ALU.add))
                                total = rden[:, r, 0:1]
                            link(nc.vector.reciprocal(rden[:, r, 1:2], total))
                            by = rden[:, r, 1:2]
                        else:
                            by = dinv[:, ds(2 * c + r, 1)]
                        dve.wait_ge(res_ready, b + 1)
                        dve.wait_ge(stored[r], 16 * (n["c2"] + c))
                        dve.wait_ge(y_turned, n["y"] + (2 if layer == 3 else 2 * c + r + 1))
                        y = ev[:P, r, :]
                        nc.vector.scalar_tensor_tensor(out=halves(y), in0=ps[:P, bank + 2 * r:bank + 2 * r + 2, 0:HALF], scalar=by,
                                                       in1=halves(ev[:P, 2 + r, :]), op0=ALU.mult, op1=ALU.add
                                                       ).then_inc(agg2_read, 1)
                    for r in range(2):
                        dve.wait_ge(agg2_read, 2 * (n["c2"] + c) + r + 1)
                        for j in range(2):
                            link(nc.vector.bn_stats(stats[:, r, j, :], ev[:P, r, j * HALF:(j + 1) * HALF]))
                        dve.sem_inc(held, 1)
                        nc.vector.bn_aggr(mv[:, r, :], stats[:, r, :, :].rearrange("p a b -> p (a b)")).then_inc(var_ready, 1)
                def normalised(c):
                    link = chain_from(ln_step, n["ln"] + (c + 1) * ln_links(kind, eps) - 1)
                    dve.wait_ge(var_ready, 2 * (n["c2"] + c) + 2)
                    dve.wait_ge(std_ready, n["c2"] + c + 1)
                    link(nc.vector.reciprocal(rstd[:], rstd[:]))
                    for r in range(2):
                        y = ev[:P, r, :]
                        nc.vector.tensor_scalar(y, y, mv[:, r, 0:1], rstd[:, r:r + 1], ALU.subtract, ALU.mult
                                                ).then_inc(y_ready, 1)

                def hook(c, bank, s):
                    if s == chunk_ends(kind) + 1:
                        statistics(c, bank)
                    if s == chunk_ends(kind) + 3:
                        normalised(c)

                tiles(n, 0, kind, BW, 0, False, lambda s: hook_weights(n, following, s))
                with dve.Fori(0, NC2 // 2) as i:
                    for k, bank in ((0, 0), (1, 4)):
                        c = 2 * i + k
                        tiles(n, c + 1, kind, BW, (c + 1) * BW, False, lambda s: hook(c, bank, s))
                statistics(NC2 - 1, 0)
                normalised(NC2 - 1)

            def none(*_):
                pass

            program(dve, Stages(graph, none, head_scores, maxima, product_sum, scores, product, columns, across, along, fold, none))

        @block.tensor
        def _(pe):
            pe.sem_inc(oh_used, OH)
            pe.sem_inc(y_turned, 2)
            pe.sem_inc(xt_ready, 2)
            pe.sem_inc(gemm_done, 2)
            pe.sem_inc(tile_used, RING)

            def graph():
                pe.wait_ge(graph_const, 1)
                pe.wait_ge(edges_flt, 1)
                for i in range(2):
                    for h in range(2):
                        o = i * EC + h * (EC // 2)
                        last = pe.transpose(ps[:P, 4, o:o + EC // 2], e_flt[:, i, h * P:(h + 1) * P],
                                            ident[0:EC // 2, 0:EC // 2])
                last.then_inc(edges_turned, 1)
                pe.wait_ge(bad_ready, 1)
                pe.matmul(ps[0:1, 4, 0:1], bad[:], ones[:, 0:1], start=True, stop=True).then_inc(bad_summed, 1)
                pe.wait_ge(par_ready, 1)
                turns = pe.value_load(params[0:1, 1:2], min_val=(WIN - 2) // OH, max_val=(ECP - 2) // OH)
                count = pe.value_load(params[0:1, 3:4], min_val=WIN, max_val=ECP)

                def add(b, j, slot, start, stop):
                    pe.wait_ge(oh_ready, count * b + j + 1)
                    for k in range(3):
                        o, w = (TW + TS * (k - 1), TS) if k else (0, TW)
                        last = pe.matmul(ps[:P, k, 0:w], oh_dst[:, slot, :], oh_src[:, slot, o:o + w],
                                         start=start, stop=stop)
                    last.then_inc(oh_used, 1)
                    return last

                with pe.Fori(0, T) as b:
                    pe.wait_ge(ct_out, b)
                    add(b, 0, 0, True, False)
                    with pe.Fori(0, turns) as i:
                        for k in range(OH):
                            add(b, i * OH + 1 + k, (1 + k) % OH, False, False)
                    add(b, count - 1, (WIN - 1) % OH, False, True)
                    pe.wait_ge(oh_used, count * b + count + OH)
                    pe.sem_inc(ct_summed, 1)
                    pe.wait_ge(ct_loop, b + 1)
                    pe.wait_ge(c_ready, b)
                    for j in range(T):
                        last = pe.transpose(ps[:P, 4 + j // 4, (j % 4) * P:(j % 4 + 1) * P], ct[:, j * P:(j + 1) * P],
                                            ident[:P, :P])
                    last.then_inc(ct_turned, 1)
                pe.wait_ge(many_ready, 1)
                pe.matmul(ps[0:1, 3, 0:1], many_any[:], ones[:, 0:1], start=True, stop=True).then_inc(many_summed, 1)

            def low_passes():
                pe.wait_ge(low_ready, 1)
                return pe.value_load(params[0:1, 0:1], min_val=0, max_val=1)

            def turn(y, r, bank):
                for k in range(KD):
                    last = pe.transpose(ps[:, bank + 2 * r + k // 3, (k % 3) * P:(k % 3 + 1) * P],
                                        ev[:P, r, k * 128:(k + 1) * 128], ident[:P, :P])
                last.then_inc(y_turned, 1)

            def turn_input():
                pe.wait_ge(c_ready, T)
                with pe.Fori(0, T // 2) as i:
                    for r in range(2):
                        pe.wait_ge(x_in[r], 16 * (i + 1))
                        pe.wait_ge(xt_ready, 2 * i + r + 1)
                        turn(2 * i + r, r, 4)

            def banks_free(n):
                pe.wait_ge(xt_ready, n["y"] + 2)
                pe.wait_ge(row_ready, n["rows"])
                pe.wait_ge(score_ready, n["sc"])
                pe.wait_ge(gemm_act, n["q"] + 2)
                pe.wait_ge(gemm_dve, n["q"] + 2)
                pe.wait_ge(ev_scaled, n["f1"])
                pe.wait_ge(r_ready, n["den"])
                pe.wait_ge(agg2_read, 2 * n["c2"])

            def row(n, k, col, parts, bank=5):
                pe.wait_ge(row_ready, n["rows"] + k)
                for t in range(T):
                    last = pe.matmul(ps[:parts, bank + t // 4, (t % 4) * P:(t % 4 + 1) * P],
                                     col(t).broadcast_to([P, parts]), ident[:P, :P], start=True, stop=True)
                last.then_inc(row_mm, 1)

            def scores(n, kb, what):
                banks_free(n)
                pe.wait_ge(ev_done, n["f1"] + 2)
                pe.wait_ge(w_dot, 2 * n["dot"] + 4)
                for t in range(T):
                    for k in range(kb):
                        last = pe.matmul(ps[:P, 4, 2 * t:2 * t + 2], source_block(kb, k, slice(t * P, (t + 1) * P)),
                                         wa[:, k, :], start=(k == 0), stop=(k == kb - 1))
                last.then_inc(score_mm, 1)
                if what == "use":
                    pe.wait_ge(score_ready, n["sc"] + 1)
                    row(n, 0, lambda t: score[:, t, 0:1], P)

            def head_scores():
                pe.wait_ge(head_dot, 2 * HEADS * KD)
                pe.wait_ge(xt_ready, T + 2)
                for t in range(T):
                    for k in range(KD):
                        last = pe.matmul(ps[:P, 4, 2 * HEADS * t:2 * HEADS * (t + 1)], XT[:, k, t * P:(t + 1) * P],
                                         wa8[:, k, :], start=(k == 0), stop=(k == KD - 1))
                last.then_inc(score_mm, 1)
                pe.wait_ge(step, GRAPH_STEPS + 1)
                source_row(dict(START, rows=0), 5)

            def source_row(n, bank):
                row(n, 0, lambda t: score[:, t, 0:1], P, bank)

            def product_sum(before, n, hd, more):
                hold(pe, w_low, 2 * n["wp"] + 2)
                pe.wait_ge(wa_low, n["av"])
                pe.wait_ge(row_ready, n["rows"])

                def one(t, r):
                    pe.wait_ge(split_high, n["q"] + t + 1)
                    pe.wait_ge(split_low, n["q"] + t + 1)
                    pe.wait_ge(gemm_act, n["q"] + t + 1)
                    pe.wait_ge(gemm_dve, n["q"] + t + 1)
                    if r == 1:
                        pe.wait_ge(r_ready, n["den"])
                    for j, (o, w) in enumerate(((0, HALF), (HALF, HW - HALF))):
                        for k in range(KH):
                            for m, (a, b) in enumerate(PASSES):
                                last = pe.matmul(ps[:P, 4 + 2 * r + j, 0:w], (ys_hi, ys_lo)[a][:, r, k, :],
                                                 w2[b][:, k, o:o + w], start=(k == 0 and m == 0),
                                                 stop=(k == KH - 1 and m == 2))
                    last.then_inc(gemm_done, 1)

                one(0, 0)
                one(1, 1)
                if more:
                    pe.wait_ge(ev_scaled, n["f1"])
                    pe.wait_ge(step, n["step"] + 1)
                    source_row(n, 0)
                with pe.Fori(1, T // 2) as i:
                    for r in range(2):
                        one(2 * i + r, r)

            def product(n, kb, width, with_max, scale, kind, hd=None):
                pe.wait_ge(agg2_read, 2 * n["c2"])
                pe.wait_ge(xt_ready, n["y"] + 2)
                pe.wait_ge(ev_scaled, n["f1"])
                if hd is None:
                    hold(pe, w_low, 2 * n["wp"] + 2)
                else:
                    hold(pe, w1_low, W1_PIECES * (hd + 1))
                    pe.wait_ge(gemm_act, n["q"] + 2)
                    pe.wait_ge(gemm_dve, n["q"] + 2)
                    pe.wait_ge(row_ready, n["rows"])
                w = (w_hi, w_lo) if hd is None else w1
                banks = 1 if width == HID else 2
                bw = width // banks

                def one(q, r):
                    pe.wait_ge(split_high, q + 1)
                    pe.wait_ge(split_low, q + 1)
                    pe.wait_ge(gemm_act, q + 1)
                    pe.wait_ge(gemm_dve, q + 1)
                    for j in range(banks):
                        for k in range(kb):
                            for m, (a, b) in enumerate(PASSES):
                                o = k * width + j * bw
                                last = pe.matmul(ps[:P, 2 * r + j, 0:bw], (ys_hi, ys_lo)[a][:, r, k, :],
                                                 w[b][:, o:o + bw], start=(k == 0 and m == 0),
                                                 stop=(k == kb - 1 and m == 2))
                    last.then_inc(gemm_done, 1)

                def pair(i):
                    for r in range(2):
                        one(n["q"] + 2 * i + r, r)

                def x_row_mm():
                    pe.wait_ge(xy_ready, n["xy"])
                    row(n, 0, lambda t: xcol[:, t:t + 1], P)

                in_segments(pe, pair, T // 2, {} if hd is None else
                            {1: x_row_mm, 3: lambda: row(n, 1, lambda t: ycol[:, t:t + 1], P)})

            def columns(n):
                pe.wait_ge(xy_ready, n["xy"] + 1)
                row(n, 0, lambda t: xcol[:, t:t + 1], P)
                row(n, 1, lambda t: ycol[:, t:t + 1], P)

            def degree_row(n):
                pe.wait_ge(dinv_ready, 1)
                row(n, 0, lambda t: dinv[:, t:t + 1], 128)

            def fold(n):
                pe.wait_ge(score_ready, n["sc"])
                banks_free(n)
                row(n, 0, lambda t: score_sum[:, t, 0:1], P)
                pe.wait_ge(fold_act, T)
                pe.wait_ge(fold_dve, T + 2)
                pe.wait_ge(ones_set, 2)

            def across(n, kind, fb, what, bias, following, eps):
                banks_free(n)
                width = HID if fb == KH else D

                low = low_passes() if kind == "gcn" else None

                def chunk(c, first):
                    t0 = n["tile"] + c * T
                    for s in range(T):
                        pe.wait_ge(p_high, t0 + s + 1)
                        pe.wait_ge(p_low, t0 + s + 1 + RING)

                        def products(f, passes, start, stop):
                            for m, (a, b) in enumerate(passes):
                                last = pe.matmul(ps[:, first_bank(fb, c) + f, 0:TW],
                                                 h_view((h_hi, h_lo)[a], width)[:, s, f * 128:(f + 1) * 128],
                                                 (p_hi, p_lo)[b][:, s % RING, :], start=(start and m == 0),
                                                 stop=(stop and m == len(passes) - 1))
                            return last

                        def free(f):
                            if s == 0 and fb == KD and not first:
                                pe.wait_ge(ev_scaled, n["f1"] + (c - 1) * fb + f + 1)
                            if s == 0 and fb == KH and c >= 2:
                                pe.wait_ge(ev_scaled, n["f1"] + (c - 2) * fb + f + 1)
                            if s == 0 and fb == KH and c >= 1 and f == KH - 1:
                                pe.wait_ge(r_ready, n["den"] + c)

                        if s == T - 1 and kind == "gat":
                            pe.wait_ge(acc_done, n["acc"] + c * T + T + RING)
                            pe.wait_ge(r_ready, n["den"] + c)
                            if fb == KH:
                                pe.wait_ge(ev_scaled, n["f1"] + c * fb)
                            pe.matmul(ps[:, sum_bank(fb, c), 0:TW], ones[:].broadcast_to([P, 128]), acc[:],
                                      start=True, stop=True).then_inc(den_mm, 1)
                        if kind == "gcn":
                            for f in range(fb):
                                free(f)
                                products(f, PASSES[0:1], s == 0, False)
                            with pe.If(low > 0):
                                for f in range(fb):
                                    products(f, PASSES[1:2], False, False)
                        for f in range(fb):
                            if kind == "gat":
                                free(f)
                                last = products(f, PASSES, s == 0, s == T - 1)
                            else:
                                last = products(f, PASSES[2:3], False, s == T - 1)
                            if s == T - 1:
                                last.then_inc(agg_mm, 1)
                        if s == T - 1:
                            pe.wait_ge(agg_mm, n["f1"] + c * fb + fb)
                            pe.sem_inc(tile_used, 1)
                        else:
                            last.then_inc(tile_used, 1)

                chunk(0, True)
                other_chunks(pe, fb, lambda c: chunk(c, False))

            def along(n, kind, layer, following, eps):
                banks_free(n)

                low = low_passes() if kind == "gcn" else None

                def chunk(c, bank, hook):
                    t0 = n["tile"] + c * T
                    for s in range(T):
                        pe.wait_ge(p_high, t0 + s + 1)
                        pe.wait_ge(p_low, t0 + s + 1 + RING)

                        def products(passes, start, stop):
                            for r in range(2):
                                for m, (a, b) in enumerate(passes):
                                    for j, w in enumerate((HALF, HALF + 2)):
                                        last = pe.matmul(ps[:P, bank + 2 * r + j, 0:w],
                                                         (p_hi, p_lo)[a][:, s % RING, r * P:(r + 1) * P],
                                                         h_view((h_hi, h_lo)[b], D)[:, s, j * HALF:j * HALF + w],
                                                         start=(start and m == 0), stop=(stop and m == len(passes) - 1))
                            return last

                        if kind == "gat":
                            last = products(PASSES, s == 0, s == T - 1)
                        else:
                            products(PASSES[0:1], s == 0, False)
                            with pe.If(low > 0):
                                products(PASSES[2:3], False, False)
                            last = products(PASSES[1:2], False, s == T - 1)
                        last.then_inc(tile_used, 1)
                        hook(s)
                    pe.wait_ge(tile_used, t0 + T + RING)
                    pe.sem_inc(agg2_mm, 1)

                def turned(c, bank):
                    for r in range(2):
                        pe.wait_ge(y_ready, 2 * (n["c2"] + c) + r + 1)
                        turn(n["y"] + 2 * c + r, r, bank)

                def banks_used(c):
                    pe.wait_ge(agg2_read, 2 * (n["c2"] + c - 1))
                    if layer < 3:
                        pe.wait_ge(xt_ready, n["y"] + 2 * (c - 1) + 2)

                chunk(0, 0, lambda s: None)
                with pe.Fori(0, NC2 // 2) as i:
                    for k, bank in ((1, 4), (2, 0)):
                        banks_used(2 * i + k)
                        chunk(2 * i + k, bank, lambda s: turned(2 * i + k - 1, 4 - bank) if s == TURN_AT and layer < 3 else None)
                if layer < 3:
                    turned(NC2 - 1, 0)

            def none(*_):
                pass

            program(pe, Stages(graph, turn_input, head_scores, none, product_sum, scores, product, columns, across, along, fold,
                               degree_row))


_INS = ['x', 'src', 'dst', 'L0_gnn_W1', 'L0_gnn_a1_src', 'L0_gnn_a1_dst', 'L0_gnn_b1', 'L0_gnn_W2', 'L0_gnn_a2_src',
        'L0_gnn_a2_dst', 'L0_gnn_b2', 'L1_gnn_W', 'L1_gnn_b', 'L2_gnn_W1', 'L2_gnn_att_src1', 'L2_gnn_att_dst1',
        'L2_gnn_b1', 'L2_gnn_W2', 'L2_gnn_att_src2', 'L2_gnn_att_dst2', 'L2_gnn_b2', 'L3_gnn_W1', 'L3_gnn_b1',
        'L3_gnn_W2', 'L3_gnn_b2']
_OUTS = [((N, D), 'float32')]


def kernel(**inputs):
    import numpy as _np
    import concourse.bacc as _bacc
    from concourse import mybir as _mybir
    from concourse.bass_utils import run_bass_kernel_spmd as _run

    nc = _bacc.Bacc("TRN2", target_bir_lowering=False, num_devices=1)
    arrays, args = {}, []
    for name in _INS:
        a = _np.ascontiguousarray(inputs[name])
        arrays[f"in_{name}_dram"] = a
        args.append(nc.dram_tensor(f"in_{name}_dram", a.shape, _mybir.dt.from_np(a.dtype), kind="ExternalInput").ap())
    for i, (shape, dtype) in enumerate(_OUTS):
        dt = _mybir.dt.from_np(_np.dtype(dtype))
        args.append(nc.dram_tensor(f"out_{i}_dram", shape, dt, kind="ExternalOutput").ap())
    build(nc, *args)
    r = _run(nc, [arrays], core_ids=[0])
    return r.results[0]["out_0_dram"]
```

```python
from collections import namedtuple
from contextlib import ExitStack

import concourse.bass as bass
from concourse import mybir

F32, F32R, BF16, F16 = mybir.dt.float32, mybir.dt.float32r, mybir.dt.bfloat16, mybir.dt.float16
I32, I16 = mybir.dt.int32, mybir.dt.int16
ALU = mybir.AluOpType
ACT = mybir.ActivationFunctionType
AX = mybir.AxisListType
ds = bass.ds

N, D, E = 1250, 768, 20000
HEADS, HID = 4, 512
P = 125
T = N // P
KD = D // 128
KH = HID // 128
HALF = D // 2
HW = D + 2
TW, TS = 418, 416
NC1 = 3
BW = 2 * P
NC2 = T // 2
RING = 5
SLOPE = 0.2
EPS = 1e-5
EXACT = 4096.0
NONE = -1e30

EC = E // P
PER = EC // T
SLACK = 2
WIN = PER + 2 * SLACK
ECP = (EC + 2 * SLACK + 4) // 5 * 5
OH = 5
W1_PIECES = 3
ZEROED = 16 * (T // 2)
ROWS = 4
SPLIT_AT = 2
TURN_AT = 8


def late(kind):
    return 2 if kind == "gat" else 0


def chunk_ends(kind):
    return RING - 2 + late(kind)


GRAPH_STEPS = 3 + 2 + 2 + 2 + 4 + T + 2

Stages = namedtuple("Stages", "graph turn_input head_scores product_sum product columns across along fold")

assert NC2 % 2 == 1 and T % 2 == 0 and T % RING == 0 and WIN % OH == 0 and ECP % OH == 0
assert TS * (NC1 - 1) + TW == N and EC * P == E and EC % 2 == 0 and PER * T == EC


def build(nc, x, src, dst, L0_W1, L0_a1s, L0_a1d, L0_b1, L0_W2, L0_a2s, L0_a2d, L0_b2, L1_W, L1_b,
          L2_W1, L2_a1s, L2_a1d, L2_b1, L2_W2, L2_a2s, L2_a2d, L2_b2, L3_W1, L3_b1, L3_W2, L3_b2, out):
    counts_dram = nc.dram_tensor("counts_dram", (T, P, N), I16, kind="Internal").ap()
    masks_dram = nc.dram_tensor("masks_dram", (T, P, N), BF16, kind="Internal").ap()
    heads_dram = nc.dram_tensor("heads_dram", (T, P, D), F32, kind="Internal").ap()
    y_dram = [nc.dram_tensor(f"y{n}_dram", (T, P, D), F32, kind="Internal").ap() for n in range(3)]
    x_blocks = x.rearrange("(t p) f -> t p f", p=P)
    out_blocks = out.rearrange("(t p) f -> t p f", p=P)

    with ExitStack() as ctx:
        place = [0]

        def at(name, shape, dt, offset=None):
            size = mybir.dt.size(dt)
            for n in shape[1:]:
                size *= n
            if offset is None:
                offset = place[0]
                place[0] += (size + 31) // 32 * 32
            return nc.alloc_sbuf_tensor_at(name, shape, dt, offset=offset)

        base0 = nc.sbuf_base
        place[0] = (base0 + 31) // 32 * 32

        def sem(name):
            return ctx.enter_context(nc.semaphore(name))

        XT = at("XT", [128, KD, N], F32)
        ys_hi = at("ys_hi", [128, 2, KD, P], F32R)
        ys_lo = at("ys_lo", [128, 2, KD, P], F32R)
        h_at = place[0]
        h_hi = at("h_hi", [P, T * HW], F32R)
        h_lo_at = place[0]
        h_lo = at("h_lo", [P, T * HW], F32R)
        w_at = place[0]
        w_hi = at("w_hi", [128, KD * D], F32R)
        w_lo = at("w_lo", [128, KD * D], F32R)
        p_hi = at("p_hi", [P, RING, TW], F32R)
        p_lo = at("p_lo", [P, RING, TW], F32R)
        x_row = at("x_row", [128, N], F32)
        y_row = at("y_row", [P, N], F32)
        tb_at = place[0]
        tb = at("tb", [P, RING, TW], F32)
        c_in = at("c_in", [P, RING, TW], I16)
        acc = at("acc", [P, TW], F32)
        r_row = at("r_row", [128, TW], F32)
        ws = at("ws", [128, 2, D], F32)
        ev = at("ev", [128, 4, D], F32)
        bias_at = place[0]
        bias_row = at("bias_row", [P, D], F32)
        a_at = place[0]
        a_row = at("a_row", [128, 2, D], F32)
        ident = at("ident", [128, 128], F32)
        ones = at("ones", [P, 1], F32)
        wa = at("wa", [128, KD, 2], F32)
        score = at("score", [P, T, 2], F32)
        score_sum = at("score_sum", [P, T, 2], F32)
        s08 = at("s08", [P, T], F32)
        s02 = at("s02", [P, T], F32)
        pair_max = at("pair_max", [P, 2], F32)
        amax = at("amax", [P, T], F32)
        mcol = at("mcol", [P, T], F32)
        xcol = at("xcol", [P, T], F32)
        ycol = at("ycol", [P, T], F32)
        deg = at("deg", [P, T], F32)
        dinv = at("dinv", [P, T], F32)
        b_col = at("b_col", [128, HEADS * KH + 2 * KD], F32)
        rden = at("rden", [P, 2, 2], F32)
        stats = at("stats", [P, 2, 2, 6], F32)
        mv = at("mv", [P, 2, 2], F32)
        rstd = at("rstd", [P, 2], F32)
        eps_col = at("eps_col", [P, 1], F32)
        params = at("params", [1, 4], I32)
        assert place[0] <= nc.sbuf_usable_end, (place[0], nc.sbuf_usable_end)

        w2 = [at(f"w2_{part}", [128, KH, HW], F32R, offset=w_at + i * KH * HW * 4) for i, part in enumerate(("hi", "lo"))]
        w1 = [at(f"w1_{part}", [128, KD * HID], F32R, offset=w_at + 2 * KH * HW * 4 + i * KD * HID * 4)
              for i, part in enumerate(("hi", "lo"))]
        assert 2 * KH * HW + 2 * KD * HID <= 2 * KD * D + 2 * RING * TW
        masks_all = at("masks_all", [P, T, N], BF16, offset=w_at + 2 * KH * HW * 4)
        assert 2 * KH * HW + T * N // 2 <= 2 * KD * D + 2 * RING * TW
        w1_rows = at("w1_rows", [128, ROWS, HEADS * HID], F32, offset=w_at)
        a1_row = at("a1_row", [128, 2 * HEADS, HID], F32, offset=w_at + ROWS * HEADS * HID * 4)
        assert (ROWS + 2) * HEADS * HID <= 2 * KD * D + 2 * RING * TW
        wa8 = at("wa8", [128, KD, 2 * HEADS], F32, offset=h_at + 2 * T * HW * 4 - KD * 2 * HEADS * 4)
        score8 = at("score8", [P, T, 2 * HEADS], F32, offset=bias_at)
        srow = at("srow", [2 * HEADS, N], F32, offset=a_at)
        w1_in = at("w1_in", [128, KD * HID], F32, offset=h_at)
        add = at("add", [P, 2, D], F32, offset=h_at + KD * HID * 4)
        assert KD * HID + 2 * D <= T * HID
        ev_flat = ev[:].rearrange("p a f -> p (a f)")

        def z_tile(f):
            return ev_flat[:, f * TW:(f + 1) * TW]

        def e_tile(f):
            return z_tile(KH + f) if f < KH - 1 else r_row[:]

        ot = [at(f"ot{i}", [128, KH // 2, N], F32, offset=o + T * HID * 4) for i, o in enumerate((h_at, h_lo_at))]
        junk = at("junk", [P, N], BF16, offset=tb_at)
        mask_in = [at(f"mask_in{i}", [P, N], BF16, offset=tb_at + 2528 * (i + 1)) for i in range(2)]
        g = [h_at]

        def graph(name, shape, dt):
            size = mybir.dt.size(dt)
            for n in shape[1:]:
                size *= n
            g[0] += (size + 31) // 32 * 32
            return at(name, shape, dt, offset=g[0] - (size + 31) // 32 * 32)

        iota_i = graph("iota_i", [P, N], I32)
        iota = graph("iota", [P, N], F16)
        oh_src = graph("oh_src", [P, OH, N], BF16)
        oh_dst = graph("oh_dst", [P, OH, P], BF16)
        ct = graph("ct", [P, 2, N], F32)
        c_out = graph("c_out", [P, T, P], I16)
        m_out = graph("m_out", [P, N], BF16)
        e_int = graph("e_int", [EC // 2, 2, BW], I32)
        e_flt = graph("e_flt", [EC // 2, 2, BW], F32)
        src_col = graph("src_col", [P, ECP], F32)
        dst_col = graph("dst_col", [P, ECP], F32)
        lim_i = graph("lim_i", [P, 2, 12 * PER], I32)
        lim = graph("lim", [P, 2, 12 * PER], F32)
        out_of = graph("out_of", [P, 2, EC], F32)
        bad = graph("bad", [P, 1], F32)
        many = graph("many", [P, T], F32)
        many_any = graph("many_any", [P, 1], F32)
        par_f = graph("par_f", [1, 4], F32)
        zeros = graph("zeros", [P, D], F32)
        assert g[0] <= h_at + 2 * T * HW * 4 - KD * 2 * HEADS * 4

        ps = ctx.enter_context(nc.psum_tensor("ps", [128, 8, 512], F32))

        edges_in, graph_const, graph_step = sem("edges_in"), sem("graph_const"), sem("graph_step")
        edges_flt, edges_turned, edges_col = sem("edges_flt"), sem("edges_turned"), sem("edges_col")
        bad_ready, bad_summed, par_ready = sem("bad_ready"), sem("bad_summed"), sem("par_ready")
        oh_ready, oh_used, ct_summed, ct_out = sem("oh_ready"), sem("oh_used"), sem("ct_summed"), sem("ct_out")
        ct_loop, ct_deg, ct_turned, c_ready = sem("ct_loop"), sem("ct_deg"), sem("ct_turned"), sem("c_ready")
        m_ready, c_stored, m_stored = sem("m_ready"), sem("c_stored"), sem("m_stored")
        many_ready, many_summed, low_ready = sem("many_ready"), sem("many_summed"), sem("low_ready")
        root, dinv_ready = sem("root"), sem("dinv_ready")
        held = sem("held")
        x_in = [sem(f"x_in{i}") for i in range(4)]
        y_ready, y_turned, xt_ready = sem("y_ready"), sem("y_turned"), sem("xt_ready")
        w_in = [sem(f"w_in{i}") for i in range(2)]
        a_in, w_high, w_low, w_dot = sem("a_in"), sem("w_high"), sem("w_low"), sem("w_dot")
        split_high, split_low, gemm_done = sem("split_high"), sem("split_low"), sem("gemm_done")
        gemm_act, gemm_dve = sem("gemm_act"), sem("gemm_dve")
        fold_high, fold_low = sem("fold_high"), sem("fold_low")
        sum_in, sum_added = [sem(f"sum_in{i}") for i in range(4)], [sem(f"sum_added{i}") for i in range(2)]
        a1_in, rows_in, head_dot = sem("a1_in"), [sem(f"rows_in{i}") for i in range(ROWS)], sem("head_dot")
        rows_more = [sem(f"rows_more{i}") for i in range(KD - ROWS)]
        w1_ld, w1_high, w1_low = sem("w1_ld"), sem("w1_high"), sem("w1_low")
        wa_high, wa_low, summed = sem("wa_high"), sem("wa_low"), sem("summed")
        ones_set = sem("ones_set")
        score_mm, score_ready, row_mm, row_ready = sem("score_mm"), sem("score_ready"), sem("row_mm"), sem("row_ready")
        srow_mm, srow_out = sem("srow_mm"), sem("srow_out")
        masks_in = sem("masks_in")
        mask_ld = [sem(f"mask_ld{i}") for i in range(2)]
        maxed, step, xy_ready, amax_ready = sem("maxed"), sem("step"), sem("xy_ready"), sem("amax_ready")
        c_ld = [sem(f"c_ld{i}") for i in range(RING)]
        t_ready, e_ready, p_ready = sem("t_ready"), sem("e_ready"), sem("p_ready")
        p_high, p_low, tile_used, acc_done = sem("p_high"), sem("p_low"), sem("tile_used"), sem("acc_done")
        den_mm, r_ready, agg_mm = sem("den_mm"), sem("r_ready"), sem("agg_mm")
        ev_scaled, ev_act, ev_exp, ev_done = sem("ev_scaled"), sem("ev_act"), sem("ev_exp"), sem("ev_done")
        b_in = sem("b_in")
        agg2_mm, agg2_read, res_in, res_ready = sem("agg2_mm"), sem("agg2_read"), [sem(f"res_in{i}") for i in range(2)], sem("res_ready")
        bias_in, var_ready, std_ready, ln_step = sem("bias_in"), sem("var_ready"), sem("std_ready"), sem("ln_step")
        stored = [sem(f"stored{i}") for i in range(2)]

        START = dict(wp=0, dot=0, av=0, q=T, sp=0, sc=1, rows=3, mp=T // 2, step=GRAPH_STEPS + 6, xy=1, tile=0, gat=0,
                     acc=0, c1=0, f1=0, den=0, elu=0, c2=0, y=T, ln=0, chunks=0, ml=T // 2)
        HEAD = dict(wp=KH // 2, dot=KH, av=1, q=2 * T, sp=T // 2, sc=0, rows=3, mp=T // 2,
                    step=6 + NC1, xy=1, tile=T * NC1, gat=T * NC1, acc=T * NC1, c1=NC1, f1=KH * NC1, den=NC1,
                    elu=KH * NC1, c2=0, y=0, ln=0, chunks=NC1, ml=T // 2)

        def in_head(hd):
            return {k: START[k] + HEAD[k] * hd for k in START}

        def after_heads():
            n = {k: START[k] + HEAD[k] * HEADS for k in START}
            return dict(n, q=n["q"] - T, rows=n["rows"] - 3, mp=n["mp"] - T // 2, ml=n["ml"] - T // 2, step=n["step"] - 6, xy=n["xy"] - 1)

        def input_begun(eng, n):
            eng.wait_ge(xt_ready, n["y"])
            if isinstance(n["f1"], int) and n["f1"]:
                eng.wait_ge(ev_done, n["f1"] - KD + 2)

        def input_whole(eng, n):
            eng.wait_ge(xt_ready, n["y"] + 2)
            eng.wait_ge(ev_done, n["f1"] + 2)

        def weights_of(name, hd=None):
            if name == "L0_W2":
                return KH, D, lambda k: L0_W2[ds(hd * HID + k * 128, 128), :]
            w = {"L1_W": L1_W, "L2_W1": L2_W1, "L2_W2": L2_W2, "L3_W1": L3_W1, "L3_W2": L3_W2}[name]
            return KD, D, lambda k: w[k * 128:(k + 1) * 128, :]

        def vectors_of(name, hd=None):
            if name == "L0_W2":
                return L0_a2s, L0_a2d
            if name == "L2_W1":
                return L2_a1s.rearrange("(a f) -> a f", a=1), L2_a1d.rearrange("(a f) -> a f", a=1)
            if name == "L2_W2":
                return L2_a2s.rearrange("(a f) -> a f", a=1), L2_a2d.rearrange("(a f) -> a f", a=1)
            return None

        def sources(kb):
            return [(XT, 0)] if kb == KD else [(ot[0], 0), (ot[1], KH // 2)]

        def source_block(kb, k, cols):
            return XT[:, k, cols] if kb == KD else ot[k // (KH // 2)][:, k % (KH // 2), cols]

        def h_view(h, width):
            return (h[:, 0:T * HID].rearrange("p (t f) -> p t f", f=HID) if width == HID
                    else h[:].rearrange("p (t f) -> p t f", f=HW))

        def h_block(h, width, t):
            v = h_view(h, width)[:, ds(t, 1), 0:width]
            return (v.rearrange("p t f -> p (t f)") if width == HID
                    else v.rearrange("p t (b f) -> p (t b) f", b=2))

        def ps_block(bank, width):
            return ps[:P, bank, 0:HID] if width == HID else ps[:P, bank:bank + 2, 0:HALF]

        def halves(tile):
            return tile.rearrange("p (b f) -> p b f", b=2)

        def w_place(i, name, k):
            return w2[i][:, k, 0:D] if name == "L0_W2" else (w_hi, w_lo)[i][:, k * D:(k + 1) * D]

        def in_segments(eng, pair, last, hooks):
            at_ = 0
            for stop in [k for k in sorted(hooks) if k < last] + [last]:
                if stop - at_ == 1:
                    pair(at_)
                else:
                    with eng.Fori(at_, stop) as i:
                        pair(i)
                if stop in hooks:
                    hooks[stop]()
                at_ = stop

        def blocks_ahead(eng, prepare, finish, started=lambda: None, hooks={}, beside=None, begun=False, then=None):
            if not begun:
                prepare(0, 0)
                prepare(1, 1)
            started()
            first, last, fn = beside or (0, 0, None)

            def pair(i, beside):
                for r in range(2):
                    finish(2 * i + r, r, i)
                    if beside:
                        fn(2 * i + r - 2 * first)
                    prepare(2 * i + r + 2, r)

            at_ = 0
            for stop in sorted({k for k in (first, last, *hooks, T // 2 - 1) if 0 < k <= T // 2 - 1}):
                if stop - at_ == 1:
                    pair(at_, first <= at_ < last)
                else:
                    with eng.Fori(at_, stop) as i:
                        pair(i, first <= at_ < last)
                if stop in hooks:
                    hooks[stop]()
                at_ = stop
            for r in range(2):
                finish(T - 2 + r, r, T // 2 - 1)
                if then is not None:
                    then(r, r)

        def graph_blocks(eng, block):
            block(0, 0, False)
            with eng.Fori(0, T // 2 - 1) as i:
                block(2 * i + 1, 1, True)
                block(2 * i + 2, 0, True)
            block(T - 1, 1, True)

        def product_bank(r, with_rows):
            return 2 * r if with_rows else 6 - 2 * r

        def chunk_width(c):
            return TS if c < NC1 - 1 else TW

        def node_chunk(c):
            return slice(c * TS, c * TS + chunk_width(c))

        def first_bank(fb, c):
            return 4 * (c % 2) if fb == KH else 0

        def sum_bank(fb, c):
            return first_bank(fb, c + 1) + KH - 1 if fb == KH else 7

        def other_chunks(eng, fb, chunk):
            if fb == KH:
                for c in range(1, NC1):
                    chunk(c)
            else:
                with eng.Fori(1, NC1) as c:
                    chunk(c)

        def program(eng, do):
            do.graph()
            do.turn_input()
            do.head_scores()
            n = dict(START, q=0, sc=0, rows=0, mp=0, ml=0, step=GRAPH_STEPS, xy=0)
            do.product(n, KD, HID, "scores", None, 0, None)

            def head(hd, more):
                n = in_head(hd)
                do.across(n, "gat", KH, "elu", hd * KH, ("L0_W2", hd), 1e-16)
                before = n
                n = dict(n, wp=n["wp"] + KH // 2, dot=n["dot"] + KH, av=n["av"] + 1, chunks=n["chunks"] + NC1, tile=n["tile"] + T * NC1,
                         gat=n["gat"] + T * NC1, acc=n["acc"] + T * NC1, c1=n["c1"] + NC1, den=n["den"] + NC1,
                         f1=n["f1"] + KH * NC1, elu=n["elu"] + KH * NC1, step=n["step"] + NC1)
                do.product_sum(before, n, hd, more)
                if more:
                    n = dict(n, q=n["q"] + T, rows=n["rows"] + 1, mp=n["mp"] + T // 2, ml=n["ml"] + T // 2, xy=n["xy"] + 1,
                             step=n["step"] + 6, sp=n["sp"] + T // 2)
                    do.product(n, KD, HID, "rows", None, hd + 1, None)

            with eng.Fori(0, HEADS - 1) as hd:
                head(hd, True)
            head(HEADS - 1, False)
            n = after_heads()
            do.fold(n)
            n = dict(n, mp=n["mp"] + T // 2, step=n["step"] + 3, rows=n["rows"] + 1)
            do.columns(n)
            n = dict(n, xy=n["xy"] + 1, rows=n["rows"] + 2, step=n["step"] + 3)
            rest = do.along(n, "gat", 0, ("L1_W", None), 1e-16)
            n = after_along(n, "gat", "L1_W", 1e-16)

            do.product(n, KD, D, None, dinv, None, rest)
            n = dict(n, q=n["q"] + T)
            rest = do.along(n, "gcn", 1, ("L2_W1", None), 0.0)
            n = after_along(n, "gcn", "L2_W1", 0.0)

            do.product(n, KD, D, "scores", None, None, rest)
            n = after_scores(n)
            rest = do.across(n, "gat", KD, "relu", HEADS * KH, ("L2_W2", None), 0.0)
            n = dict(n, wp=n["wp"] + KD // 2, dot=n["dot"] + KD, av=n["av"] + 1, chunks=n["chunks"] + NC1, tile=n["tile"] + T * NC1,
                     gat=n["gat"] + T * NC1, acc=n["acc"] + T * NC1, c1=n["c1"] + NC1, den=n["den"] + NC1,
                     f1=n["f1"] + KD * NC1)
            do.product(n, KD, D, "scores", None, None, rest)
            n = after_scores(n)
            rest = do.along(n, "gat", 2, ("L3_W1", None), 0.0)
            n = after_along(n, "gat", "L3_W1", 0.0)

            do.product(n, KD, D, "degree", dinv, None, rest)
            n = dict(n, q=n["q"] + T, rows=n["rows"] + 1)
            rest = do.across(n, "gcn", KD, "relu", HEADS * KH + KD, ("L3_W2", None), 0.0)
            n = dict(n, wp=n["wp"] + KD // 2, chunks=n["chunks"] + NC1, tile=n["tile"] + T * NC1, c1=n["c1"] + NC1, f1=n["f1"] + KD * NC1)
            do.product(n, KD, D, None, dinv, None, rest)
            n = dict(n, q=n["q"] + T)
            do.along(n, "gcn", 3, None, 0.0)

        def after_scores(n):
            return dict(n, q=n["q"] + T, sc=n["sc"] + 1, rows=n["rows"] + 3, mp=n["mp"] + T // 2, ml=n["ml"] + T // 2, xy=n["xy"] + 1,
                        step=n["step"] + 5)

        def ln_links(kind, eps):
            return (0 if kind == "gcn" else 4 if eps else 2) + 5

        def after_along(n, kind, following, eps):
            n = dict(n, chunks=n["chunks"] + NC2, tile=n["tile"] + T * NC2, c2=n["c2"] + NC2, y=n["y"] + T, wp=n["wp"] + KD // 2,
                     ln=n["ln"] + NC2 * ln_links(kind, eps))
            if kind == "gat":
                n["gat"] += T * NC2
            if vectors_of(following) is not None:
                n = dict(n, dot=n["dot"] + KD, av=n["av"] + 1)
            return n

        C_T = counts_dram.rearrange("t p n -> p t n")
        PASSES = ((0, 0), (0, 1), (1, 0))

        def hold(eng, semaphore, value):
            eng.wait_ge(semaphore, value)
            eng.sem_inc(held, 1)

        block = ctx.enter_context(nc.Block())

        @block.sync
        def _(sp):
            sp.sem_inc(c_stored, 1)

            def load_x(t):
                sp.dma_start(ev[:P, t % 4, :], x_blocks[t]).then_inc(x_in[t % 4], 16)

            def graph():
                for i, e in enumerate((src, dst)):
                    sp.dma_start(e_int[:, i, :], e.rearrange("(q c) -> q c", c=BW)).then_inc(edges_in, 16)
                for i, (b, o, k) in enumerate(((L0_b1, 0, HEADS * KH), (L2_b1, HEADS * KH, KD),
                                               (L3_b1, HEADS * KH + KD, KD))):
                    sp.dma_start(b_col[:, o:o + k], b.rearrange("(k p) -> p k", p=128),
                                 allow_slow_non_contiguous=True).then_inc(b_in, 16)
                for j, a in enumerate((L0_a1s, L0_a1d)):
                    sp.dma_start(a1_row[:, j * HEADS:(j + 1) * HEADS, :].rearrange("p h f -> p (h f)"),
                                 a.rearrange("(a h) f -> a (h f)", a=1).broadcast_to([128, HEADS * HID])).then_inc(a1_in, 16)
                for k in range(ROWS):
                    sp.dma_start(w1_rows[:, k, :], L0_W1[k * 128:(k + 1) * 128, :]).then_inc(rows_in[k], 16)
                for t in range(4):
                    load_x(t)
                with sp.Fori(0, T) as b:
                    hold(sp, m_ready, b + 1)
                    sp.dma_start(masks_dram[ds(b, 1)].rearrange("b p n -> (b p) n"), m_out[:]).then_inc(m_stored, 16)
                    hold(sp, c_ready, b + 1 + 1)
                    sp.dma_start(C_T[:, :, ds(b * P, P)], c_out[:]).then_inc(c_stored, 16)

            def turn_input():
                for t in range(4, T):
                    sp.wait_ge(xt_ready, t - 4 + 3)
                    load_x(t)
                sp.wait_ge(c_stored, 16 * T + 1)
                sp.wait_ge(m_stored, 16 * T)

            def load_w1(n, hd):
                sp.dma_start(w1_in[:].rearrange("p (k f) -> p k f", f=HID),
                             L0_W1[:, ds(hd * HID, HID)].rearrange("(k p) f -> p k f", p=128)).then_inc(w1_ld, 16)

            def head_scores():
                sp.wait_ge(dinv_ready, 1)
                load_w1(START, 0)

            def masks(n):
                with sp.Fori(0, T // 2) as i:
                    for r in range(2):
                        mask(n, i, r)

            def product_sum(before, n, hd, more):
                if more:
                    hold(sp, tile_used, n["tile"] + RING)
                    load_w1(n, hd + 1)
                    masks_free(n)
                    masks(n)
                else:
                    sp.wait_ge(tile_used, n["tile"] + RING)
                    sp.wait_ge(p_low, n["tile"] + RING)
                    sp.dma_start(masks_all[:], masks_dram.rearrange("t p n -> p t n")).then_inc(masks_in, 16)

            def vectors(n, name, hd):
                hold(sp, w_dot, 2 * n["dot"] + 4)
                hold(sp, score_ready, n["sc"])
                hold(sp, row_ready, n["rows"])
                for j, a in enumerate(vectors_of(name, hd)):
                    width = a.shape[1]
                    sp.dma_start(a_row[:, j, 0:width], a.broadcast_to([128, width])).then_inc(a_in, 16)

            def piece(n, name, hd, k):
                kb, width, rows = weights_of(name, hd)
                if k == 0 and vectors_of(name, hd) is not None:
                    vectors(n, name, hd)
                hold(sp, w_low, 2 * n["wp"] + k + 1)
                hold(sp, w_dot, 2 * n["dot"] + (4 if vectors_of(name, hd) is None else 2 * k + 2))
                sp.dma_start(ws[:, k % 2, 0:width], rows(k)).then_inc(w_in[k % 2], 16)

            def masks_free(n):
                hold(sp, p_low, n["tile"] + RING)
                hold(sp, acc_done, n["acc"] + RING)

            def mask(n, i, r):
                hold(sp, maxed, 2 * n["mp"] + 2 * i + r + 1)
                sp.dma_start(mask_in[r][:], masks_dram[ds(2 * i + r, 1)].rearrange("t p n -> (t p) n")
                             ).then_inc(mask_ld[r], 16)

            def product(n, kb, width, beside, scale, hd, rest):
                if beside == "scores":
                    masks_free(n)
                    masks(n)

            def fold(n):
                for r in range(2):
                    sp.wait_ge(sum_added[r], 16 * n["sp"] + ZEROED)
                sp.wait_ge(ev_done, n["f1"] + 2)
                for t in range(T):
                    if t >= 4:
                        sp.wait_ge(fold_low, t - 4 + 3)
                    sp.dma_start(ev[:P, t % 4, :], heads_dram[t]).then_inc(sum_in[t % 4], 16)

            def counts(n, c, cstat, width, off, hook):
                tile = n["tile"] + c * T
                for s in range(T):
                    hold(sp, p_low, tile + s + 1)
                    sp.dma_start(c_in[:, s % RING, 0:width], counts_dram[s][:, ds(off, width)]
                                 ).then_inc(c_ld[s % RING], 16)
                    hook(s)

            def hook_weights(n, following):
                def hook(s):
                    if following is not None and 0 <= s - SPLIT_AT < weights_of(*following)[0]:
                        piece(n, *following, s - SPLIT_AT)
                return hook

            def across(n, kind, fb, act, bias, following, eps):
                counts(n, 0, 0, TW, 0, hook_weights(n, following))
                with sp.Fori(1, NC1) as c:
                    counts(n, c, 1, TW, c * TS, lambda s: None)

            def along(n, kind, layer, following, eps):
                hold(sp, ev_done, n["f1"] + 2)
                sp.wait_ge(fold_low, T + 2)
                if layer:
                    for r in range(2):
                        hold(sp, stored[r], 16 * n["c2"] + 16)
                res = x_blocks if layer == 0 else y_dram[layer - 1]
                hold(sp, res_ready, 2 * n["c2"])
                last_bias = (L0_b2, L1_b, L2_b2, L3_b2)[layer]
                sp.dma_start(bias_row[:], last_bias.rearrange("(a f) -> a f", a=1).broadcast_to([P, D])
                             ).then_inc(bias_in, 16)

                def residual(c):
                    for r in range(2):
                        hold(sp, agg2_read, 2 * n["c2"] + 2 * c + 1)
                        sp.dma_start(ev[:P, 2 + r, :], res[ds(2 * c + r, 1)].rearrange("t p f -> (t p) f")
                                     ).then_inc(res_in[r], 16)

                residual(0)
                counts(n, 0, 0, BW, 0, hook_weights(n, following))
                with sp.Fori(1, NC2) as c:
                    counts(n, c, 1, BW, c * BW, lambda s: residual(c) if s == 8 else None)

            def none(*_):
                pass

            program(sp, Stages(graph, turn_input, head_scores, product_sum, product, none, across, along, fold))

        @block.gpsimd
        def _(pool):
            pool.sem_inc(w_low, 2)
            pool.sem_inc(fold_low, 2)
            pool.sem_inc(acc_done, RING)

            def graph():
                nc.gpsimd.memset(ident[:], 0.0).then_inc(graph_step, 1)
                nc.gpsimd.memset(ones[:], 1.0).then_inc(graph_step, 1)
                pool.wait_ge(graph_step, 2)
                nc.gpsimd.affine_select(out=ident[:], in_=ident[:], compare_op=ALU.not_equal, fill=1.0, base=0,
                                        pattern=[[-1, 128]], channel_multiplier=1).then_inc(graph_const, 1)
                nc.gpsimd.memset(zeros[:], 0.0).then_inc(graph_const, 1)
                nc.gpsimd.iota(iota_i[:], pattern=[[1, N]], base=0, channel_multiplier=0).then_inc(graph_const, 1)
                nc.gpsimd.iota(lim_i[:, 0, :], pattern=[[P, 12], [0, PER]], base=-P,
                               channel_multiplier=0).then_inc(graph_const, 1)
                nc.gpsimd.iota(lim_i[:, 1, :], pattern=[[P, 12], [0, PER]], base=P,
                               channel_multiplier=0).then_inc(graph_const, 1)
                pool.wait_ge(graph_const, 2)
                for t in range(T):
                    pool.dma_start(heads_dram[t], zeros[:]).then_inc(sum_added[t % 2], 16)
                for r in range(2):
                    pool.dma_start(y_dram[0][r], zeros[:]).then_inc(stored[r], 16)

                def block(b, r, _):
                    hold(pool, ct_out, b + 1)
                    diagonal = ct[:, r, ds(b * P, P)]
                    nc.gpsimd.tensor_tensor(diagonal, diagonal, ident[:P, :P], ALU.add).then_inc(ct_loop, 1)
                    hold(pool, ct_loop, b + 1)
                    if not isinstance(b, int) or b:
                        hold(pool, m_stored, 16 * b)
                    nc.gpsimd.tensor_scalar(m_out[:], ct[:, r, :], 0.0, NONE, ALU.is_equal, ALU.mult).then_inc(m_ready, 1)

                graph_blocks(pool, block)

            def piece(n, name, hd, k):
                pool.wait_ge(w_high, 2 * n["wp"] + k + 1)
                nc.gpsimd.tensor_tensor(w_place(1, name, k), ws[:, k % 2, :], w_place(0, name, k).bitcast(F32),
                                        ALU.subtract).then_inc(w_low, 1)
                if name == "L0_W2" and k == KH - 1:
                    pool.wait_ge(wa_high, n["av"] + 1)
                    nc.gpsimd.tensor_tensor(w2[1][:, :, D:HW], wa[:, 0:KH, :], w2[0][:, :, D:HW].bitcast(F32),
                                            ALU.subtract).then_inc(wa_low, 1)

            def split_w1(hd):
                for k in range(W1_PIECES):
                    cols = slice(k * KD * HID // W1_PIECES, (k + 1) * KD * HID // W1_PIECES)
                    pool.wait_ge(w1_high, W1_PIECES * hd + k + 1)
                    nc.gpsimd.tensor_tensor(w1[1][:, cols], w1_in[:, cols], w1[0][:, cols].bitcast(F32),
                                            ALU.subtract).then_inc(w1_low, 1)

            def head_scores():
                for k in range(ROWS, KD):
                    pool.wait_ge(head_dot, 2 * HEADS * (k - ROWS + 1))
                    pool.dma_start(w1_rows[:, k % ROWS, :], L0_W1[k * 128:(k + 1) * 128, :]).then_inc(rows_more[k - ROWS], 16)
                split_w1(0)

            def product_sum(before, n, hd, more):
                for r in range(2):
                    pool.wait_ge(sum_added[r], ZEROED)

                def pair(i):
                    for r in range(2):
                        q = n["q"] + 2 * i + r
                        pool.wait_ge(gemm_act, q + 3)
                        pool.wait_ge(gemm_dve, q + 3)
                        pool.dma_start(heads_dram[ds(2 * i + r, 1)].rearrange("t p f -> (t p) f"), add[:, r, :],
                                       accum_op=ALU.add).then_inc(sum_added[r], 16)

                in_segments(pool, pair, T // 2, {3: lambda: split_w1(hd + 1)} if more else {})

            def hook_weights(n, following, s):
                if following is not None and 0 <= s - SPLIT_AT < weights_of(*following)[0]:
                    piece(n, *following, s - SPLIT_AT)

            def sum_tiles(n, c, hook):
                g, a = n["gat"] + c * T, n["acc"] + c * T
                for s in range(T):
                    pool.wait_ge(p_ready, g + s + 1)
                    if s == 0:
                        hold(pool, den_mm, n["den"] + c + 1)
                        nc.gpsimd.tensor_copy(acc[:], tb[:, 0, :]).then_inc(acc_done, 1)
                    else:
                        pool.wait_ge(acc_done, a + s + RING)
                        nc.gpsimd.tensor_tensor(acc[:], acc[:], tb[:, s % RING, :], ALU.add).then_inc(acc_done, 1)
                    hook(s)

            def across(n, kind, fb, act, bias, following, eps):
                if kind == "gat":
                    sum_tiles(n, 0, lambda s: hook_weights(n, following, s))
                else:
                    for s in range(T):
                        hook_weights(n, following, s)
                if kind == "gat":
                    with pool.Fori(1, NC1) as c:
                        sum_tiles(n, c, lambda s: None)

            def along(n, kind, layer, following, eps):
                dest = out_blocks if layer == 3 else y_dram[layer]

                def residual(c):
                    for r in range(2):
                        pool.wait_ge(bias_in, 16 * (layer + 1))
                        pool.wait_ge(res_in[r], 16 * (n["c2"] + c + 1))
                        nc.gpsimd.tensor_tensor(ev[:P, 2 + r, :], ev[:P, 2 + r, :], bias_row[:],
                                                ALU.add).then_inc(res_ready, 1)

                def store(c):
                    for r in range(2):
                        pool.wait_ge(y_ready, 2 * (n["c2"] + c) + r + 1 + 1)
                        pool.dma_start(dest[ds(2 * c + r, 1)].rearrange("t p f -> (t p) f"), ev[:P, r, :]
                                       ).then_inc(stored[r], 16)

                residual(0)
                for s in range(T):
                    hook_weights(n, following, s)
                with pool.Fori(1, NC2) as c:
                    store(c - 1)
                    residual(c)
                store(NC2 - 1)
                if layer == 3:
                    for r in range(2):
                        pool.wait_ge(stored[r], 16 * (n["c2"] + NC2) + 16)

            def fold(n):
                for t in range(T):
                    pool.wait_ge(fold_high, t + 1)
                    nc.gpsimd.tensor_tensor(h_block(h_lo, D, t), halves(ev[:P, t % 4, :]),
                                            h_block(h_hi, D, t).bitcast(F32), ALU.subtract).then_inc(fold_low, 1)

            def none(*_):
                pass

            program(pool, Stages(graph, none, head_scores, product_sum, none, none, across, along, fold))

        @block.scalar
        def _(act):
            act.sem_inc(c_ready, 1)

            def graph():
                def turned_out(b, r):
                    act.wait_ge(ct_turned, b + 1)
                    if not isinstance(b, int) or b:
                        act.wait_ge(c_stored, 16 * b + 1)
                    for j in range(3):
                        k = min(4, T - 4 * j)
                        last = nc.scalar.activation(c_out[:, 4 * j:4 * j + k, :],
                                                    ps[:P, 3 * r + j, 0:k * P].rearrange("p (k q) -> p k q", q=P), ACT.Copy)
                    last.then_inc(c_ready, 1)

                def block(b, r, later):
                    if later:
                        turned_out(b - 1, 1 - r)
                        act.wait_ge(m_ready, b)
                        act.wait_ge(ct_deg, b)
                    act.wait_ge(ct_summed, b + 1)
                    for j in range(3):
                        o, w = (TW + TS * (j - 1), TS) if j else (0, TW)
                        last = nc.scalar.activation(ct[:, r, o:o + w], ps[:P, 3 * r + j, 0:w], ACT.Copy)
                    last.then_inc(ct_out, 1)

                graph_blocks(act, block)
                turned_out(T - 1, 1)
                act.wait_ge(ct_deg, T)
                nc.scalar.activation(dinv[:], deg[:], ACT.Sqrt).then_inc(root, 1)

            def turned(y, t, r, bank):
                act.wait_ge(y_turned, y + 3)
                for j in range(2):
                    last = nc.scalar.activation(XT[:, 3 * j:3 * j + 3, ds(t * P, P)],
                                                ps[:, bank + 2 * r + j, 0:3 * P].rearrange("p (k q) -> p k q", q=P), ACT.Copy)
                last.then_inc(xt_ready, 1)

            def turn_input():
                with act.Fori(0, T // 2) as i:
                    for r in range(2):
                        turned(2 * i + r, 2 * i + r, r, 4)

            def piece(n, name, hd, k):
                if k == 0:
                    act.wait_ge(gemm_done, n["q"] + 2)
                act.wait_ge(w_in[k % 2], 16 * (n["wp"] + k // 2 + 1))
                nc.scalar.activation(w_place(0, name, k), ws[:, k % 2, :], ACT.Copy).then_inc(w_high, 1)

            def split_w1(hd):
                act.wait_ge(w1_ld, 16 * (hd + 1))
                for k in range(W1_PIECES):
                    cols = slice(k * KD * HID // W1_PIECES, (k + 1) * KD * HID // W1_PIECES)
                    nc.scalar.activation(w1[0][:, cols], w1_in[:, cols], ACT.Copy).then_inc(w1_high, 1)

            def head_scores():
                act.wait_ge(head_dot, 2 * HEADS * KD)
                split_w1(0)

            def product_sum(before, n, hd, more):
                act.wait_ge(ev_done, n["f1"] - KH + 2)

                def finish(t, r, i):
                    act.wait_ge(gemm_done, n["q"] + t + 3)
                    act.wait_ge(sum_added[r], 16 * (n["sp"] + i) + ZEROED)
                    nc.scalar.activation(add[:, r, 0:HALF], ps[:P, 4 + 2 * r, 0:HALF], ACT.Copy).then_inc(gemm_act, 1)

                def next_scores():
                    if more:
                        act.wait_ge(t_ready, n["gat"])
                        row(x_row, P, n, 0, 0)
                        act.sem_inc(held, 1)

                def whole():
                    act.wait_ge(ev_done, n["f1"] + 2)
                    act.sem_inc(held, 1)

                hooks = {1: next_scores, 2: whole}
                if more:
                    hooks[3] = lambda: split_w1(hd + 1)
                blocks_ahead(act, lambda t, r: split_block(n, KH, t, r), finish,
                             lambda: finish_across(before, NC1 - 1, KH, "elu", hd * KH), hooks,
                             then=(lambda t, r: split_block(dict(n, q=n["q"] + T), KD, t, r)) if more else None)

            def row(dest, parts, n, k, bank=5):
                act.wait_ge(row_mm, n["rows"] + k + 1)
                for j in range(3):
                    w = min(4, T - 4 * j) * P
                    last = nc.scalar.activation(dest[:parts, 4 * P * j:4 * P * j + w], ps[:parts, bank + j, 0:w], ACT.Copy)
                last.then_inc(row_ready, 1)

            def split_block(n, kb, t, r):
                act.wait_ge(gemm_done, n["q"] + t + 1)
                src_ = sources(kb)
                for tile, k0 in src_:
                    kn = kb // len(src_)
                    last = nc.scalar.activation(ys_hi[:, r, k0:k0 + kn, :], tile[:, 0:kn, ds(t * P, P)], ACT.Copy)
                last.then_inc(split_high, 1)

            def score_rows(n, m):
                for c in range(NC1):
                    act.wait_ge(srow_mm, NC1 * n["sc"] + c + 1)
                    nc.scalar.activation(srow[0:m, node_chunk(c)], ps[0:m, 6 + c % 2, 0:chunk_width(c)], ACT.Copy
                                         ).then_inc(srow_out, 1)
                act.wait_ge(t_ready, n["gat"])
                act.wait_ge(row_mm, n["rows"] + 1)
                for c in range(NC1):
                    last = nc.scalar.activation(x_row[:P, node_chunk(c)], ps[:P, c, 0:chunk_width(c)], ACT.Copy)
                last.then_inc(row_ready, 1)

            def product(n, kb, width, beside, scale, hd, rest):
                input_begun(act, n)
                with_rows = beside == "rows"

                def finish(t, r, i):
                    act.wait_ge(gemm_done, n["q"] + t + 3)
                    nc.scalar.activation(h_block(h_hi, width, t), ps_block(product_bank(r, with_rows), width), ACT.Copy,
                                         scale=1.0 if scale is None else scale[:, ds(t, 1)]).then_inc(gemm_act, 1)

                def started():
                    if rest is not None:
                        rest()
                    if beside == "scores":
                        score_rows(n, 2 if hd is None else 2 * HEADS)
                    if scale is not None:
                        act.wait_ge(dinv_ready, 1)
                    input_whole(act, n)
                    if with_rows:
                        for r in range(2):
                            act.wait_ge(sum_added[r], 16 * n["sp"] + ZEROED)
                    act.sem_inc(held, 1)

                k, bank = (1, 0) if beside == "scores" else (0, 5)

                def x_out():
                    act.wait_ge(maxed, 2 * n["mp"] + (T if beside == "scores" else 0) + 2)
                    row(x_row, P, n, k, bank)
                    act.sem_inc(held, 1)

                def y_out():
                    act.wait_ge(t_ready, n["gat"])
                    row(y_row, P, n, k + 1, bank)

                hooks = {"rows": {1: x_out, 3: y_out}, "scores": {3: x_out, 4: y_out},
                         "degree": {3: lambda: row(x_row, 128, n, 0, 0)}, None: {}}[beside]
                blocks_ahead(act, lambda t, r: split_block(n, kb, t, r), finish, started, hooks, begun=with_rows)

            def columns(n):
                act.wait_ge(maxed, 2 * n["mp"] + 2)
                row(x_row, P, n, 0)
                act.wait_ge(t_ready, n["gat"])
                row(y_row, P, n, 1)

            def fold(n):
                act.wait_ge(t_ready, n["gat"])
                row(x_row, P, n, 0)
                for t in range(T):
                    act.wait_ge(sum_in[t % 4], 16 * (t // 4 + 1))
                    nc.scalar.activation(h_block(h_hi, D, t), halves(ev[:P, t % 4, :]), ACT.Copy).then_inc(fold_high, 1)

            def tiles(n, c, kind, width, hook):
                t0, g = n["tile"] + c * T, n["gat"] + c * T

                def exp(s):
                    act.wait_ge(t_ready, g + s + 1)
                    nc.scalar.activation(tb[:, s % RING, 0:width], tb[:, s % RING, 0:width], ACT.Exp,
                                         bias=s02[:, s:s + 1]).then_inc(e_ready, 1)

                def high(s):
                    if kind == "gat":
                        act.wait_ge(p_ready, g + s + 1)
                        tile = tb[:, s % RING, 0:width]
                    else:
                        act.wait_ge(c_ld[s % RING], 16 * (2 * (n["chunks"] + c) + s // RING + 1))
                        tile = c_in[:, s % RING, 0:width]
                    act.wait_ge(tile_used, t0 + s + 1)
                    nc.scalar.activation(p_hi[:, s % RING, 0:width], tile, ACT.Copy).then_inc(p_high, 1)

                for s in range(T + 1):
                    if s < T and kind == "gat":
                        exp(s)
                    if s < T and kind == "gcn":
                        high(s)
                    if s >= 1 and kind == "gat":
                        high(s - 1)
                    hook(s)

            def hook_weights(n, following, s):
                if following is not None and 0 <= s - SPLIT_AT < weights_of(*following)[0]:
                    piece(n, *following, s - SPLIT_AT)

            def finish_across(n, c, fb, what, bias, blocks=None):
                for f in blocks or range(fb):
                    v = n["f1"] + c * fb + f
                    act.wait_ge(ev_scaled, v + 1 + 1)
                    z, b = z_tile(f), b_col[:, ds(bias + f, 1)]
                    if what == "elu":
                        nc.scalar.activation(e_tile(f), z, ACT.Exp, bias=b).then_inc(ev_act, 1)
                        hold(act, ev_act, 2 * (n["elu"] + c * fb + f) + 1)
                        nc.scalar.activation(z, z, ACT.Relu, bias=b).then_inc(ev_act, 1)
                    else:
                        nc.scalar.activation(XT[:, f, ds(c * TS, TW)], z, ACT.Relu, bias=b).then_inc(ev_done, 1)

            def across(n, kind, fb, what, bias, following, eps):
                act.wait_ge(b_in, 48)
                act.wait_ge(gemm_done, n["q"] + 2)

                def hook(s):
                    hook_weights(n, following, s)
                    if following[0] == "L0_W2" and s == T:
                        act.wait_ge(w_dot, 2 * (n["dot"] + KH) + 4)
                        nc.scalar.activation(w2[0][:, :, D:HW], wa[:, 0:KH, :], ACT.Copy).then_inc(wa_high, 1)

                tiles(n, 0, kind, TW, hook)
                first = chunk_ends(kind) + (1 if kind == "gcn" or what == "elu" else 0)
                steps = {first: range(0, fb // 2), first + 2: range(fb // 2, fb)} if what == "elu" else {first: None}
                with act.Fori(1, NC1) as c:
                    tiles(n, c, kind, TW, lambda s: finish_across(n, c - 1, fb, what, bias, steps[s]) if s in steps else None)
                return lambda: finish_across(n, NC1 - 1, fb, what, bias)

            def along(n, kind, layer, following, eps):
                def deviation(c):
                    act.wait_ge(var_ready, 2 * (n["c2"] + c) + 2)
                    nc.scalar.activation(rstd[:], mv[:, :, 1], ACT.Sqrt, bias=eps_col[:, 0:1]).then_inc(std_ready, 1)

                def turn(c, bank):
                    if layer < 3:
                        for r in range(2):
                            turned(n["y"] + 2 * c + r, 2 * c + r, r, bank)

                tiles(n, 0, kind, BW, lambda s: hook_weights(n, following, s))
                with act.Fori(0, NC2 // 2) as i:
                    for k, bank in ((0, 0), (1, 4)):
                        c = 2 * i + k
                        tiles(n, c + 1, kind, BW,
                              lambda s: deviation(c) if s == chunk_ends(kind) + 2
                              else turn(c, bank) if s == T else None)

                def rest():
                    deviation(NC2 - 1)
                    turn(NC2 - 1, 0)

                if following is not None:
                    return rest
                rest()

            program(act, Stages(graph, turn_input, head_scores, product_sum, product, columns, across, along, fold))

        @block.vector
        def _(dve):
            for started_at_1 in (amax_ready, ev_scaled, y_ready, r_ready, agg2_read, oh_ready):
                dve.sem_inc(started_at_1, 1)
            dve.sem_inc(w_dot, 4)
            dve.sem_inc(gemm_dve, 2)
            dve.sem_inc(gemm_act, 2)
            dve.sem_inc(maxed, 2)
            dve.sem_inc(p_low, RING)
            dve.sem_inc(ev_done, 2)

            def graph():
                chain = [0]

                def link(ins):
                    chain[0] += 1
                    ins.then_inc(step, 1)
                    dve.wait_ge(step, chain[0])

                link(nc.vector.memset(eps_col[:], EPS))
                nc.vector.memset(score_sum[:], 0.0).then_inc(summed, 1)
                link(nc.vector.memset(src_col[:], 0.0))
                link(nc.vector.memset(dst_col[:], -1.0))
                dve.wait_ge(edges_in, 32)
                nc.vector.tensor_copy(e_flt[:], e_int[:]).then_inc(edges_flt, 1)
                dve.wait_ge(edges_turned, 1)
                for i, col in enumerate((src_col, dst_col)):
                    link(nc.vector.tensor_copy(col[:, SLACK:SLACK + EC].rearrange("p (q h) -> p h q", h=2),
                                               ps[:P, 7, i * EC:(i + 1) * EC].rearrange("p (h q) -> p h q", h=2)))
                dve.wait_ge(graph_const, 5)
                link(nc.vector.tensor_copy(iota[:], iota_i[:]))
                link(nc.vector.tensor_copy(lim[:], lim_i[:]))
                real = dst_col[:, SLACK:SLACK + EC]
                low = lim[:, 0, PER - SLACK:PER - SLACK + EC]
                high = lim[:, 1, SLACK:SLACK + EC]
                link(nc.vector.tensor_tensor(out_of[:, 0, :], low, real, ALU.is_gt))
                link(nc.vector.tensor_tensor(out_of[:, 1, :], real, high, ALU.is_ge))
                nc.vector.tensor_reduce(bad[:], out_of[:].rearrange("p a c -> p (a c)"), AX.X, ALU.add
                                        ).then_inc(bad_ready, 1)
                dve.wait_ge(bad_summed, 1)
                link(nc.vector.tensor_scalar(par_f[:, 0:1], ps[0:1, 7, 0:1], 1.0, None, ALU.min))
                for j, (sorted_, all_) in enumerate(((WIN // OH - 2, ECP // OH - 2), (PER, 0), (WIN, ECP))):
                    link(nc.vector.tensor_scalar(par_f[:, j + 1:j + 2], par_f[:, 0:1], float(all_ - sorted_),
                                                 float(sorted_), ALU.mult, ALU.add))
                nc.vector.tensor_copy(params[:], par_f[:]).then_inc(par_ready, 1)
                dve.wait_ge(par_ready, 1)
                turns = dve.value_load(params[0:1, 1:2], min_val=WIN // OH - 2, max_val=ECP // OH - 2)
                stride = dve.value_load(params[0:1, 2:3], min_val=0, max_val=PER)
                count = dve.value_load(params[0:1, 3:4], min_val=WIN, max_val=ECP)

                def one_hot(b, j, slot):
                    col = ds(nc.s_assert_within(stride * b + j, 0, ECP - 1, skip_runtime_bounds_check_because=
                                              "stride, turns and count come as (PER, ., WIN) or (0, ., ECP)"), 1)
                    dve.wait_ge(oh_used, count * b + j + 1)
                    nc.vector.tensor_scalar(oh_src[:, slot, :], iota[:], src_col[:, col], None, ALU.is_equal)
                    nc.vector.tensor_scalar(oh_dst[:, slot, :], iota[:, 0:P], dst_col[:, col], None,
                                            ALU.is_equal).then_inc(oh_ready, 1)

                def degrees(b, r):
                    hold(dve, ct_loop, b + 1)
                    nc.vector.tensor_reduce(deg[:, ds(b, 1)], ct[:, r, :], AX.X, ALU.add).then_inc(ct_deg, 1)

                def block(b, r, later):
                    for k in range(OH):
                        one_hot(b, k, k)
                    with dve.Fori(0, turns) as i:
                        for k in range(OH):
                            one_hot(b, i * OH + OH + k, k)
                    if later:
                        degrees(b - 1, 1 - r)
                    for k in range(OH):
                        one_hot(b, turns * OH + OH + k, k)
                    dve.wait_ge(oh_ready, count * b + count + 1)
                    nc.vector.tensor_scalar(dst_col[:], dst_col[:], float(-P), None, ALU.add).then_inc(step, 1)
                    dve.wait_ge(step, b + (chain[0] + 1))
                    dve.sem_inc(held, 1)

                graph_blocks(dve, block)
                degrees(T - 1, 1)
                dve.wait_ge(ct_deg, T)
                nc.vector.tensor_scalar(many[:], deg[:], EXACT, None, ALU.is_gt).then_inc(step, 1)
                dve.wait_ge(step, chain[0] + T + 1)
                nc.vector.tensor_reduce(many_any[:], many[:], AX.X, ALU.add).then_inc(many_ready, 1)
                dve.wait_ge(many_summed, 1)
                nc.vector.tensor_scalar(par_f[:, 0:1], ps[0:1, 6, 0:1], 1.0, None, ALU.min).then_inc(step, 1)
                dve.wait_ge(step, chain[0] + T + 2)
                nc.vector.tensor_copy(params[:, 0:1], par_f[:, 0:1]).then_inc(low_ready, 1)
                dve.wait_ge(root, 1)
                nc.vector.reciprocal(dinv[:], dinv[:]).then_inc(dinv_ready, 1)
                assert chain[0] + T + 2 == GRAPH_STEPS, chain[0]

            def chain_from(semaphore, start):
                at_ = [start]

                def link(ins):
                    at_[0] = at_[0] + 1
                    ins.then_inc(semaphore, 1)
                    dve.wait_ge(semaphore, at_[0])
                return link

            def piece(n, name, hd, k):
                width = weights_of(name, hd)[1]
                if vectors_of(name, hd) is None:
                    return
                if k == 0:
                    dve.wait_ge(score_mm, n["sc"])
                    dve.wait_ge(a_in, 32 * n["av"] + 32)
                    dve.wait_ge(ev_scaled, n["f1"] + 1)
                    dve.wait_ge(ev_done, n["f1"] + 2)
                dve.wait_ge(w_in[k % 2], 16 * (n["wp"] + k // 2 + 1))
                for j in range(2):
                    hold(dve, w_dot, 2 * (n["dot"] + k) + j + 4)
                    nc.vector.tensor_tensor_reduce(
                        out=r_row[:].bitcast(BF16)[:, 0:width], in0=ws[:, k % 2, 0:width], in1=a_row[:, j, 0:width],
                        scale=1.0, scalar=0.0, op0=ALU.mult, op1=ALU.add, accum_out=wa[:, k, j:j + 1]).then_inc(w_dot, 1)

            def head_scores():
                dve.wait_ge(a1_in, 32)
                for k in range(KD):
                    dve.wait_ge(rows_in[k] if k < ROWS else rows_more[k - ROWS], 16)
                    for hd in range(HEADS):
                        for j in range(2):
                            at_ = 2 * (HEADS * k + hd) + j
                            if at_:
                                dve.wait_ge(head_dot, at_)
                            nc.vector.tensor_tensor_reduce(
                                out=r_row[:].bitcast(BF16)[:, 0:HID], in0=w1_rows[:, k % ROWS, hd * HID:(hd + 1) * HID],
                                in1=a1_row[:, j * HEADS + hd, :], scale=1.0, scalar=0.0, op0=ALU.mult, op1=ALU.add,
                                accum_out=wa8[:, k, 2 * hd + j:2 * hd + j + 1]).then_inc(head_dot, 1)

            def take_scores(n, hd):
                link = chain_from(step, n["step"])
                link(nc.vector.tensor_copy(score[:], score8[:, :, ds(2 * hd, 2)]))
                source_columns(link)

            def product_sum(before, n, hd, more):
                def finish(t, r, i):
                    dve.wait_ge(gemm_done, n["q"] + t + 3)
                    scores_ = ps[:P, 5 + 2 * r, HALF:HALF + 2]
                    nc.vector.tensor_tensor(score_sum[:, ds(t, 1), :].rearrange("p t j -> p (t j)"),
                                            score_sum[:, ds(t, 1), :].rearrange("p t j -> p (t j)"), scores_,
                                            ALU.add).then_inc(summed, 1)
                    dve.wait_ge(sum_added[r], 16 * (n["sp"] + i) + ZEROED)
                    nc.vector.tensor_copy(add[:, r, HALF:D], ps[:P, 5 + 2 * r, 0:HALF]).then_inc(gemm_dve, 1)

                def started():
                    weights_summed(before, NC1 - 1, "gat", ("L0_W2", hd), 1e-16)
                    scaled(before, NC1 - 1, "gat", KH)
                    if more:
                        dve.wait_ge(e_ready, n["gat"])
                        dve.wait_ge(xy_ready, n["xy"])
                        take_scores(n, hd + 1)
                    hold(dve, summed, 2 * n["sp"] + 1)

                def last_chunk():
                    elu_sum(before, NC1 - 1, KH)
                    if more:
                        dve.wait_ge(p_low, n["tile"] + RING)
                        dve.wait_ge(acc_done, n["acc"] + RING)
                        dve.wait_ge(row_ready, n["rows"] + 1)
                        dve.sem_inc(held, 1)

                def max_pair(j):
                    for r in range(2):
                        masked_max(n, j, r)

                def last_max():
                    max_pair(T // 2 - 1)
                    columns(dict(n, mp=n["mp"] + T // 2, step=n["step"] + 3))

                blocks_ahead(dve, lambda t, r: split_block(n, KH, t, r), finish, started,
                             {1: last_chunk, 3: last_max} if more else {1: last_chunk},
                             (1, 3, max_pair) if more else None,
                             then=(lambda t, r: split_block(dict(n, q=n["q"] + T), KD, t, r)) if more else None)

            def source_columns(link):
                link(nc.vector.tensor_scalar(s08[:], score[:, :, 0], 1.0 - SLOPE, None, ALU.mult))
                link(nc.vector.tensor_scalar(s02[:], score[:, :, 0], SLOPE, None, ALU.mult))

            def scores(n, hd):
                dve.wait_ge(score_mm, n["sc"] + 1)
                m, dest = (2, score) if hd is None else (2 * HEADS, score8)
                nc.vector.tensor_copy(dest[:], ps[:P, 4, 0:m * T].rearrange("p (t j) -> p t j", j=m)
                                      ).then_inc(score_ready, 1)
                dve.wait_ge(score_ready, n["sc"] + 1)
                if hd is None:
                    source_columns(chain_from(step, n["step"]))
                else:
                    take_scores(n, hd)

            def masked_max(n, i, r, loaded=None):
                dve.wait_ge(maxed, 2 * (n["mp"] + i) + r + 2)
                dve.wait_ge(amax_ready, n["mp"] + i + 1)
                hold(dve, *((mask_ld[r], 16 * (n["ml"] + i + 1)) if loaded is None else (masks_in, 16)))
                nc.vector.tensor_tensor_reduce(out=junk[:], in0=x_row[:P, :], in1=mask_in[r][:] if loaded is None else loaded, scale=1.0, scalar=NONE,
                                               op0=ALU.add, op1=ALU.max, accum_out=pair_max[:, r:r + 1]).then_inc(maxed, 1)
                if r == 1:
                    dve.wait_ge(maxed, 2 * (n["mp"] + i) + 4)
                    nc.vector.tensor_copy(amax[:, ds(2 * i, 2)], pair_max[:]).then_inc(amax_ready, 1)

            def split_block(n, kb, t, r):
                dve.wait_ge(split_high, n["q"] + t + 1)
                src_ = sources(kb)
                for tile, k0 in src_:
                    kn = kb // len(src_)
                    last = nc.vector.tensor_tensor(ys_lo[:, r, k0:k0 + kn, :], tile[:, 0:kn, ds(t * P, P)],
                                                   ys_hi[:, r, k0:k0 + kn, :].bitcast(F32), ALU.subtract)
                last.then_inc(split_low, 1)

            def product(n, kb, width, beside, scale, hd, rest):
                input_begun(dve, n)

                def started():
                    if rest is not None:
                        rest()
                    if beside == "scores":
                        scores(n, hd)
                    if scale is not None:
                        dve.wait_ge(dinv_ready, 1)
                    input_whole(dve, n)
                    dve.sem_inc(held, 1)
                    if beside == "scores":
                        dve.wait_ge(p_low, n["tile"] + RING)
                        dve.wait_ge(acc_done, n["acc"] + RING)
                        dve.wait_ge(row_ready, n["rows"] + 1)

                def finish(t, r, i):
                    q = n["q"] + t
                    dve.wait_ge(gemm_done, q + 3)
                    dve.wait_ge(gemm_act, q + 3)
                    nc.vector.scalar_tensor_tensor(
                        out=h_block(h_lo, width, t), in0=ps_block(product_bank(r, beside == "rows"), width),
                        scalar=1.0 if scale is None else scale[:, ds(t, 1)],
                        in1=h_block(h_hi, width, t).bitcast(F32), op0=ALU.mult, op1=ALU.subtract).then_inc(gemm_dve, 1)

                def max_pair(j):
                    for r in range(2):
                        masked_max(n, j, r)

                if beside == "scores":
                    def last_max():
                        max_pair(T // 2 - 1)
                        columns(dict(n, mp=n["mp"] + T // 2, step=n["step"] + (2 if hd is None else 3)))

                    assert T // 2 == 2 * 2 + 1
                    blocks_ahead(dve, lambda t, r: split_block(n, kb, t, r), finish, started, {2: last_max}, (0, 2, max_pair))
                else:
                    blocks_ahead(dve, lambda t, r: split_block(n, kb, t, r), finish, started, begun=beside == "rows")

            def columns(n):
                link = chain_from(step, n["step"])
                dve.wait_ge(amax_ready, n["mp"] + 1)
                link(nc.vector.tensor_tensor(mcol[:], amax[:], score[:, :, 1], ALU.add))
                link(nc.vector.scalar_tensor_tensor(out=mcol[:], in0=mcol[:], scalar=SLOPE, in1=mcol[:],
                                                    op0=ALU.mult, op1=ALU.max))
                link(nc.vector.tensor_tensor(xcol[:], score[:, :, 1], mcol[:], ALU.subtract))
                nc.vector.scalar_tensor_tensor(out=ycol[:], in0=score[:, :, 1], scalar=SLOPE, in1=mcol[:],
                                               op0=ALU.mult, op1=ALU.subtract).then_inc(xy_ready, 1)

            def fold(n):
                dve.wait_ge(gemm_done, n["q"] + 2)
                for r in range(2):
                    dve.wait_ge(sum_added[r], 16 * n["sp"] + ZEROED)
                dve.wait_ge(summed, 2 * n["sp"] + 1)
                link = chain_from(step, n["step"])
                nc.vector.memset(h_view(h_hi, D)[:, :, D:HW].bitcast(F32), 1.0).then_inc(ones_set, 1)
                nc.vector.memset(h_view(h_lo, D)[:, :, D:HW].bitcast(F32), 0.0).then_inc(ones_set, 1)
                link(nc.vector.tensor_copy(score[:], score_sum[:]))
                source_columns(link)
                dve.wait_ge(p_low, n["tile"] + RING)
                dve.wait_ge(acc_done, n["acc"] + RING)
                dve.wait_ge(row_ready, n["rows"] + 1)
                for t in range(T):
                    masked_max(n, t // 2, t % 2, masks_all[:, t, :])

            def tiles(n, c, kind, width, off, sums, hook):
                t0, g, a = n["tile"] + c * T, n["gat"] + c * T, n["acc"] + c * T

                def larger(s):
                    dve.wait_ge(p_low, t0 + s + 1)
                    if sums:
                        dve.wait_ge(acc_done, a + s + 1)
                    nc.vector.scalar_tensor_tensor(out=tb[:, s % RING, 0:width], in0=x_row[:P, ds(off, width)],
                                                   scalar=s08[:, s:s + 1], in1=y_row[:, ds(off, width)],
                                                   op0=ALU.add, op1=ALU.max).then_inc(t_ready, 1)

                def count(s):
                    dve.wait_ge(e_ready, g + s + 1)
                    dve.wait_ge(c_ld[s % RING], 16 * (2 * (n["chunks"] + c) + s // RING + 1))
                    nc.vector.scalar_tensor_tensor(out=tb[:, s % RING, 0:width], in0=tb[:, s % RING, 0:width],
                                                   scalar=1.0, in1=c_in[:, s % RING, 0:width],
                                                   op0=ALU.min, op1=ALU.mult).then_inc(p_ready, 1)

                def low(s):
                    dve.wait_ge(p_high, t0 + s + 1)
                    tile = tb if kind == "gat" else c_in
                    nc.vector.tensor_tensor(p_lo[:, s % RING, 0:width], tile[:, s % RING, 0:width],
                                            p_hi[:, s % RING, 0:width].bitcast(F32), ALU.subtract).then_inc(p_low, 1)

                if kind == "gcn":
                    for s in range(T):
                        low(s)
                        hook(s)
                    return
                for s in range(T + 2):
                    if s < T:
                        larger(s)
                    if 1 <= s <= T:
                        count(s - 1)
                    if s >= 2:
                        low(s - 2)
                    hook(s)

            def hook_weights(n, following, s):
                if following is not None and 0 <= s - SPLIT_AT < weights_of(*following)[0]:
                    piece(n, *following, s - SPLIT_AT)

            def weights_summed(n, c, kind, following, eps):
                dots = n["dot"] + (weights_of(*following)[0] if vectors_of(*following) else 0)
                dve.wait_ge(w_dot, 2 * dots + 4)
                if kind == "gcn":
                    return
                fb = KH if eps else KD
                dve.wait_ge(ev_scaled, n["f1"] + c * fb + 1)
                dve.wait_ge(ev_done, n["f1"] + c * fb + 2)
                dve.wait_ge(den_mm, n["den"] + c + 1 + 1)
                total = ps[:, sum_bank(fb, c), 0:TW]
                if eps:
                    link = chain_from(step, n["step"] + c)
                    link(nc.vector.tensor_scalar(r_row[:], total, eps, None, ALU.add))
                    total = r_row[:]
                nc.vector.reciprocal(r_row[:], total).then_inc(r_ready, 1)

            def scaled(n, c, kind, fb):
                dve.wait_ge(ev_done, n["f1"] + c * fb + 2)
                if kind == "gat":
                    dve.wait_ge(r_ready, n["den"] + c + 1 + 1)
                scale = r_row[:] if kind == "gat" else x_row[:, ds(c * TS, TW)]
                for f in range(fb):
                    dve.wait_ge(agg_mm, n["f1"] + c * fb + f + 1)
                    nc.vector.tensor_tensor(z_tile(f), ps[:, first_bank(fb, c) + f, 0:TW], scale, ALU.mult
                                            ).then_inc(ev_scaled, 1)

            def elu_sum(n, c, fb):
                e0 = n["elu"] + c * fb
                for f in range(fb):
                    hold(dve, ev_act, 2 * (e0 + f) + 1)
                    nc.vector.tensor_scalar(e_tile(f), e_tile(f), 1.0, -1.0, ALU.min, ALU.add).then_inc(ev_exp, 1)
                for f in range(fb):
                    dve.wait_ge(ev_act, 2 * (e0 + f) + 2)
                    dve.wait_ge(ev_exp, e0 + f + 1)
                    nc.vector.tensor_tensor(ot[f // 2][:, f % 2, ds(c * TS, TW)], z_tile(f), e_tile(f),
                                            ALU.add).then_inc(ev_done, 1)

            def across(n, kind, fb, what, bias, following, eps):
                dve.wait_ge(maxed, 2 * n["mp"] + 2)
                dve.wait_ge(row_ready, n["rows"])
                dve.wait_ge(gemm_done, n["q"] + 2)
                if kind == "gcn" or fb == KD:
                    for r in range(2):
                        dve.wait_ge(stored[r], 16 * n["c2"] + 16)

                tiles(n, 0, kind, TW, 0, kind == "gat", lambda s: hook_weights(n, following, s))

                def hook(c, s):
                    if s == chunk_ends(kind):
                        weights_summed(n, c, kind, following, eps)
                    if s == chunk_ends(kind) + (1 if what == "elu" else 0):
                        scaled(n, c, kind, fb)
                    if s == chunk_ends(kind) + 4 and what == "elu":
                        elu_sum(n, c, fb)

                other_chunks(dve, fb, lambda c: tiles(n, c, kind, TW, c * TS, kind == "gat", lambda s: hook(c - 1, s)))

                def rest():
                    weights_summed(n, NC1 - 1, kind, following, eps)
                    scaled(n, NC1 - 1, kind, fb)

                return rest

            def along(n, kind, layer, following, eps):
                dve.wait_ge(maxed, 2 * n["mp"] + 2)
                dve.wait_ge(row_ready, n["rows"])

                def statistics(c, bank):
                    link = chain_from(ln_step, n["ln"] + c * ln_links(kind, eps))
                    dve.wait_ge(y_ready, 2 * (n["c2"] + c) + 1)
                    for r in range(2):
                        b = 2 * (n["c2"] + c) + r
                        dve.wait_ge(agg2_mm, n["c2"] + c + 1)
                        if kind == "gat":
                            total = ps[:P, bank + 2 * r + 1, HALF:HALF + 1]
                            if eps:
                                link(nc.vector.tensor_scalar(rden[:, r, 0:1], total, eps, None, ALU.add))
                                total = rden[:, r, 0:1]
                            link(nc.vector.reciprocal(rden[:, r, 1:2], total))
                            by = rden[:, r, 1:2]
                        else:
                            by = dinv[:, ds(2 * c + r, 1)]
                        dve.wait_ge(res_ready, b + 1)
                        dve.wait_ge(stored[r], 16 * (n["c2"] + c) + 16)
                        dve.wait_ge(y_turned, n["y"] + (2 if layer == 3 else 2 * c + r + 1))
                        y = ev[:P, r, :]
                        nc.vector.scalar_tensor_tensor(out=halves(y), in0=ps[:P, bank + 2 * r:bank + 2 * r + 2, 0:HALF], scalar=by,
                                                       in1=halves(ev[:P, 2 + r, :]), op0=ALU.mult, op1=ALU.add
                                                       ).then_inc(agg2_read, 1)
                    for r in range(2):
                        dve.wait_ge(agg2_read, 2 * (n["c2"] + c) + r + 1 + 1)
                        for j in range(2):
                            link(nc.vector.bn_stats(stats[:, r, j, :], ev[:P, r, j * HALF:(j + 1) * HALF]))
                        dve.sem_inc(held, 1)
                        nc.vector.bn_aggr(mv[:, r, :], stats[:, r, :, :].rearrange("p a b -> p (a b)")).then_inc(var_ready, 1)
                def normalised(c):
                    link = chain_from(ln_step, n["ln"] + (c + 1) * ln_links(kind, eps) - 1)
                    dve.wait_ge(var_ready, 2 * (n["c2"] + c) + 2)
                    dve.wait_ge(std_ready, n["c2"] + c + 1)
                    link(nc.vector.reciprocal(rstd[:], rstd[:]))
                    for r in range(2):
                        y = ev[:P, r, :]
                        nc.vector.tensor_scalar(y, y, mv[:, r, 0:1], rstd[:, r:r + 1], ALU.subtract, ALU.mult
                                                ).then_inc(y_ready, 1)

                def hook(c, bank, s):
                    if s == chunk_ends(kind) + 1:
                        statistics(c, bank)
                    if s == chunk_ends(kind) + 3:
                        normalised(c)

                tiles(n, 0, kind, BW, 0, False, lambda s: hook_weights(n, following, s))
                with dve.Fori(0, NC2 // 2) as i:
                    for k, bank in ((0, 0), (1, 4)):
                        c = 2 * i + k
                        tiles(n, c + 1, kind, BW, (c + 1) * BW, False, lambda s: hook(c, bank, s))

                def rest():
                    statistics(NC2 - 1, 0)
                    normalised(NC2 - 1)

                if following is not None:
                    return rest
                rest()

            def none(*_):
                pass

            program(dve, Stages(graph, none, head_scores, product_sum, product, columns, across, along, fold))

        @block.tensor
        def _(pe):
            pe.sem_inc(den_mm, 1)
            pe.sem_inc(oh_used, OH)
            pe.sem_inc(y_turned, 2)
            pe.sem_inc(xt_ready, 2)
            pe.sem_inc(gemm_done, 2)
            pe.sem_inc(tile_used, RING)

            def graph():
                pe.wait_ge(graph_const, 1)
                pe.wait_ge(edges_flt, 1)
                for i in range(2):
                    for h in range(2):
                        o = i * EC + h * (EC // 2)
                        last = pe.transpose(ps[:P, 7, o:o + EC // 2], e_flt[:, i, h * P:(h + 1) * P],
                                            ident[0:EC // 2, 0:EC // 2])
                last.then_inc(edges_turned, 1)
                pe.wait_ge(bad_ready, 1)
                pe.matmul(ps[0:1, 7, 0:1], bad[:], ones[:, 0:1], start=True, stop=True).then_inc(bad_summed, 1)
                pe.wait_ge(par_ready, 1)
                turns = pe.value_load(params[0:1, 1:2], min_val=WIN // OH - 2, max_val=ECP // OH - 2)
                count = pe.value_load(params[0:1, 3:4], min_val=WIN, max_val=ECP)

                def add(b, r, j, slot, start, stop):
                    pe.wait_ge(oh_ready, count * b + j + 1 + 1)
                    for k in range(3):
                        o, w = (TW + TS * (k - 1), TS) if k else (0, TW)
                        last = pe.matmul(ps[:P, 3 * r + k, 0:w], oh_dst[:, slot, :], oh_src[:, slot, o:o + w],
                                         start=start, stop=stop)
                    last.then_inc(oh_used, 1)
                    return last

                def turned(b, r):
                    pe.wait_ge(ct_loop, b + 1)
                    for j in range(T):
                        last = pe.transpose(ps[:P, 3 * r + j // 4, (j % 4) * P:(j % 4 + 1) * P],
                                            ct[:, r, j * P:(j + 1) * P], ident[:P, :P])
                    last.then_inc(ct_turned, 1)

                def block(b, r, later):
                    if later:
                        hold(pe, c_ready, b - 1 + 1)
                    for k in range(OH):
                        add(b, r, k, k, k == 0, False)
                    with pe.Fori(0, turns) as i:
                        for k in range(OH):
                            add(b, r, i * OH + OH + k, k, False, False)
                    if later:
                        turned(b - 1, 1 - r)
                    for k in range(OH):
                        add(b, r, turns * OH + OH + k, k, False, k == OH - 1)
                    pe.wait_ge(oh_used, count * b + count + OH)
                    pe.sem_inc(ct_summed, 1)

                graph_blocks(pe, block)
                turned(T - 1, 1)
                pe.wait_ge(many_ready, 1)
                pe.matmul(ps[0:1, 6, 0:1], many_any[:], ones[:, 0:1], start=True, stop=True).then_inc(many_summed, 1)

            def low_passes():
                pe.wait_ge(low_ready, 1)
                return pe.value_load(params[0:1, 0:1], min_val=0, max_val=1)

            def turn(tile, r, bank):
                for k in range(KD):
                    last = pe.transpose(ps[:, bank + 2 * r + k // 3, (k % 3) * P:(k % 3 + 1) * P],
                                        ev[:P, tile, k * 128:(k + 1) * 128], ident[:P, :P])
                last.then_inc(y_turned, 1)

            def turn_input():
                pe.wait_ge(c_ready, T + 1)
                for t in range(T):
                    pe.wait_ge(x_in[t % 4], 16 * (t // 4 + 1))
                    pe.wait_ge(xt_ready, t + 1)
                    if t == 1:
                        pe.wait_ge(low_ready, 1)
                    turn(t % 4, t % 2, 4)

            def banks_free(n):
                pe.wait_ge(xt_ready, n["y"] + 2)
                pe.wait_ge(row_ready, n["rows"])
                pe.wait_ge(score_ready, n["sc"])
                pe.wait_ge(gemm_act, n["q"] + 2)
                pe.wait_ge(gemm_dve, n["q"] + 2)
                pe.wait_ge(ev_scaled, n["f1"] + 1)
                pe.wait_ge(r_ready, n["den"] + 1)
                pe.wait_ge(agg2_read, 2 * n["c2"] + 1)

            def row(n, k, col, parts, bank=5):
                pe.wait_ge(row_ready, n["rows"] + k)
                for t in range(T):
                    last = pe.matmul(ps[:parts, bank + t // 4, (t % 4) * P:(t % 4 + 1) * P],
                                     col(t).broadcast_to([P, parts]), ident[:P, :P], start=True, stop=True)
                last.then_inc(row_mm, 1)

            def source_row(n, bank):
                row(n, 0, lambda t: score[:, t, 0:1], P, bank)

            def product_sum(before, n, hd, more):
                hold(pe, w_low, 2 * n["wp"] + 2)
                pe.wait_ge(wa_low, n["av"])
                pe.wait_ge(row_ready, n["rows"])

                def one(t, r):
                    pe.wait_ge(split_high, n["q"] + t + 1)
                    pe.wait_ge(split_low, n["q"] + t + 1)
                    pe.wait_ge(gemm_act, n["q"] + t + 1)
                    pe.wait_ge(gemm_dve, n["q"] + t + 1)
                    if r == 1:
                        pe.wait_ge(r_ready, n["den"] + 1)
                    for j, (o, w) in enumerate(((0, HALF), (HALF, HW - HALF))):
                        for k in range(KH):
                            for m, (a, b) in enumerate(PASSES):
                                last = pe.matmul(ps[:P, 4 + 2 * r + j, 0:w], (ys_hi, ys_lo)[a][:, r, k, :],
                                                 w2[b][:, k, o:o + w], start=(k == 0 and m == 0),
                                                 stop=(k == KH - 1 and m == 2))
                    last.then_inc(gemm_done, 1)

                one(0, 0)
                one(1, 1)
                if more:
                    pe.wait_ge(ev_scaled, n["f1"] + 1)
                    pe.wait_ge(step, n["step"] + 1)
                    source_row(n, 0)
                with pe.Fori(1, T // 2) as i:
                    for r in range(2):
                        one(2 * i + r, r)

            def scores_mm(n, m, vectors, rest):
                s0 = NC1 * n["sc"]

                def chunk(c):
                    if c == 2:
                        pe.wait_ge(srow_out, s0 + 1)
                    for k in range(KD):
                        last = pe.matmul(ps[0:m, 6 + c % 2, 0:chunk_width(c)], vectors[:, k, :], XT[:, k, node_chunk(c)],
                                         start=(k == 0), stop=(k == KD - 1))
                    last.then_inc(srow_mm, 1)

                pe.wait_ge(gemm_act, n["q"] + 2)
                pe.wait_ge(gemm_dve, n["q"] + 2)
                pe.wait_ge(row_ready, n["rows"])
                pe.wait_ge(r_ready, n["den"] + 1)
                chunk(0)
                chunk(1)
                if rest is not None:
                    rest()
                input_whole(pe, n)
                chunk(2)
                pe.wait_ge(ev_scaled, n["f1"] + 1)
                pe.wait_ge(agg2_read, 2 * n["c2"] + 1)
                pe.wait_ge(srow_out, s0 + NC1)
                for c in range(NC1):
                    last = pe.matmul(ps[:P, c, 0:chunk_width(c)], ident[0:m, 0:1].broadcast_to([m, P]), srow[0:m, node_chunk(c)],
                                     start=True, stop=True)
                last.then_inc(row_mm, 1)
                for t in range(T):
                    last = pe.transpose(ps[:P, 4, m * t:m * (t + 1)], srow[0:m, t * P:(t + 1) * P], ident[0:m, 0:m])
                last.then_inc(score_mm, 1)

            def product(n, kb, width, beside, scale, hd, rest):
                input_begun(pe, n)
                with_rows = beside == "rows"
                if beside == "scores":
                    if hd is None:
                        pe.wait_ge(w_dot, 2 * n["dot"] + 4)
                        scores_mm(n, 2, wa, rest)
                    else:
                        pe.wait_ge(head_dot, 2 * HEADS * KD)
                        input_whole(pe, n)
                        scores_mm(n, 2 * HEADS, wa8, rest)
                    pe.wait_ge(score_ready, n["sc"] + 1)
                if hd is None:
                    hold(pe, w_low, 2 * n["wp"] + 2)
                else:
                    hold(pe, w1_low, W1_PIECES * (hd + 1))
                if with_rows:
                    pe.wait_ge(gemm_act, n["q"] + 2)
                    pe.wait_ge(gemm_dve, n["q"] + 2)
                    pe.wait_ge(ev_scaled, n["f1"] + 1)
                    pe.wait_ge(row_ready, n["rows"])
                w = (w_hi, w_lo) if hd is None else w1
                banks = 1 if width == HID else 2
                bw = width // banks

                def one(q, r):
                    pe.wait_ge(split_high, q + 1)
                    pe.wait_ge(split_low, q + 1)
                    pe.wait_ge(gemm_act, q + 1)
                    pe.wait_ge(gemm_dve, q + 1)
                    if r == 1 and not with_rows:
                        pe.wait_ge(ev_scaled, n["f1"] + 1)
                    for j in range(banks):
                        for k in range(kb):
                            for m, (a, b) in enumerate(PASSES):
                                o = k * width + j * bw
                                last = pe.matmul(ps[:P, product_bank(r, with_rows) + j, 0:bw],
                                                 (ys_hi, ys_lo)[a][:, r, k, :], w[b][:, o:o + bw],
                                                 start=(k == 0 and m == 0), stop=(k == kb - 1 and m == 2))
                    last.then_inc(gemm_done, 1)

                def pair(i):
                    for r in range(2):
                        one(n["q"] + 2 * i + r, r)

                k, bank = (1, 0) if beside == "scores" else (0, 5)

                def x_mm():
                    pe.wait_ge(xy_ready, n["xy"] + k)
                    row(n, k, lambda t: xcol[:, t:t + 1], P, bank)

                def y_mm():
                    row(n, k + 1, lambda t: ycol[:, t:t + 1], P, bank)

                def degree_mm():
                    pe.wait_ge(agg2_read, 2 * n["c2"] + 1)
                    row(n, 0, lambda t: dinv[:, t:t + 1], 128, 0)

                hooks = {"rows": {1: x_mm, 3: y_mm}, "scores": {3: x_mm, 4: y_mm}, "degree": {3: degree_mm},
                         None: {}}[beside]
                if rest is not None and beside != "scores":
                    hooks[1] = rest
                in_segments(pe, pair, T // 2, hooks)

            def columns(n):
                pe.wait_ge(xy_ready, n["xy"] + 1)
                row(n, 0, lambda t: xcol[:, t:t + 1], P)
                row(n, 1, lambda t: ycol[:, t:t + 1], P)

            def fold(n):
                pe.wait_ge(score_ready, n["sc"])
                banks_free(n)
                row(n, 0, lambda t: score_sum[:, t, 0:1], P)
                pe.wait_ge(fold_high, T)
                pe.wait_ge(fold_low, T + 2)
                pe.wait_ge(ones_set, 2)

            def across(n, kind, fb, what, bias, following, eps):
                banks_free(n)
                width = HID if fb == KH else D

                low = low_passes() if kind == "gcn" else None

                def chunk(c, first):
                    t0 = n["tile"] + c * T
                    for s in range(T):
                        pe.wait_ge(p_high, t0 + s + 1)
                        pe.wait_ge(p_low, t0 + s + 1 + RING)

                        def products(f, passes, start, stop):
                            for m, (a, b) in enumerate(passes):
                                last = pe.matmul(ps[:, first_bank(fb, c) + f, 0:TW],
                                                 h_view((h_hi, h_lo)[a], width)[:, s, f * 128:(f + 1) * 128],
                                                 (p_hi, p_lo)[b][:, s % RING, :], start=(start and m == 0),
                                                 stop=(stop and m == len(passes) - 1))
                            return last

                        def free(f):
                            if s == 0 and fb == KD and not first:
                                pe.wait_ge(ev_scaled, n["f1"] + (c - 1) * fb + f + 1 + 1)
                            if s == 0 and fb == KH and c >= 2:
                                pe.wait_ge(ev_scaled, n["f1"] + (c - 2) * fb + f + 1 + 1)
                            if s == 0 and fb == KH and c >= 1 and f == KH - 1:
                                pe.wait_ge(r_ready, n["den"] + c + 1)

                        if s == T - 1 and kind == "gat":
                            pe.wait_ge(acc_done, n["acc"] + c * T + T + RING)
                            pe.wait_ge(r_ready, n["den"] + c + 1)
                            if fb == KH:
                                pe.wait_ge(ev_scaled, n["f1"] + c * fb + 1)
                            pe.matmul(ps[:, sum_bank(fb, c), 0:TW], ones[:].broadcast_to([P, 128]), acc[:],
                                      start=True, stop=True).then_inc(den_mm, 1)
                        if kind == "gcn":
                            for f in range(fb):
                                free(f)
                                products(f, PASSES[0:1], s == 0, False)
                            with pe.If(low > 0):
                                for f in range(fb):
                                    products(f, PASSES[1:2], False, False)
                        for f in range(fb):
                            if kind == "gat":
                                free(f)
                                last = products(f, PASSES, s == 0, s == T - 1)
                            else:
                                last = products(f, PASSES[2:3], False, s == T - 1)
                            if s == T - 1:
                                last.then_inc(agg_mm, 1)
                        if s == T - 1:
                            pe.wait_ge(agg_mm, n["f1"] + c * fb + fb)
                            pe.sem_inc(tile_used, 1)
                        else:
                            last.then_inc(tile_used, 1)

                chunk(0, True)
                other_chunks(pe, fb, lambda c: chunk(c, False))

            def along(n, kind, layer, following, eps):
                banks_free(n)

                low = low_passes() if kind == "gcn" else None

                def chunk(c, bank, hook):
                    t0 = n["tile"] + c * T
                    for s in range(T):
                        pe.wait_ge(p_high, t0 + s + 1)
                        pe.wait_ge(p_low, t0 + s + 1 + RING)

                        def products(passes, start, stop):
                            for r in range(2):
                                for m, (a, b) in enumerate(passes):
                                    for j, w in enumerate((HALF, HALF + 2)):
                                        last = pe.matmul(ps[:P, bank + 2 * r + j, 0:w],
                                                         (p_hi, p_lo)[a][:, s % RING, r * P:(r + 1) * P],
                                                         h_view((h_hi, h_lo)[b], D)[:, s, j * HALF:j * HALF + w],
                                                         start=(start and m == 0), stop=(stop and m == len(passes) - 1))
                            return last

                        if kind == "gat":
                            last = products(PASSES, s == 0, s == T - 1)
                        else:
                            products(PASSES[0:1], s == 0, False)
                            with pe.If(low > 0):
                                products(PASSES[2:3], False, False)
                            last = products(PASSES[1:2], False, s == T - 1)
                        last.then_inc(tile_used, 1)
                        hook(s)
                    pe.wait_ge(tile_used, t0 + T + RING)
                    pe.sem_inc(agg2_mm, 1)

                def turned(c, bank):
                    for r in range(2):
                        pe.wait_ge(y_ready, 2 * (n["c2"] + c) + r + 1 + 1)
                        turn(r, r, bank)

                def banks_used(c):
                    pe.wait_ge(agg2_read, 2 * (n["c2"] + c - 1) + 1)
                    if layer < 3:
                        pe.wait_ge(xt_ready, n["y"] + 2 * (c - 1) + 2)

                chunk(0, 0, lambda s: None)
                with pe.Fori(0, NC2 // 2) as i:
                    for k, bank in ((1, 4), (2, 0)):
                        banks_used(2 * i + k)
                        chunk(2 * i + k, bank, lambda s: turned(2 * i + k - 1, 4 - bank) if s == TURN_AT and layer < 3 else None)
                if layer < 3:
                    return lambda: turned(NC2 - 1, 0)

            def none(*_):
                pass

            program(pe, Stages(graph, turn_input, none, product_sum, product, columns, across, along, fold))


_INS = ['x', 'src', 'dst', 'L0_gnn_W1', 'L0_gnn_a1_src', 'L0_gnn_a1_dst', 'L0_gnn_b1', 'L0_gnn_W2', 'L0_gnn_a2_src',
        'L0_gnn_a2_dst', 'L0_gnn_b2', 'L1_gnn_W', 'L1_gnn_b', 'L2_gnn_W1', 'L2_gnn_att_src1', 'L2_gnn_att_dst1',
        'L2_gnn_b1', 'L2_gnn_W2', 'L2_gnn_att_src2', 'L2_gnn_att_dst2', 'L2_gnn_b2', 'L3_gnn_W1', 'L3_gnn_b1',
        'L3_gnn_W2', 'L3_gnn_b2']
_OUTS = [((N, D), 'float32')]


def kernel(**inputs):
    import numpy as _np
    import concourse.bacc as _bacc
    from concourse import mybir as _mybir
    from concourse.bass_utils import run_bass_kernel_spmd as _run

    nc = _bacc.Bacc("TRN2", target_bir_lowering=False, num_devices=1)
    arrays, args = {}, []
    for name in _INS:
        a = _np.ascontiguousarray(inputs[name])
        arrays[f"in_{name}_dram"] = a
        args.append(nc.dram_tensor(f"in_{name}_dram", a.shape, _mybir.dt.from_np(a.dtype), kind="ExternalInput").ap())
    for i, (shape, dtype) in enumerate(_OUTS):
        dt = _mybir.dt.from_np(_np.dtype(dtype))
        args.append(nc.dram_tensor(f"out_{i}_dram", shape, dt, kind="ExternalOutput").ap())
    build(nc, *args)
    r = _run(nc, [arrays], core_ids=[0])
    return r.results[0]["out_0_dram"]
```
